# Optimizing a Trainium2 kernel written in Bass

```python
import numpy as np
import jax
import jax.numpy as jnp

def _softmax(x, axis=-1):
    return jax.nn.softmax(x, axis=axis)

def _gelu(x):
    return jax.nn.gelu(x, approximate=True)

def _silu(x):
    return jax.nn.silu(x)

def _sigmoid(x):
    return jax.nn.sigmoid(x)

def _layernorm(x, axis=-1, eps=1e-05):
    m = jnp.mean(x, axis=axis, keepdims=True)
    v = jnp.var(x, axis=axis, keepdims=True)
    return (x - m) / jnp.sqrt(v + eps)

def _scatter_add(tgt, idx, src, axis=0):
    return tgt.at[idx].add(src)

def _segment_sum(src, seg, n):
    return jax.ops.segment_sum(src, seg, n)
kernel_name = 'mk_decoder_postln_d1_seqx_r8_68d850'

def setup_inputs(seed: int=0):
    np.random.seed(seed)
    _w = jnp.asarray

    def _rec_inputs():
        import jax
        import jax.numpy as jnp
        _rk = jax.random.key(seed)
        x = -0.0002928 + 1 * jax.random.normal(jax.random.fold_in(_rk, 1), (64, 64, 128), jnp.float32)
        _lenS = 64 - jax.random.randint(jax.random.fold_in(_rk, 7), (64,), 0, max(1, 64 // 4) + 1, jnp.int32)
        _lenS2 = 64 - jax.random.randint(jax.random.fold_in(_rk, 8), (64,), 0, max(1, 64 // 4) + 1, jnp.int32)
        _ctx_768P = jax.random.normal(jax.random.fold_in(_rk, 11), (64, 16, 96), jnp.float32)
        _ctx_768c = jax.random.dirichlet(jax.random.fold_in(_rk, 511), 0.3 * jnp.ones((16,), jnp.float32), (64, 64))
        _ctx_768t = jnp.einsum('bsk,bkd->bsd', _ctx_768c, _ctx_768P)
        _ctx_768t = _ctx_768t * jax.lax.rsqrt(jnp.mean(jnp.square(_ctx_768t)) + 1e-12) * 0.953939
        ctx_768 = -0.00055796 + 0.999787 * (_ctx_768t + 0.3 * jax.random.normal(jax.random.fold_in(_rk, 611), (64, 64, 96), jnp.float32))
        return (x, ctx_768)
    x, ctx_768 = _rec_inputs()

    def _L0_attn_setup():
        import jax, jax.numpy as jnp
        import numpy as np
        DIM = 128
        HEADS = 16
        DIM_HEAD = 64
        SCALE = 16.0
        EPS = 1e-05

        def layernorm(x, g):
            mean = jnp.mean(x, axis=-1, keepdims=True)
            var = jnp.var(x, axis=-1, keepdims=True)
            return (x - mean) * jax.lax.rsqrt(var + EPS) * g

        def l2norm(t):
            return t / jnp.maximum(jnp.linalg.norm(t, axis=-1, keepdims=True), 1e-12)
        key = jax.random.key(seed)
        ks = jax.random.split(key, 5)
        inner = HEADS * DIM_HEAD
        x = jax.random.normal(ks[0], (2, 256, DIM), dtype=jnp.float32)
        Wq = jax.random.normal(ks[1], (inner, DIM), dtype=jnp.float32) * 0.02
        Wkv = jax.random.normal(ks[2], (2 * DIM_HEAD, DIM), dtype=jnp.float32) * 0.02
        Wout = jax.random.normal(ks[3], (DIM, inner), dtype=jnp.float32) * 0.02
        g1 = jnp.ones((DIM,), dtype=jnp.float32)
        g2 = jnp.ones((DIM,), dtype=jnp.float32)
        return {'x': x, 'g1': g1, 'Wq': Wq, 'Wkv': Wkv, 'Wout': Wout, 'g2': g2}
    _L0_attn_all = _L0_attn_setup()
    _L0_attn_in = {k: v for k, v in _L0_attn_all.items() if k in ('g1', 'Wq', 'Wkv', 'Wout', 'g2')}
    del _L0_attn_all

    def _L0_xattn_setup():
        import jax, jax.numpy as jnp
        import numpy as np
        HEADS = 16
        DIM_HEAD = 64
        key = jax.random.key(seed)
        ks = jax.random.split(key, 7)
        b, n, m = (2, 256, 128)
        query_dim, context_dim = (128, 96)
        inner = HEADS * DIM_HEAD
        s_q = 1.0 / np.sqrt(query_dim)
        s_c = 1.0 / np.sqrt(context_dim)
        s_i = 1.0 / np.sqrt(inner)
        return {'x': jax.random.normal(ks[0], (b, n, query_dim), jnp.float32), 'context': jax.random.normal(ks[1], (b, m, context_dim), jnp.float32), 'Wq': jax.random.normal(ks[2], (query_dim, inner), jnp.float32) * s_q, 'Wk': jax.random.normal(ks[3], (context_dim, inner), jnp.float32) * s_c, 'Wv': jax.random.normal(ks[4], (context_dim, inner), jnp.float32) * s_c, 'Wo': jax.random.normal(ks[5], (inner, query_dim), jnp.float32) * s_i, 'bo': jax.random.normal(ks[6], (query_dim,), jnp.float32) * 0.01}
    _L0_xattn_all = _L0_xattn_setup()
    _L0_xattn_in = {k: v for k, v in _L0_xattn_all.items() if k in ('Wq', 'Wk', 'Wv', 'Wo', 'bo')}
    del _L0_xattn_all

    def _L0_ffn_setup():
        import jax, jax.numpy as jnp
        import numpy as np
        D, H, N, K = (128, 256, 8, 2)
        B, S = (4, 256)
        key = jax.random.key(seed)
        ks = jax.random.split(key, 4)
        x = jax.random.normal(ks[0], (B, S, D), dtype=jnp.float32)
        Wr = jax.random.normal(ks[1], (N, D), dtype=jnp.float32) / np.sqrt(D)
        br = jnp.zeros((N,), jnp.float32)
        Wl1 = jax.random.normal(ks[2], (N, D, 2 * H), dtype=jnp.float32) / np.sqrt(D)
        bl1 = jnp.zeros((N, 2 * H), jnp.float32)
        Wl2 = jax.random.normal(ks[3], (N, H, D), dtype=jnp.float32) / np.sqrt(H)
        bl2 = jnp.zeros((N, D), jnp.float32)
        biases_N = jnp.zeros((N,), jnp.float32)
        return {'x': x, 'Wr': Wr, 'br': br, 'Wl1': Wl1, 'bl1': bl1, 'Wl2': Wl2, 'bl2': bl2, 'biases_N': biases_N}
    _L0_ffn_all = _L0_ffn_setup()
    _L0_ffn_in = {k: v for k, v in _L0_ffn_all.items() if k in ('Wr', 'br', 'Wl1', 'bl1', 'Wl2', 'bl2', 'biases_N')}
    del _L0_ffn_all
    return {'x': x, 'ctx_768': ctx_768, 'L0_attn_g1': _L0_attn_in['g1'], 'L0_attn_Wq': _L0_attn_in['Wq'], 'L0_attn_Wkv': _L0_attn_in['Wkv'], 'L0_attn_Wout': _L0_attn_in['Wout'], 'L0_attn_g2': _L0_attn_in['g2'], 'L0_xattn_Wq': _L0_xattn_in['Wq'], 'L0_xattn_Wk': _L0_xattn_in['Wk'], 'L0_xattn_Wv': _L0_xattn_in['Wv'], 'L0_xattn_Wo': _L0_xattn_in['Wo'], 'L0_xattn_bo': _L0_xattn_in['bo'], 'L0_ffn_Wr': _L0_ffn_in['Wr'], 'L0_ffn_br': _L0_ffn_in['br'], 'L0_ffn_Wl1': _L0_ffn_in['Wl1'], 'L0_ffn_bl1': _L0_ffn_in['bl1'], 'L0_ffn_Wl2': _L0_ffn_in['Wl2'], 'L0_ffn_bl2': _L0_ffn_in['bl2'], 'L0_ffn_biases_N': _L0_ffn_in['biases_N']}

def reference(x, ctx_768, L0_attn_g1, L0_attn_Wq, L0_attn_Wkv, L0_attn_Wout, L0_attn_g2, L0_xattn_Wq, L0_xattn_Wk, L0_xattn_Wv, L0_xattn_Wo, L0_xattn_bo, L0_ffn_Wr, L0_ffn_br, L0_ffn_Wl1, L0_ffn_bl1, L0_ffn_Wl2, L0_ffn_bl2, L0_ffn_biases_N):
    import jax
    import jax.numpy as jnp

    def _L0_attn_ref(x, g1, Wq, Wkv, Wout, g2):
        import jax, jax.numpy as jnp
        import numpy as np
        DIM = 128
        HEADS = 16
        DIM_HEAD = 64
        SCALE = 16.0
        EPS = 1e-05

        def layernorm(x, g):
            mean = jnp.mean(x, axis=-1, keepdims=True)
            var = jnp.var(x, axis=-1, keepdims=True)
            return (x - mean) * jax.lax.rsqrt(var + EPS) * g

        def l2norm(t):
            return t / jnp.maximum(jnp.linalg.norm(t, axis=-1, keepdims=True), 1e-12)
        b, n, _ = x.shape
        xn = layernorm(x, g1)
        q = xn @ Wq.T
        kv = xn @ Wkv.T
        k, v = (kv[..., :DIM_HEAD], kv[..., DIM_HEAD:])
        q = q.reshape(b, n, HEADS, DIM_HEAD).transpose(0, 2, 1, 3)
        q = q * SCALE
        q, k = (l2norm(q), l2norm(k))
        srt = np.sqrt(SCALE).astype(np.float32)
        q, k = (q * srt, k * srt)
        sim = jnp.einsum('bhid,bjd->bhij', q, k)
        max_neg = -jnp.finfo(sim.dtype).max
        causal_mask = jnp.triu(jnp.ones((n, n), dtype=bool), 1)
        sim = jnp.where(causal_mask, max_neg, sim)
        attn = jax.nn.softmax(sim.astype(jnp.float32), axis=-1).astype(sim.dtype)
        out = jnp.einsum('bhij,bjd->bhid', attn, v)
        out = out.transpose(0, 2, 1, 3).reshape(b, n, HEADS * DIM_HEAD)
        out = out @ Wout.T
        return layernorm(out, g2)

    def _L0_xattn_ref(x, context, Wq, Wk, Wv, Wo, bo):
        import jax, jax.numpy as jnp
        import numpy as np
        HEADS = 16
        DIM_HEAD = 64
        b, n, _ = x.shape
        h, d = (HEADS, DIM_HEAD)
        scale = d ** (-0.5)
        q = (x @ Wq).reshape(b, n, h, d).transpose(0, 2, 1, 3)
        k = (context @ Wk).reshape(b, -1, h, d).transpose(0, 2, 1, 3)
        v = (context @ Wv).reshape(b, -1, h, d).transpose(0, 2, 1, 3)
        sim = jnp.einsum('bhid,bhjd->bhij', q, k) * scale
        attn = jax.nn.softmax(sim, axis=-1)
        out = jnp.einsum('bhij,bhjd->bhid', attn, v)
        out = out.transpose(0, 2, 1, 3).reshape(b, n, h * d)
        return out @ Wo + bo

    def _L0_ffn_ref(x, Wr, br, Wl1, bl1, Wl2, bl2, biases_N):
        import jax, jax.numpy as jnp
        import numpy as np
        D, H, N, K = (128, 256, 8, 2)
        B, S = (4, 256)
        Bb, Ss, Dd = x.shape
        scores_BSN = jnp.einsum('bsd,nd->bsn', x, Wr) + br
        w_BSN = jax.nn.softmax(scores_BSN, axis=-1)
        _, idx_BSK = jax.lax.top_k(scores_BSN + biases_N[None, None, :], K)
        val_BSK = jnp.take_along_axis(w_BSN, idx_BSK, axis=-1)
        val_BSK = val_BSK / jnp.sum(val_BSK, axis=-1, keepdims=True)
        M = Bb * Ss
        x_MD = x.reshape(M, Dd)
        idx_MK = idx_BSK.reshape(M, K)
        val_MK = val_BSK.reshape(M, K)
        h_NM2H = jnp.einsum('md,ndh->nmh', x_MD, Wl1) + bl1[:, None, :]
        a_NMH, b_NMH = (h_NM2H[..., :H], h_NM2H[..., H:])
        y_NMD = jnp.einsum('nmh,nhd->nmd', jax.nn.silu(a_NMH) * b_NMH, Wl2) + bl2[:, None, :]
        ew_MN = jnp.zeros((M, N), x.dtype)
        ew_MN = ew_MN.at[jnp.arange(M)[:, None], idx_MK].set(val_MK)
        y_MD = jnp.einsum('mn,nmd->md', ew_MN, y_NMD)
        return y_MD.reshape(Bb, Ss, Dd)
    x = _layernorm(x + _L0_attn_ref(x, L0_attn_g1, L0_attn_Wq, L0_attn_Wkv, L0_attn_Wout, L0_attn_g2), axis=-1)
    x = _layernorm(x + _L0_xattn_ref(x, ctx_768, L0_xattn_Wq, L0_xattn_Wk, L0_xattn_Wv, L0_xattn_Wo, L0_xattn_bo), axis=-1)
    x = _layernorm(x + _L0_ffn_ref(x, L0_ffn_Wr, L0_ffn_br, L0_ffn_Wl1, L0_ffn_bl1, L0_ffn_Wl2, L0_ffn_bl2, L0_ffn_biases_N), axis=-1)
    return x

_drawn_inputs = setup_inputs


def setup_inputs(seed=0):
    import zlib

    import numpy as np

    out = dict(_drawn_inputs(seed))
    spreads = {'L0_attn_g1': (1.0, 0.2),
     'L0_attn_g2': (1.0, 0.2),
     'L0_ffn_br': (0.0, 0.1),
     'L0_ffn_bl1': (0.0, 0.1),
     'L0_ffn_bl2': (0.0, 0.1),
     'L0_ffn_biases_N': (0.0, 0.1)}
    factors = {}
    for name, (base, spread) in spreads.items():
        noise = np.random.default_rng([zlib.crc32(name.encode()), seed]).standard_normal(out[name].shape)
        drawn = base * np.exp(spread * noise) if base else spread * noise
        out[name] = jnp.asarray(drawn.astype(out[name].dtype))
    for name, factor in factors.items():
        out[name] = (out[name] * factor).astype(out[name].dtype)
    return out
```

```python
from contextlib import ExitStack

import concourse.bass as bass
from concourse import mybir

F32 = mybir.dt.float32
F32R = mybir.dt.float32r
BF16 = mybir.dt.bfloat16
ALU = mybir.AluOpType
ACT = mybir.ActivationFunctionType
AX = mybir.AxisListType

P = 128
D = 128
SEQ = 64
PB = P // SEQ
HEADS = 16
DH = 64
NBLK = HEADS * DH // P
HBLK = NBLK // 2
EPS = 1e-5
FUTURE = -32768.0


def later(t, n):
    return t >= n if isinstance(t, int) else True


def decoder(nc, x, ctxT, g1, wqT, wkvT, woutT, g2, xwq, xwk, xwv, xwo, bo, wrT, br, wl1, bl1, wl2, bl2, bN, out):
    TOK = x.shape[0]
    T = TOK // P
    CD = ctxT.shape[0]
    NE = wrT.shape[1]
    HID = wl2.shape[2] * P
    NH = HID // P
    GT = 4
    G = T // GT
    GN = GT * P
    W = NBLK * P
    HW = W // 2

    ctx = ExitStack()
    with ctx:
        def sb(name, shape, dt=F32):
            return ctx.enter_context(nc.sbuf_tensor(name, shape, dt))

        def sem(name):
            return ctx.enter_context(nc.semaphore(name))

        bank = [ctx.enter_context(nc.psum_tensor(f"bank{i}", [P, 512], F32)) for i in range(8)]

        ident = sb("ident", [P, P])
        ident_b = sb("ident_b", [P, P], BF16)
        causal = sb("causal", [P, HEADS // 2, SEQ], BF16)
        seen = sb("seen", [P, 2])
        ones = sb("ones", [P, 1])
        mhalf = sb("mhalf", [P, 32])
        euler = sb("euler", [P, 32])
        caps = sb("caps", [P, HEADS + 1])
        g1_sb = sb("g1_sb", [P, 1])
        g2_sb = sb("g2_sb", [P, D])
        bo_sb = sb("bo_sb", [P, D])
        br_sb = sb("br_sb", [P, NE])
        bN_sb = sb("bN_sb", [P, NE])
        stage = sb("stage", [P, 512])
        wq_hi, wq_lo = sb("wq_hi", [P, W], F32R), sb("wq_lo", [P, W], F32R)
        wkv_sb = sb("wkv_sb", [P, 2 * DH])
        wout_sb = sb("wout_sb", [P, NBLK, D])
        xwq_sb = sb("xwq_sb", [P, W])
        xwk_sb = sb("xwk_sb", [CD, W])
        xwv_hi, xwv_lo = sb("xwv_hi", [CD, W], F32R), sb("xwv_lo", [CD, W], F32R)
        xwo_sb = sb("xwo_sb", [P, NBLK, D])
        wr_sb = sb("wr_sb", [P, NE])
        wl1_hi, wl1_lo = sb("wl1_hi", [P, NE, 2 * HID], F32R), sb("wl1_lo", [P, NE, 2 * HID], F32R)
        wl2_sb = sb("wl2_sb", [P, NE, NH, D])
        bl1_sb = sb("bl1_sb", [P, NE, 2 * NH])
        bl2_sb = sb("bl2_sb", [NE, D])

        X = sb("X", [P, T, D])

        st = sb("st", [P, 6])
        mv = sb("mv", [P, 2, 2])
        ve = sb("ve", [P, 2, 1])
        rs = sb("rs", [P, 2, 1])
        xn = sb("xn", [P, 2, D])
        xs = sb("xs", [P, 2, D])
        yS = sb("yS", [P, D])
        yg = sb("yg", [P, D])
        vS = sb("vS", [P, 2, DH])
        xT = sb("xT", [P, 2, P])
        xT_hi, xT_lo = sb("xT_hi", [P, 2, P], F32R), sb("xT_lo", [P, 2, P], F32R)
        wide = sb("wide", [P, W + DH])
        ssq = sb("ssq", [P, HEADS + 1])
        rq = sb("rq", [P, HEADS + 1])
        rinv = sb("rinv", [P, HEADS + 1])
        qn = sb("qn", [P, W])
        kn = sb("kn", [P, PB, DH])
        QT = sb("QT", [P, 2, NBLK, P])
        KBD = sb("KBD", [P, 2, PB, NBLK, P])
        VBD = sb("VBD", [P, 2, PB, NBLK, P])
        PR = sb("PR", [P, 2, W])
        PT = sb("PT", [P, W])
        OT = sb("OT", [P, NBLK, P])
        L = sb("L", [P, HEADS])
        rL = sb("rL", [P, 2, HEADS])
        mx = sb("mx", [P, HEADS])
        st2 = sb("st2", [P, 6])
        mv2 = sb("mv2", [P, 2])
        ve2 = sb("ve2", [P, 1])
        rs2 = sb("rs2", [P, 1])
        r1 = sb("r1", [P, D])
        r2 = sb("r2", [P, D])
        st3 = sb("st3", [P, 6])
        mv3 = sb("mv3", [P, 2])
        ve3 = sb("ve3", [P, 1])
        rs3 = sb("rs3", [P, 1])
        cT = sb("cT", [CD, 2, P])
        cT_hi, cT_lo = sb("cT_hi", [CD, 2, P], F32R), sb("cT_lo", [CD, 2, P], F32R)

        xg = sb("xg", [P, GT, D])
        iota8 = sb("iota8", [P, NE])
        topi = sb("topi", [P, GT, 8], mybir.dt.uint32)
        topf = sb("topf", [P, GT, 8])
        sel1 = sb("sel1", [P, GT, NE])
        fT = sb("fT", [P, 2, GN])
        fT_hi, fT_lo = sb("fT_hi", [P, 2, GN], F32R), sb("fT_lo", [P, 2, GN], F32R)
        sg = sb("sg", [P, 2, GN])
        gT = sb("gT", [P, 2, NH, GN])
        sc = sb("sc", [P, GT, NE])
        scb = sb("scb", [P, GT, NE])
        top = sb("top", [P, GT, 8])
        sel = sb("sel", [P, GT, NE])
        smax = sb("smax", [P, GT])
        sh = sb("sh", [P, GT, NE])
        ex = sb("ex", [P, GT, NE])
        exs = sb("exs", [P, GT, NE])
        es = sb("es", [P, GT])
        er = sb("er", [P, GT])
        ew = sb("ew", [P, 2, GT, NE])
        ewT = sb("ewT", [NE, GN])
        yacc = sb("yacc", [P, GT, D])
        fst = sb("fst", [P, GT, 6])
        fmv = sb("fmv", [P, GT, 2])
        fve = sb("fve", [P, GT])
        frs = sb("frs", [P, GT])
        yo = sb("yo", [P, 2, GT, D])

        block = ctx.enter_context(nc.Block())

        x_first, x_rest = sem("x_first"), sem("x_rest")
        w_self, w_cross, w_ffn = sem("w_self"), sem("w_cross"), sem("w_ffn")
        staged, split, consts = sem("staged"), sem("split"), sem("consts")
        zeroed = sem("zeroed")

        slices = []
        for c in range(2):
            slices.append((wqT[:, c * HW:(c + 1) * HW], P, wq_hi[:, c * HW:(c + 1) * HW], wq_lo[:, c * HW:(c + 1) * HW]))
        for c in range(2):
            slices.append((xwv[:, c * HW:(c + 1) * HW], CD, xwv_hi[:, c * HW:(c + 1) * HW],
                           xwv_lo[:, c * HW:(c + 1) * HW]))
        for n in range(NE):
            slices.append((wl1[:, n, :], P, wl1_hi[:, n, :], wl1_lo[:, n, :]))
        SELF_SPLITS, CROSS_SPLITS, ALL_SPLITS = 2, 4, len(slices)

        a = {n: sem("a_" + n) for n in (
            "stats", "aggr", "var", "rstd", "xn", "xT_ps", "xT", "xhi", "xlo", "kv", "q", "sq", "vS", "v", "ssq", "pow",
            "cap", "qn", "kn", "knT", "kbd", "qT_ps", "qT", "s", "exp", "sum", "rl", "norm", "pT_ps", "pT",
            "o", "oT", "y", "yS", "y1", "y2", "y3", "yrstd", "yn", "yr", "z1", "z2", "z3", "zrstd", "x1")}
        b = {n: sem("b_" + n) for n in (
            "ctx", "chi", "clo", "xs", "xT_ps", "xT", "q", "qT", "k", "kbd", "v", "vbd0", "vbd1", "s", "max", "sub", "exp",
            "zero", "sum", "rl", "pT_ps", "pT", "pv", "on", "oT_ps", "oT", "y", "r", "rb", "z1", "z2", "z3", "zrstd", "x2")}
        f = {n: sem("f_" + n) for n in (
            "xs", "xT_ps", "xT", "xhi", "xlo", "sc_ps", "sc", "scb", "top", "topi", "topf", "sel1", "sel", "smax",
            "sh", "ex", "exs", "es", "er", "ew", "ewT_ps", "ewT", "bias", "init", "w1", "silu", "g", "w2", "acc",
            "st", "mv", "ve", "rstd", "yo", "out")}

        def pipeline(eng, body, first, last):
            for i in range(first):
                body(i, i % 2)
            with eng.Fori(first // 2, T // 2 - 1) as j:
                body(2 * j, 0)
                body(2 * j + 1, 1)
            for i in range(T - 2, last + 1):
                body(i, i % 2)

        A_FIRST, B_FIRST = 6, 4

        def ffn_loop(eng, group):
            group(0, 0)
            group(1, 1)
            with eng.Fori(1, G // 2 - 1) as j:
                group(2 * j, 0)
                group(2 * j + 1, 1)
            group(G - 2, 0)
            group(G - 1, 1)

        def dve_wait(sem_, value):
            nc.vector.wait_ge(sem_, value)
            nc.vector.tensor_copy(seen[:, 1:2], seen[:, 0:1])

        def pool_copy(dst, src):
            one = ones[:, :]
            if len(src.shape) == 3:
                one = one.unsqueeze(2)
            return nc.gpsimd.tensor_tensor(dst, src, one.broadcast_to(list(src.shape)), ALU.mult)

        def b_vbd(copy, eng, t, p, c):
            eng.wait_ge(b["v"], 2 * t + c + 1)
            if later(t, 2):
                eng.wait_ge(b["pv"], 2 * (t - 2) + c + 1)
            for s in range(PB):
                for h in range(2):
                    v = copy(VBD[h * DH:(h + 1) * DH, p, s, c * HBLK:(c + 1) * HBLK, h * DH:(h + 1) * DH],
                             bank[2 + c][s * SEQ:(s + 1) * SEQ, :].rearrange("k (a h d) -> k a h d", a=HBLK, h=2)
                             [:, :, h, :])
            v.then_inc(b["vbd1" if c else "vbd0"], 1)

        def stage_of(fn, i, p, back):
            t = i - back
            if isinstance(t, int) and not 0 <= t < T:
                return
            fn(t, (p - back) % 2)

        @block.sync
        def _(sp):
            x_v = x.rearrange("(t p) d -> p t d", p=P)
            sp.dma_start(X[:, 0:4, :], x_v[:, 0:4, :]).then_inc(x_first, 16)
            small = ((g1_sb[:, :], g1.rearrange("(p a) -> p a", a=1)), (wkv_sb[:, :], wkvT))
            for dst, src in small:
                sp.dma_start(dst, src).then_inc(w_self, 16)
            for n, (src, rows, _, _) in enumerate(slices):
                if n:
                    sp.wait_ge(split, 2 * n)
                sp.dma_start(stage[0:rows, :], src).then_inc(staged, 16)
                if n == 0:
                    sp.dma_start(wout_sb[:, :, :], woutT).then_inc(w_self, 16)
                    sp.dma_start(g2_sb[:, :], g2.partition_broadcast(P)).then_inc(w_self, 16)
                if n == 1:
                    sp.dma_start(X[:, 4:T, :], x_v[:, 4:T, :]).then_inc(x_rest, 16)

        @block.gpsimd
        def _(pool):
            nc.gpsimd.memset(ident[:, :], 1.0).then_inc(consts, 1)
            nc.gpsimd.memset(ones[:, :], 1.0)
            nc.gpsimd.memset(ident_b[:, :], 1.0)
            nc.gpsimd.memset(causal[:, :, :], 0.0).then_inc(consts, 1)
            nc.gpsimd.memset(mhalf[:, :], -0.5).then_inc(consts, 1)
            nc.gpsimd.memset(euler[:, :], 2.718281828459045).then_inc(consts, 1)
            nc.gpsimd.memset(caps[:, 0:HEADS], 16.0e12).then_inc(consts, 1)
            nc.gpsimd.memset(caps[:, HEADS:HEADS + 1], 1.0e12).then_inc(consts, 1)
            pool.wait_ge(consts, 6)
            nc.gpsimd.affine_select(out=ident[:, :], in_=ident[:, :], compare_op=ALU.is_equal, fill=0.0, base=0,
                                    pattern=[[-1, P]], channel_multiplier=1).then_inc(consts, 1)
            pool.wait_ge(consts, 7)
            nc.gpsimd.iota(iota8[:, :], pattern=[[1, NE]], base=0, channel_multiplier=0,
                           allow_small_or_imprecise_dtypes=True).then_inc(consts, 1)
            for h in range(PB):
                pool.wait_ge(consts, 8 + h)
                c = causal[h * SEQ:(h + 1) * SEQ, :, :]
                nc.gpsimd.affine_select(out=c, in_=c, compare_op=ALU.is_ge, fill=FUTURE, base=0,
                                        pattern=[[0, HEADS // 2], [-1, SEQ]], channel_multiplier=1)\
                  .then_inc(consts, 1)
            pool.wait_ge(consts, 8 + PB)
            nc.gpsimd.affine_select(out=ident_b[:, :], in_=ident_b[:, :], compare_op=ALU.is_equal, fill=0.0, base=0,
                                    pattern=[[-1, P]], channel_multiplier=1).then_inc(consts, 1)
            nc.gpsimd.dma_start(xwq_sb[:, :], xwq).then_inc(w_cross, 16)
            nc.gpsimd.dma_start(xwk_sb[:, :], xwk).then_inc(w_cross, 16)
            nc.gpsimd.dma_start(xwo_sb[:, :, :], xwo).then_inc(w_cross, 16)
            nc.gpsimd.dma_start(bo_sb[:, :], bo.partition_broadcast(P)).then_inc(w_cross, 16)
            nc.gpsimd.dma_start(wr_sb[:, :], wrT).then_inc(w_ffn, 16)
            nc.gpsimd.dma_start(br_sb[:, :], br.partition_broadcast(P)).then_inc(w_ffn, 16)
            nc.gpsimd.dma_start(bN_sb[:, :], bN.partition_broadcast(P)).then_inc(w_ffn, 16)
            nc.gpsimd.dma_start(wl2_sb[:, :, :, :], wl2).then_inc(w_ffn, 16)
            nc.gpsimd.dma_start(bl1_sb[:, :, :], bl1).then_inc(w_ffn, 16)
            nc.gpsimd.dma_start(bl2_sb[:, :], bl2).then_inc(w_ffn, 16)
            pool.wait_ge(consts, 11)

            def ln_in(t, p):
                pool.wait_ge(a["var"], t + 1)
                nc.gpsimd.tensor_tensor(rs[:, p, :], ve[:, p, :], mhalf[:, 0:1], ALU.pow).then_inc(a["rstd"], 1)

            def norms(t, p):
                pool.wait_ge(a["ssq"], t + 1)
                if later(t, 1):
                    pool.wait_ge(a["cap"], t)
                nc.gpsimd.tensor_tensor(rq[:, :], ssq[:, :], mhalf[:, 0:HEADS + 1], ALU.pow).then_inc(a["pow"], 1)

            def weights(t, p):
                pool.wait_ge(a["rl"], t + 1)
                v = PR[:, p, :].rearrange("q (h k) -> q h k", k=SEQ)
                nc.gpsimd.tensor_tensor(v, v, rL[:, p, :].unsqueeze(2).broadcast_to([P, HEADS, SEQ]), ALU.mult)\
                  .then_inc(a["norm"], 1)

            def y_rstd(t, p):
                pool.wait_ge(a["y3"], t + 1)
                nc.gpsimd.tensor_tensor(rs2[:, :], ve2[:, :], mhalf[:, 0:1], ALU.pow).then_inc(a["yrstd"], 1)

            def z_rstd(t, p):
                pool.wait_ge(a["z3"], t + 1)
                nc.gpsimd.tensor_tensor(rs3[:, :], ve3[:, :], mhalf[:, 0:1], ALU.pow).then_inc(a["zrstd"], 1)

            def body(i, p):
                if isinstance(i, int) and i == 0:
                    ln_in(0, 0)
                stage_of(ln_in, i, p, -1)
                stage_of(y_rstd, i, p, 4)
                stage_of(norms, i, p, 0)
                stage_of(z_rstd, i, p, 4)
                stage_of(weights, i, p, 1)
            pipeline(pool, body, A_FIRST, T + 3)

            def fetch(t, p):
                pool.wait_ge(a["x1"], t + 1)
                if later(t, 2):
                    pool.wait_ge(b["xT_ps"], t - 1)
                pool_copy(xs[:, p, :], X[:, bass.ds(t, 1), :].rearrange("q a d -> q (a d)"))\
                  .then_inc(b["xs"], 1)

            def cross_tail(t, p):
                pool.wait_ge(b["z3"], t + 1)
                nc.gpsimd.tensor_tensor(rs3[:, :], ve3[:, :], mhalf[:, 0:1], ALU.pow).then_inc(b["zrstd"], 1)

            def cross(i, p):
                if isinstance(i, int) and i == 0:
                    fetch(0, 0)
                stage_of(fetch, i, p, -1)
                stage_of(cross_tail, i, p, 3)
            pipeline(pool, cross, B_FIRST, T + 2)

            def group_front(g, p):
                pool.wait_ge(b["x2"], GT * (g + 1))
                if later(g, 1):
                    pool.wait_ge(f["xT_ps"], g)
                pool_copy(xg[:, :, :], X[:, bass.ds(g * GT, GT), :]).then_inc(f["xs"], 1)
                pool.wait_ge(f["sh"], g + 1)
                nc.gpsimd.tensor_tensor(ex[:, :, :].rearrange("p a b -> p (a b)"), euler[:, 0:GT * NE],
                                        sh[:, :, :].rearrange("p a b -> p (a b)"), ALU.pow).then_inc(f["ex"], 1)

            def group_tail(g, p):
                pool.wait_ge(f["ve"], g + 1)
                nc.gpsimd.tensor_tensor(frs[:, :], fve[:, :], mhalf[:, 0:GT], ALU.pow).then_inc(f["rstd"], 1)

            def group(g, p):
                if later(g, 1):
                    group_tail(g - 1, 1 - p)
                if not (isinstance(g, int) and g == G - 1):
                    group_front(g + 1, 1 - p)
            group_front(0, 0)
            ffn_loop(pool, group)
            group_tail(G - 1, 1)

        @block.scalar
        def _(act):
            def x_T(t, p):
                act.wait_ge(a["xT_ps"], t + 1)
                if later(t, 2):
                    act.wait_ge(a["q"], 2 * (t - 1))
                    act.wait_ge(a["xlo"], t - 1)
                nc.scalar.activation(xT[:, p, :], bank[0][:, 0:P], ACT.Copy, scale=g1_sb[:, 0:1]).then_inc(a["xT"], 1)
                act.wait_ge(a["xT"], t + 1)
                nc.scalar.activation(xT_hi[:, p, :], xT[:, p, :], ACT.Copy).then_inc(a["xhi"], 1)

            def squares(t, p):
                act.wait_ge(a["kv"], t + 1)
                if later(t, 1):
                    act.wait_ge(a["ssq"], t)
                nc.scalar.activation(wide[:, W:W + DH], bank[1][:, 0:DH], ACT.Square).then_inc(a["sq"], 1)
                if later(t, 2):
                    act.wait_ge(a["v"], t - 1)
                nc.scalar.activation(vS[:, p, :], bank[1][:, DH:2 * DH], ACT.Copy).then_inc(a["vS"], 1)
                for c in range(2):
                    act.wait_ge(a["q"], 2 * t + c + 1)
                    nc.scalar.activation(wide[:, c * HW:(c + 1) * HW], bank[2 + c][:, :], ACT.Square)\
                      .then_inc(a["sq"], 1)

            def q_T(t, p):
                act.wait_ge(a["knT"], t + 1)
                if later(t, 2):
                    act.wait_ge(a["s"], 2 * (t - 1))
                for h in range(2):
                    r = slice(h * DH, (h + 1) * DH)
                    k = nc.scalar.activation(KBD[r, p, :, 0, r], bank[7][r, 0:P].rearrange("d (s k) -> d s k", s=PB),
                                             ACT.Copy)
                k.then_inc(a["kbd"], 1)
                for c in range(2):
                    act.wait_ge(a["qT_ps"], 2 * t + c + 1)
                    nc.scalar.activation(QT[:, p, c * HBLK:(c + 1) * HBLK, :].rearrange("d a q -> d (a q)"),
                                         bank[4 + c][:, :], ACT.Copy).then_inc(a["qT"], 1)

            def exp_half(t, p, c):
                if later(t, 2):
                    act.wait_ge(a["pT_ps"], 2 * (t - 1))
                act.wait_ge(a["s"], 2 * t + c + 1)
                nc.scalar.activation(PR[:, p, c * HW:(c + 1) * HW], bank[6][:, :], ACT.Exp, scale=16.0)\
                  .then_inc(a["exp"], 1)

            def p_T(t, p, c):
                if later(t, 1):
                    act.wait_ge(a["o"], 2 * t)
                v = PT[:, :].rearrange("k (s a q) -> k s a q", s=PB, a=NBLK)
                act.wait_ge(a["pT_ps"], 2 * t + c + 1)
                nc.scalar.activation(v[:, :, c * HBLK:(c + 1) * HBLK, :],
                                     bank[4 + c][:, :].rearrange("k (a s q) -> k s a q", a=HBLK, s=PB),
                                     ACT.Copy).then_inc(a["pT"], 1)

            def o_T(t, p, s):
                if later(t, 1):
                    act.wait_ge(a["y"], t)
                act.wait_ge(a["o"], 2 * t + s + 1)
                nc.scalar.activation(OT[:, :, s * SEQ:(s + 1) * SEQ],
                                     bank[0 if s else 7][:, :].rearrange("d (a q) -> d a q", a=NBLK), ACT.Copy)\
                  .then_inc(a["oT"], 1)

            def y_evac(t, p):
                act.wait_ge(a["y"], t + 1)
                if later(t, 1):
                    act.wait_ge(a["yn"], t)
                nc.scalar.activation(yS[:, :], bank[0][:, 0:D], ACT.Copy).then_inc(a["yS"], 1)

            act.wait_ge(w_self, 64)
            act.wait_ge(zeroed, 1)

            def body(i, p):
                if isinstance(i, int) and i == 0:
                    x_T(0, 0)
                stage_of(squares, i, p, 0)
                stage_of(q_T, i, p, 1)
                stage_of(y_evac, i, p, 3)
                stage_of(lambda t, q: exp_half(t, q, 0), i, p, 1)
                stage_of(lambda t, q: p_T(t, q, 0), i, p, 2)
                stage_of(lambda t, q: p_T(t, q, 1), i, p, 2)
                stage_of(x_T, i, p, -1)
                stage_of(lambda t, q: exp_half(t, q, 1), i, p, 1)
                stage_of(lambda t, q: o_T(t, q, 0), i, p, 2)
                stage_of(lambda t, q: o_T(t, q, 1), i, p, 2)
            pipeline(act, body, A_FIRST, T + 3)

            act.dma_start(cT[:, 0, :], ctxT[:, 0:P]).then_inc(b["ctx"], 16)
            act.wait_ge(a["x1"], T)
            act.wait_ge(b["zero"], 1)

            def bx_T(t, p):
                act.wait_ge(b["xT_ps"], t + 1)
                if later(t, 2):
                    act.wait_ge(b["q"], 2 * (t - 1))
                nc.scalar.activation(xT[:, p, :], bank[0][:, 0:P], ACT.Copy).then_inc(b["xT"], 1)

            def c_hi(t, p):
                act.wait_ge(b["ctx"], 16 * (t + 1))
                if later(t, 2):
                    act.wait_ge(b["v"], 2 * (t - 1))
                nc.scalar.activation(cT_hi[:, p, :], cT[:, p, :], ACT.Copy).then_inc(b["chi"], 1)

            def load_ctx(t, p):
                if later(t, 1):
                    act.wait_ge(b["ctx"], 16 * t)
                if later(t, 2):
                    act.wait_ge(b["k"], 2 * (t - 1))
                    act.wait_ge(b["chi"], t - 1)
                    act.wait_ge(b["clo"], t - 1)
                act.dma_start(cT[:, p, :], ctxT[:, bass.ds(t * P, P)]).then_inc(b["ctx"], 16)

            def b_q(t, p, c):
                if later(t, 2):
                    act.wait_ge(b["s"], 2 * (t - 1))
                act.wait_ge(b["q"], 2 * t + c + 1)
                nc.scalar.activation(QT[:, p, c * HBLK:(c + 1) * HBLK, :].rearrange("d a q -> d (a q)"),
                                     bank[2 + c][:, :], ACT.Copy).then_inc(b["qT"], 1)

            def b_k(t, p, c):
                act.wait_ge(b["k"], 2 * t + c + 1)
                for h in range(2):
                    r = slice(h * DH, (h + 1) * DH)
                    k = nc.scalar.activation(KBD[r, p, :, c * HBLK:(c + 1) * HBLK, r],
                                             bank[2 + c][r, :].rearrange("d (a s k) -> d s a k", a=HBLK, s=PB),
                                             ACT.Copy)
                k.then_inc(b["kbd"], 1)

            def b_exp(t, p, c):
                act.wait_ge(b["sub"], 2 * t + c + 1)
                v = PR[:, p, c * HW:(c + 1) * HW]
                nc.scalar.activation(v, v, ACT.Exp, scale=DH ** -0.5).then_inc(b["exp"], 1)

            def b_oT(t, p):
                if later(t, 1):
                    act.wait_ge(b["y"], t)
                for c in range(2):
                    act.wait_ge(b["oT_ps"], 2 * t + c + 1)
                    nc.scalar.activation(OT[:, c * HBLK:(c + 1) * HBLK, :].rearrange("d a q -> d (a q)"),
                                         bank[4 + c][:, :], ACT.Copy).then_inc(b["oT"], 1)

            def b_pT(t, p):
                if later(t, 1):
                    act.wait_ge(b["pv"], 2 * t)
                for c in range(2):
                    act.wait_ge(b["pT_ps"], 2 * t + c + 1)
                    nc.scalar.activation(PT[:, c * HW:(c + 1) * HW], bank[4 + c][:, :], ACT.Copy)\
                      .then_inc(b["pT"], 1)

            def cross(i, p):
                if isinstance(i, int) and i == 0:
                    load_ctx(1, 1)
                    c_hi(0, 0)
                    bx_T(0, 0)
                stage_of(lambda t, q: b_q(t, q, 0), i, p, 0)
                stage_of(b_oT, i, p, 3)
                stage_of(lambda t, q: b_exp(t, q, 0), i, p, 1)
                stage_of(lambda t, q: b_q(t, q, 1), i, p, 0)
                stage_of(lambda t, q: b_k(t, q, 0), i, p, 0)
                stage_of(lambda t, q: b_exp(t, q, 1), i, p, 1)
                stage_of(b_pT, i, p, 2)
                stage_of(lambda t, q: b_k(t, q, 1), i, p, 0)
                stage_of(bx_T, i, p, -1)
                stage_of(c_hi, i, p, -1)
                stage_of(load_ctx, i, p, -2)
                stage_of(lambda t, q: b_vbd(nc.scalar.copy, act, t, q, 1), i, p, 0)
            pipeline(act, cross, B_FIRST, T + 2)

            act.wait_ge(w_ffn, 96)

            def front_x(g, p):
                act.wait_ge(f["xT_ps"], g + 1)
                if later(g, 2):
                    act.wait_ge(f["sc_ps"], g - 1)
                    act.wait_ge(f["xlo"], g - 1)
                nc.scalar.activation(fT[:, p, :], bank[6][:, :], ACT.Copy).then_inc(f["xT"], 1)
                act.wait_ge(f["xT"], g + 1)
                if later(g, 2):
                    act.wait_ge(f["w1"], 2 * NH * NE * (g - 1))
                nc.scalar.activation(fT_hi[:, p, :], fT[:, p, :], ACT.Copy).then_inc(f["xhi"], 1)

            def front_ew(g, p):
                act.wait_ge(f["ewT_ps"], g + 1)
                if later(g, 1):
                    act.wait_ge(f["bias"], g)
                nc.scalar.activation(ewT[:, :], bank[6][0:NE, :], ACT.Copy).then_inc(f["ewT"], 1)

            out_v = out.rearrange("(t p) d -> p t d", p=P)

            def store(g, p):
                act.wait_ge(f["yo"], g + 1)
                if later(g, 1):
                    act.wait_ge(f["out"], 16 * g)
                act.dma_start(out_v[:, bass.ds(g * GT, GT), :], yo[:, p, :, :]).then_inc(f["out"], 16)

            def silus(g, n):
                for c in range(NH):
                    k = NE * NH * g + NH * n + c
                    act.wait_ge(f["w1"], 2 * k + 1)
                    if later(k, NH):
                        act.wait_ge(f["g"], k - NH + 1)
                    nc.scalar.activation(sg[:, c, :], bank[2 * c][:, :], ACT.Silu, bias=bl1_sb[:, n, c:c + 1])\
                      .then_inc(f["silu"], 1)

            def group(g, p):
                more = not (isinstance(g, int) and g == G - 1)
                for n in range(NE):
                    silus(g, n)
                    if n == 1 and more:
                        front_x(g + 1, 1 - p)
                    if n == 6 and more:
                        front_ew(g + 1, 1 - p)
                    if n == 4 and later(g, 1):
                        store(g - 1, 1 - p)
            front_x(0, 0)
            front_ew(0, 0)
            ffn_loop(act, group)
            store(G - 1, 1)
            act.wait_ge(f["out"], 16 * G)

        @block.vector
        def _(dve):
            V = nc.vector

            V.memset(seen[:, :], 0.0)
            V.memset(KBD[:, :, :, 0, :], 0.0)
            V.memset(VBD[:, :, :, 0, :], 0.0).then_inc(zeroed, 1)

            def split_slice(n):
                _, rows, hi, lo = slices[n]
                dve.wait_ge(staged, 16 * (n + 1))
                V.tensor_copy(hi, stage[0:rows, :]).then_inc(split, 1)
                dve.wait_ge(split, 2 * n + 1)
                V.tensor_tensor(lo, stage[0:rows, :], hi.bitcast(F32), ALU.subtract).then_inc(split, 1)

            def ln_a(t, p):
                V.bn_stats(st[:, :], X[:, bass.ds(t, 1), :].rearrange("q a d -> q (a d)")).then_inc(a["stats"], 1)
                dve_wait(a["stats"], t + 1)
                V.bn_aggr(mv[:, p, :], st[:, :]).then_inc(a["aggr"], 1)
                dve.wait_ge(a["aggr"], t + 1)
                V.tensor_scalar(ve[:, p, :], mv[:, p, 1:2], EPS, None, ALU.add).then_inc(a["var"], 1)

            def ln_b(t, p):
                dve.wait_ge(a["rstd"], t + 1)
                if later(t, 2):
                    dve.wait_ge(a["xT_ps"], t - 1)
                V.tensor_scalar(xn[:, p, :], X[:, bass.ds(t, 1), :].rearrange("q a d -> q (a d)"), mv[:, p, 0:1],
                                rs[:, p, :], ALU.subtract, ALU.mult).then_inc(a["xn"], 1)

            def x_lo(t, p):
                dve.wait_ge(a["xhi"], t + 1)
                V.tensor_tensor(xT_lo[:, p, :], xT[:, p, :], xT_hi[:, p, :].bitcast(F32), ALU.subtract)\
                  .then_inc(a["xlo"], 1)

            def sums(t, p):
                dve.wait_ge(a["sq"], 3 * (t + 1))
                if later(t, 1):
                    dve.wait_ge(a["pow"], t)
                V.tensor_reduce(ssq[:, :], wide[:, :].rearrange("q (h d) -> q h d", d=DH), AX.X, ALU.add)\
                 .then_inc(a["ssq"], 1)

            def normalise(t, p):
                dve.wait_ge(a["pow"], t + 1)
                if later(t, 1):
                    dve.wait_ge(a["kn"], t)
                V.tensor_tensor(rinv[:, :], rq[:, :], caps[:, :], ALU.min).then_inc(a["cap"], 1)
                dve.wait_ge(a["cap"], t + 1)
                dve.wait_ge(a["vS"], t + 1)
                if later(t, 1):
                    dve.wait_ge(a["knT"], t)
                V.tensor_scalar(kn[:, :, :], bank[1][:, 0:DH].unsqueeze(1).broadcast_to([P, PB, DH]),
                                rinv[:, HEADS:HEADS + 1], None, ALU.mult).then_inc(a["kn"], 1)
                for c in range(2):
                    if later(t, 1):
                        dve.wait_ge(a["qT_ps"], 2 * t)
                    hs = slice(c * HEADS // 2, (c + 1) * HEADS // 2)
                    V.tensor_tensor(qn[:, c * HW:(c + 1) * HW].rearrange("q (h d) -> q h d", d=DH),
                                    bank[2 + c][:, :].rearrange("q (h d) -> q h d", d=DH),
                                    rinv[:, hs].unsqueeze(2).broadcast_to([P, HEADS // 2, DH]), ALU.mult)\
                     .then_inc(a["qn"], 1)

            def v_bd(t, p):
                dve.wait_ge(a["vS"], t + 1)
                if later(t, 2):
                    dve.wait_ge(a["o"], 2 * (t - 1))
                for s in range(PB):
                    for h in range(2):
                        v = V.tensor_copy(VBD[h * DH:(h + 1) * DH, p, s, 0, h * DH:(h + 1) * DH],
                                          vS[s * SEQ:(s + 1) * SEQ, p, :])
                v.then_inc(a["v"], 1)

            def softmax(t, p):
                dve.wait_ge(a["exp"], 2 * (t + 1))
                v = PR[:, p, :].rearrange("q (h k) -> q h k", k=SEQ)
                V.tensor_reduce(L[:, :], v, AX.X, ALU.add).then_inc(a["sum"], 1)
                dve.wait_ge(a["sum"], t + 1)
                V.reciprocal(rL[:, p, :], L[:, :]).then_inc(a["rl"], 1)

            def tail_a(t, p):
                dve.wait_ge(a["yS"], t + 1)
                V.bn_stats(st2[:, :], yS[:, :]).then_inc(a["y1"], 1)
                dve_wait(a["y1"], t + 1)
                V.bn_aggr(mv2[:, :], st2[:, :]).then_inc(a["y2"], 1)
                dve.wait_ge(a["y2"], t + 1)
                V.tensor_scalar(ve2[:, :], mv2[:, 1:2], EPS, None, ALU.add).then_inc(a["y3"], 1)
                V.scalar_tensor_tensor(out=yg[:, :], in0=yS[:, :], scalar=mv2[:, 0:1], in1=g2_sb[:, :],
                                       op0=ALU.subtract, op1=ALU.mult).then_inc(a["yn"], 1)

            def tail_b(t, p):
                dve.wait_ge(a["yrstd"], t + 1)
                if later(t, 1):
                    dve.wait_ge(a["x1"], t)
                dve.wait_ge(a["yn"], t + 1)
                V.scalar_tensor_tensor(out=r1[:, :], in0=yg[:, :], scalar=rs2[:, :],
                                       in1=X[:, bass.ds(t, 1), :].rearrange("q a d -> q (a d)"),
                                       op0=ALU.mult, op1=ALU.add).then_inc(a["yr"], 1)
                dve.wait_ge(a["yr"], t + 1)
                V.bn_stats(st3[:, :], r1[:, :]).then_inc(a["z1"], 1)
                dve_wait(a["z1"], t + 1)
                V.bn_aggr(mv3[:, :], st3[:, :]).then_inc(a["z2"], 1)
                dve.wait_ge(a["z2"], t + 1)
                V.tensor_scalar(ve3[:, :], mv3[:, 1:2], EPS, None, ALU.add).then_inc(a["z3"], 1)

            def tail_c(t, p):
                dve.wait_ge(a["zrstd"], t + 1)
                V.tensor_scalar(X[:, bass.ds(t, 1), :].rearrange("q a d -> q (a d)"), r1[:, :], mv3[:, 0:1],
                                rs3[:, :], ALU.subtract, ALU.mult).then_inc(a["x1"], 1)

            dve.wait_ge(x_first, 16)
            for n in range(SELF_SPLITS):
                split_slice(n)
            dve.wait_ge(consts, 11)
            dve.wait_ge(w_self, 64)

            def body(i, p):
                if isinstance(i, int) and i == 0:
                    ln_a(0, 0)
                    ln_b(0, 0)
                    x_lo(0, 0)
                if isinstance(i, int) and i == 3:
                    dve.wait_ge(x_rest, 16)
                stage_of(ln_a, i, p, -1)
                stage_of(sums, i, p, 0)
                stage_of(tail_b, i, p, 4)
                stage_of(ln_b, i, p, -1)
                stage_of(tail_a, i, p, 3)
                stage_of(v_bd, i, p, 1)
                stage_of(normalise, i, p, 0)
                stage_of(x_lo, i, p, -1)
                stage_of(softmax, i, p, 1)
                stage_of(tail_c, i, p, 4)
                if isinstance(i, int) and i < 5:
                    for n in range(SELF_SPLITS + 2 * i, SELF_SPLITS + 2 * i + 2):
                        split_slice(n)
            pipeline(dve, body, A_FIRST, T + 3)

            V.memset(KBD[:, :, :, 1:NBLK, :], 0.0)
            V.memset(VBD[:, :, :, 1:NBLK, :], 0.0).then_inc(b["zero"], 1)

            def c_lo(t, p):
                dve.wait_ge(b["chi"], t + 1)
                if later(t, 2):
                    dve.wait_ge(b["v"], 2 * (t - 1))
                V.tensor_tensor(cT_lo[:, p, :], cT[:, p, :], cT_hi[:, p, :].bitcast(F32), ALU.subtract)\
                 .then_inc(b["clo"], 1)

            def b_max(t, p, c):
                dve.wait_ge(b["s"], 2 * t + c + 1)
                v = bank[6][:, :].rearrange("q (h k) -> q h k", k=SEQ)
                V.tensor_reduce(mx[:, 0:HEADS // 2], v, AX.X, ALU.max).then_inc(b["max"], 1)
                dve.wait_ge(b["max"], 2 * t + c + 1)
                if later(t, 2):
                    dve.wait_ge(b["pT_ps"], 2 * (t - 1))
                V.tensor_tensor(PR[:, p, c * HW:(c + 1) * HW].rearrange("q (h k) -> q h k", k=SEQ), v,
                                mx[:, 0:HEADS // 2].unsqueeze(2).broadcast_to([P, HEADS // 2, SEQ]), ALU.subtract)\
                 .then_inc(b["sub"], 1)

            def b_sum(t, p):
                dve.wait_ge(b["exp"], 2 * (t + 1))
                V.tensor_reduce(L[:, :], PR[:, p, :].rearrange("q (h k) -> q h k", k=SEQ), AX.X, ALU.add)\
                 .then_inc(b["sum"], 1)
                dve.wait_ge(b["sum"], t + 1)
                V.reciprocal(rL[:, p, :], L[:, :]).then_inc(b["rl"], 1)

            def b_on(t, p, c):
                dve.wait_ge(b["pv"], 2 * t + c + 1)
                dve.wait_ge(b["rl"], t + 1)
                if later(t, 1):
                    dve.wait_ge(b["oT_ps"], 2 * t)
                hs = slice(c * HEADS // 2, (c + 1) * HEADS // 2)
                V.tensor_tensor(wide[:, c * HW:(c + 1) * HW].rearrange("q (h d) -> q h d", d=DH),
                                bank[7][:, :].rearrange("q (h d) -> q h d", d=DH),
                                rL[:, p, hs].unsqueeze(2).broadcast_to([P, HEADS // 2, DH]), ALU.mult)\
                 .then_inc(b["on"], 1)

            def b_tail_a(t, p):
                dve.wait_ge(b["y"], t + 1)
                V.tensor_tensor(r1[:, :], bank[1][:, 0:D], X[:, bass.ds(t, 1), :].rearrange("q a d -> q (a d)"),
                                ALU.add).then_inc(b["r"], 1)
                dve.wait_ge(b["r"], t + 1)
                V.tensor_tensor(r2[:, :], r1[:, :], bo_sb[:, :], ALU.add).then_inc(b["rb"], 1)
                dve.wait_ge(b["rb"], t + 1)
                V.bn_stats(st3[:, :], r2[:, :]).then_inc(b["z1"], 1)
                dve_wait(b["z1"], t + 1)
                V.bn_aggr(mv3[:, :], st3[:, :]).then_inc(b["z2"], 1)
                dve.wait_ge(b["z2"], t + 1)
                V.tensor_scalar(ve3[:, :], mv3[:, 1:2], EPS, None, ALU.add).then_inc(b["z3"], 1)

            def b_tail_b(t, p):
                dve.wait_ge(b["zrstd"], t + 1)
                V.tensor_scalar(X[:, bass.ds(t, 1), :].rearrange("q a d -> q (a d)"), r2[:, :], mv3[:, 0:1],
                                rs3[:, :], ALU.subtract, ALU.mult).then_inc(b["x2"], 1)

            dve.wait_ge(w_cross, 64)

            def cross(i, p):
                if isinstance(i, int) and i == 0:
                    c_lo(0, 0)
                stage_of(lambda t, q: b_max(t, q, 0), i, p, 1)
                stage_of(lambda t, q: b_max(t, q, 1), i, p, 1)
                stage_of(b_sum, i, p, 1)
                stage_of(b_tail_a, i, p, 3)
                stage_of(lambda t, q: b_on(t, q, 0), i, p, 2)
                stage_of(lambda t, q: b_vbd(V.tensor_copy, dve, t, q, 0), i, p, 0)
                stage_of(lambda t, q: b_on(t, q, 1), i, p, 2)
                stage_of(b_tail_b, i, p, 3)
                stage_of(c_lo, i, p, -1)
            pipeline(dve, cross, B_FIRST, T + 2)

            dve.wait_ge(w_ffn, 96)

            def front(g, p):
                dve.wait_ge(f["xhi"], g + 1)
                if later(g, 2):
                    dve.wait_ge(f["w1"], 2 * NH * NE * (g - 1))
                V.tensor_tensor(fT_lo[:, p, :], fT[:, p, :], fT_hi[:, p, :].bitcast(F32), ALU.subtract)\
                 .then_inc(f["xlo"], 1)

            def router(g, p):
                shape = [P, GT, NE]
                dve.wait_ge(f["sc_ps"], g + 1)
                V.tensor_tensor(sc[:, :, :], bank[7][:, 0:GT * NE].rearrange("p (a b) -> p a b", a=GT),
                                br_sb[:, :].unsqueeze(1).broadcast_to(shape), ALU.add).then_inc(f["sc"], 1)
                dve.wait_ge(f["sc"], g + 1)
                V.tensor_tensor(scb[:, :, :], sc[:, :, :], bN_sb[:, :].unsqueeze(1).broadcast_to(shape), ALU.add)\
                 .then_inc(f["scb"], 1)
                V.tensor_reduce(smax[:, :], sc[:, :, :], AX.X, ALU.max).then_inc(f["smax"], 1)
                dve.wait_ge(f["smax"], g + 1)
                V.tensor_tensor(sh[:, :, :], sc[:, :, :], smax[:, :].unsqueeze(2).broadcast_to(shape), ALU.subtract)\
                 .then_inc(f["sh"], 1)
                dve_wait(f["scb"], g + 1)
                for k in range(GT):
                    V.max(top[:, k, :], scb[:, k, :]).then_inc(f["top"], 1)
                dve_wait(f["top"], GT * (g + 1))
                for k in range(GT):
                    m = V.max_index(topi[:, k, :], top[:, k, :], scb[:, k, :])
                m.then_inc(f["topi"], 1)
                dve.wait_ge(f["topi"], g + 1)
                V.tensor_copy(topf[:, :, :], topi[:, :, :]).then_inc(f["topf"], 1)
                dve.wait_ge(f["topf"], g + 1)
                io = iota8[:, :].unsqueeze(1).broadcast_to(shape)
                V.tensor_tensor(sel[:, :, :], io, topf[:, :, 0:1].broadcast_to(shape), ALU.is_equal)
                V.tensor_tensor(sel1[:, :, :], io, topf[:, :, 1:2].broadcast_to(shape), ALU.is_equal)\
                 .then_inc(f["sel1"], 1)
                dve.wait_ge(f["sel1"], g + 1)
                V.tensor_tensor(sel[:, :, :], sel[:, :, :], sel1[:, :, :], ALU.add).then_inc(f["sel"], 1)

            def router_weights(g, p):
                shape = [P, GT, NE]
                dve.wait_ge(f["sel"], g + 1)
                dve.wait_ge(f["ex"], g + 1)
                V.tensor_tensor(exs[:, :, :], ex[:, :, :], sel[:, :, :], ALU.mult).then_inc(f["exs"], 1)
                dve.wait_ge(f["exs"], g + 1)
                V.tensor_reduce(es[:, :], exs[:, :, :], AX.X, ALU.add).then_inc(f["es"], 1)
                dve.wait_ge(f["es"], g + 1)
                V.reciprocal(er[:, :], es[:, :]).then_inc(f["er"], 1)
                dve.wait_ge(f["er"], g + 1)
                V.tensor_tensor(ew[:, p, :, :], exs[:, :, :], er[:, :].unsqueeze(2).broadcast_to(shape), ALU.mult)\
                 .then_inc(f["ew"], 1)

            def gates(g, n):
                q = n % 2
                for c in range(NH):
                    k = NE * NH * g + NH * n + c
                    dve.wait_ge(f["silu"], k + 1)
                    dve.wait_ge(f["w1"], 2 * k + 2)
                    if c == 0 and later(NE * g + n, 2):
                        dve.wait_ge(f["w2"], NE * g + n - 1)
                    V.scalar_tensor_tensor(out=gT[:, q, c, :], in0=bank[2 * c + 1][:, :],
                                           scalar=bl1_sb[:, n, NH + c:NH + c + 1], in1=sg[:, c, :],
                                           op0=ALU.add, op1=ALU.mult).then_inc(f["g"], 1)

            def accumulate(g, n, p):
                k = NE * g + n
                dve.wait_ge(f["w2"], k + 1)
                dve.wait_ge(f["init"], g + 1)
                if later(k, 1):
                    dve.wait_ge(f["acc"], k)
                for tt in range(GT):
                    m = V.scalar_tensor_tensor(out=yacc[:, tt, :], in0=bank[4 + n % 2][:, tt * D:(tt + 1) * D],
                                               scalar=ew[:, p, tt, n:n + 1], in1=yacc[:, tt, :],
                                               op0=ALU.mult, op1=ALU.add)
                m.then_inc(f["acc"], 1)

            def init(g, p):
                dve.wait_ge(f["bias"], g + 1)
                V.tensor_tensor(yacc[:, :, :], bank[7][:, :].rearrange("p (a d) -> p a d", a=GT),
                                X[:, bass.ds(g * GT, GT), :], ALU.add).then_inc(f["init"], 1)

            def out_a(g):
                dve.wait_ge(f["acc"], NE * (g + 1))
                for tt in range(GT):
                    m = V.bn_stats(fst[:, tt, :], yacc[:, tt, :])
                m.then_inc(f["st"], 1)
                dve_wait(f["st"], g + 1)
                for tt in range(GT):
                    m = V.bn_aggr(fmv[:, tt, :], fst[:, tt, :])
                m.then_inc(f["mv"], 1)
                dve.wait_ge(f["mv"], g + 1)
                V.tensor_scalar(fve[:, :], fmv[:, :, 1], EPS, None, ALU.add).then_inc(f["ve"], 1)

            def out_b(g, p):
                dve.wait_ge(f["rstd"], g + 1)
                if later(g, 2):
                    dve.wait_ge(f["out"], 16 * (g - 1))
                for tt in range(GT):
                    m = V.tensor_scalar(yo[:, p, tt, :], yacc[:, tt, :], fmv[:, tt, 0:1], frs[:, tt:tt + 1],
                                        ALU.subtract, ALU.mult)
                m.then_inc(f["yo"], 1)

            def group(g, p):
                more = not (isinstance(g, int) and g == G - 1)
                for n in range(NE):
                    gates(g, n)
                    if n == 0:
                        if later(g, 1):
                            accumulate(g - 1, NE - 1, 1 - p)
                            out_a(g - 1)
                        else:
                            init(0, 0)
                    else:
                        if n == 1 and later(g, 1):
                            out_b(g - 1, 1 - p)
                            dve.wait_ge(f["yo"], g)
                            init(g, p)
                        accumulate(g, n - 1, p)
                    if n == 2 and more:
                        front(g + 1, 1 - p)
                    if n == 3 and more:
                        router(g + 1, 1 - p)
                    if n == 5 and more:
                        router_weights(g + 1, 1 - p)
            front(0, 0)
            router(0, 0)
            router_weights(0, 0)
            ffn_loop(dve, group)
            accumulate(G - 1, NE - 1, 1)
            out_a(G - 1)
            out_b(G - 1, 1)

        @block.tensor
        def _(pe):
            M = nc.tensor.matmul

            def three(out_, l_hi, l_lo, r_hi, r_lo):
                M(out_, l_hi, r_lo, start=True, stop=False)
                M(out_, l_lo, r_hi, start=False, stop=False)
                return M(out_, l_hi, r_hi, start=False, stop=True)

            def x_T(t, p):
                pe.wait_ge(a["xn"], t + 1)
                if later(t, 4):
                    pe.wait_ge(a["yS"], t - 3)
                elif t:
                    pe.wait_ge(a["xT"], t)
                nc.tensor.transpose(bank[0][:, 0:P], xn[:, p, :], ident[:, :]).then_inc(a["xT_ps"], 1)

            def qkv(t, p):
                pe.wait_ge(a["xT"], t + 1)
                if later(t, 1):
                    pe.wait_ge(a["kn"], t)
                M(bank[1][:, 0:2 * DH], xT[:, p, :], wkv_sb[:, :], start=True, stop=True).then_inc(a["kv"], 1)
                pe.wait_ge(a["xlo"], t + 1)
                if later(t, 1):
                    pe.wait_ge(a["qn"], 2 * t)
                for c in range(2):
                    s = slice(c * HW, (c + 1) * HW)
                    three(bank[2 + c][:, :], xT_hi[:, p, :], xT_lo[:, p, :], wq_hi[:, s], wq_lo[:, s])\
                        .then_inc(a["q"], 1)

            def qk_T(t, p):
                pe.wait_ge(a["kn"], t + 1)
                if later(t, 2):
                    pe.wait_ge(a["oT"], 2 * (t - 1))
                elif t:
                    pe.wait_ge(a["kbd"], t)
                nc.tensor.transpose(bank[7][:, 0:P], kn[:, :, :].rearrange("q s d -> q (s d)"), ident[:, :])\
                  .then_inc(a["knT"], 1)
                for c in range(2):
                    pe.wait_ge(a["qn"], 2 * t + c + 1)
                    if later(t, 2):
                        pe.wait_ge(a["pT"], 2 * (t - 2) + c + 1)
                    for k in range(HBLK):
                        blk = c * HBLK + k
                        m = nc.tensor.transpose(bank[4 + c][:, k * P:(k + 1) * P], qn[:, blk * P:(blk + 1) * P],
                                                ident[:, :])
                    m.then_inc(a["qT_ps"], 1)

            def scores(t, p, c):
                pe.wait_ge(a["kbd"], t + 1)
                pe.wait_ge(a["qT"], 2 * t + c + 1)
                if later(t, 1) or c:
                    pe.wait_ge(a["exp"], 2 * t + c)
                M(bank[6][:, :], ident_b[:, :], causal[:, :, :].rearrange("q h k -> q (h k)"), start=True, stop=False)
                for k in range(HBLK):
                    for s in range(PB):
                        m = M(bank[6][s * SEQ:(s + 1) * SEQ, k * P:(k + 1) * P],
                              QT[:, p, c * HBLK + k, s * SEQ:(s + 1) * SEQ], KBD[:, p, s, 0, :],
                              start=False, stop=(k == HBLK - 1))
                m.then_inc(a["s"], 1)

            def p_T(t, p, c):
                pe.wait_ge(a["norm"], t + 1)
                if isinstance(t, int) and t + 1 >= T:
                    pe.wait_ge(a["qT"], 2 * T)
                else:
                    pe.wait_ge(a["qT"], 2 * (t + 1) + c + 1)
                for k in range(HBLK):
                    blk = c * HBLK + k
                    m = nc.tensor.transpose(bank[4 + c][:, k * P:(k + 1) * P], PR[:, p, blk * P:(blk + 1) * P],
                                            ident[:, :])
                m.then_inc(a["pT_ps"], 1)

            def values(t, p, s):
                pe.wait_ge(a["pT"], 2 * (t + 1))
                pe.wait_ge(a["v"], t + 1)
                if s and isinstance(t, int) and t >= T - 3:
                    pe.wait_ge(a["xT"], T)
                    pe.wait_ge(a["yS"], t)
                elif s:
                    pe.wait_ge(a["xT"], t + 4)
                elif isinstance(t, int) and t == T - 1:
                    pe.wait_ge(a["oT"], 2 * t)
                else:
                    pe.wait_ge(a["kbd"], t + 2)
                M(bank[0 if s else 7][:, :], VBD[:, p, s, 0, :], PT[:, s * HW:(s + 1) * HW], start=True, stop=True)\
                    .then_inc(a["o"], 1)

            def project(t, p):
                pe.wait_ge(a["oT"], 2 * (t + 1))
                for k in range(NBLK):
                    m = M(bank[0][:, 0:D], OT[:, k, :], wout_sb[:, k, :], start=(k == 0), stop=(k == NBLK - 1))
                m.then_inc(a["y"], 1)

            pe.wait_ge(consts, 11)
            pe.wait_ge(w_self, 64)
            pe.wait_ge(split, 2 * SELF_SPLITS)
            pe.wait_ge(zeroed, 1)

            def body(i, p):
                if isinstance(i, int) and i == 0:
                    x_T(0, 0)
                stage_of(qkv, i, p, 0)
                stage_of(qk_T, i, p, 1)
                stage_of(project, i, p, 3)
                stage_of(lambda t, q: scores(t, q, 0), i, p, 1)
                stage_of(lambda t, q: p_T(t, q, 0), i, p, 2)
                stage_of(lambda t, q: p_T(t, q, 1), i, p, 2)
                stage_of(x_T, i, p, -1)
                stage_of(lambda t, q: scores(t, q, 1), i, p, 1)
                stage_of(lambda t, q: values(t, q, 0), i, p, 2)
                stage_of(lambda t, q: values(t, q, 1), i, p, 2)
            pipeline(pe, body, A_FIRST, T + 3)

            pe.wait_ge(a["x1"], T)
            pe.wait_ge(w_cross, 64)
            pe.wait_ge(split, 2 * CROSS_SPLITS)
            pe.wait_ge(b["zero"], 1)

            def bx_T(t, p):
                pe.wait_ge(b["xs"], t + 1)
                if later(t, 1):
                    pe.wait_ge(b["xT"], t)
                nc.tensor.transpose(bank[0][:, 0:P], xs[:, p, :], ident[:, :]).then_inc(b["xT_ps"], 1)

            def b_q(t, p, c):
                pe.wait_ge(b["xT"], t + 1)
                if later(t, 1):
                    pe.wait_ge(b["vbd1" if c else "vbd0"], t)
                for k in range(HBLK):
                    blk = c * HBLK + k
                    m = M(bank[2 + c][:, k * P:(k + 1) * P], xwq_sb[:, blk * P:(blk + 1) * P], xT[:, p, :],
                          start=True, stop=True)
                m.then_inc(b["q"], 1)

            def b_k(t, p, c):
                pe.wait_ge(b["ctx"], 16 * (t + 1))
                pe.wait_ge(b["qT"], 2 * t + c + 1)
                for k in range(HBLK):
                    blk = c * HBLK + k
                    m = M(bank[2 + c][:, k * P:(k + 1) * P], xwk_sb[:, blk * P:(blk + 1) * P], cT[:, p, :],
                          start=True, stop=True)
                m.then_inc(b["k"], 1)

            def b_v(t, p, c):
                pe.wait_ge(b["clo"], t + 1)
                pe.wait_ge(b["kbd"], 2 * t + c + 1)
                s = slice(c * HW, (c + 1) * HW)
                three(bank[2 + c][:, :], cT_hi[:, p, :], cT_lo[:, p, :], xwv_hi[:, s], xwv_lo[:, s])\
                    .then_inc(b["v"], 1)

            def b_s(t, p, c):
                pe.wait_ge(b["qT"], 2 * t + c + 1)
                pe.wait_ge(b["kbd"], 2 * t + c + 1)
                if later(t, 1) or c:
                    pe.wait_ge(b["sub"], 2 * t + c)
                for k in range(HBLK):
                    for s in range(PB):
                        m = M(bank[6][s * SEQ:(s + 1) * SEQ, k * P:(k + 1) * P],
                              QT[:, p, c * HBLK + k, s * SEQ:(s + 1) * SEQ], KBD[:, p, s, c * HBLK + k, :],
                              start=True, stop=True)
                m.then_inc(b["s"], 1)

            def b_oT(t, p):
                pe.wait_ge(b["on"], 2 * (t + 1))
                for c in range(2):
                    pe.wait_ge(b["pT"], 2 * t + c + 1)
                    for k in range(HBLK):
                        blk = c * HBLK + k
                        m = nc.tensor.transpose(bank[4 + c][:, k * P:(k + 1) * P], wide[:, blk * P:(blk + 1) * P],
                                                ident[:, :])
                    m.then_inc(b["oT_ps"], 1)

            def b_pT(t, p):
                pe.wait_ge(b["exp"], 2 * (t + 1))
                for c in range(2):
                    if later(t, 1):
                        pe.wait_ge(b["oT"], 2 * (t - 1) + c + 1)
                    for k in range(HBLK):
                        blk = c * HBLK + k
                        m = nc.tensor.transpose(bank[4 + c][:, k * P:(k + 1) * P], PR[:, p, blk * P:(blk + 1) * P],
                                                ident[:, :])
                    m.then_inc(b["pT_ps"], 1)

            def b_y(t, p):
                pe.wait_ge(b["oT"], 2 * (t + 1))
                if later(t, 1):
                    pe.wait_ge(b["r"], t)
                for k in range(NBLK):
                    m = M(bank[1][:, 0:D], OT[:, k, :], xwo_sb[:, k, :], start=(k == 0), stop=(k == NBLK - 1))
                m.then_inc(b["y"], 1)

            def b_pv(t, p, c):
                pe.wait_ge(b["pT"], 2 * t + c + 1)
                pe.wait_ge(b["vbd1" if c else "vbd0"], t + 1)
                if later(t, 1) or c:
                    pe.wait_ge(b["on"], 2 * t + c)
                for k in range(HBLK):
                    for s in range(PB):
                        blk = c * HBLK + k
                        m = M(bank[7][s * SEQ:(s + 1) * SEQ, k * P:(k + 1) * P],
                              PT[:, blk * P + s * SEQ:blk * P + (s + 1) * SEQ], VBD[:, p, s, blk, :],
                              start=True, stop=True)
                m.then_inc(b["pv"], 1)

            def cross(i, p):
                if isinstance(i, int) and i == 0:
                    bx_T(0, 0)
                stage_of(lambda t, q: b_s(t, q, 0), i, p, 1)
                stage_of(lambda t, q: b_q(t, q, 0), i, p, 0)
                stage_of(b_oT, i, p, 3)
                stage_of(lambda t, q: b_q(t, q, 1), i, p, 0)
                stage_of(lambda t, q: b_s(t, q, 1), i, p, 1)
                stage_of(lambda t, q: b_k(t, q, 0), i, p, 0)
                stage_of(b_y, i, p, 3)
                stage_of(b_pT, i, p, 2)
                stage_of(lambda t, q: b_k(t, q, 1), i, p, 0)
                stage_of(bx_T, i, p, -1)
                stage_of(lambda t, q: b_pv(t, q, 0), i, p, 2)
                stage_of(lambda t, q: b_v(t, q, 0), i, p, 0)
                stage_of(lambda t, q: b_pv(t, q, 1), i, p, 2)
                stage_of(lambda t, q: b_v(t, q, 1), i, p, 0)
            pipeline(pe, cross, B_FIRST, T + 2)

            pe.wait_ge(b["x2"], T)
            pe.wait_ge(w_ffn, 96)
            pe.wait_ge(split, 2 * ALL_SPLITS)

            def front_x(g, p):
                pe.wait_ge(f["xs"], g + 1)
                if later(g, 1):
                    pe.wait_ge(f["ewT"], g)
                for tt in range(GT):
                    m = nc.tensor.transpose(bank[6][:, tt * P:(tt + 1) * P], xg[:, tt, :], ident[:, :])
                m.then_inc(f["xT_ps"], 1)

            def front_scores(g, p):
                pe.wait_ge(f["xT"], g + 1)
                if later(g, 1):
                    pe.wait_ge(f["init"], g)
                for tt in range(GT):
                    m = M(bank[7][:, tt * NE:(tt + 1) * NE], fT[:, p, tt * P:(tt + 1) * P], wr_sb[:, :],
                          start=True, stop=True)
                m.then_inc(f["sc_ps"], 1)

            def front_ew(g, p):
                pe.wait_ge(f["ew"], g + 1)
                for tt in range(GT):
                    m = nc.tensor.transpose(bank[6][0:NE, tt * P:(tt + 1) * P], ew[:, p, tt, :], ident[:, :])
                m.then_inc(f["ewT_ps"], 1)

            def front_bias(g, p):
                pe.wait_ge(f["ewT"], g + 1)
                for tt in range(GT):
                    m = M(bank[7][:, tt * D:(tt + 1) * D], ewT[:, tt * P:(tt + 1) * P], bl2_sb[:, :],
                          start=True, stop=True)
                m.then_inc(f["bias"], 1)

            def layer1(g, n, p):
                for c in range(NH):
                    k = NE * NH * g + NH * n + c
                    for up in range(2):
                        if later(k, NH):
                            pe.wait_ge(f["g"] if up else f["silu"], k - NH + 1)
                        s = slice(up * HID + c * P, up * HID + (c + 1) * P)
                        three(bank[2 * c + up][:, :], wl1_hi[:, n, s], wl1_lo[:, n, s], fT_hi[:, p, :],
                              fT_lo[:, p, :]).then_inc(f["w1"], 1)

            def layer2(g, n):
                k = NE * g + n
                pe.wait_ge(f["g"], NH * (k + 1))
                if later(k, 2):
                    pe.wait_ge(f["acc"], k - 1)
                for tt in range(GT):
                    for c in range(NH):
                        m = M(bank[4 + n % 2][:, tt * D:(tt + 1) * D], gT[:, n % 2, c, tt * P:(tt + 1) * P],
                              wl2_sb[:, n, c, :], start=(c == 0), stop=(c == NH - 1))
                m.then_inc(f["w2"], 1)

            def group(g, p):
                more = not (isinstance(g, int) and g == G - 1)
                for n in range(NE):
                    if n == 0:
                        pe.wait_ge(f["xlo"], g + 1)
                    layer1(g, n, p)
                    if n:
                        layer2(g, n - 1)
                    elif later(g, 1):
                        layer2(g - 1, NE - 1)
                    if more:
                        if n == 1:
                            front_x(g + 1, 1 - p)
                        if n == 2:
                            front_scores(g + 1, 1 - p)
                        if n == 6:
                            front_ew(g + 1, 1 - p)
                        if n == 7:
                            front_bias(g + 1, 1 - p)
            front_x(0, 0)
            front_scores(0, 0)
            front_ew(0, 0)
            front_bias(0, 0)
            ffn_loop(pe, group)
            layer2(G - 1, NE - 1)


def kernel(x, ctx_768, L0_attn_g1, L0_attn_Wq, L0_attn_Wkv, L0_attn_Wout, L0_attn_g2, L0_xattn_Wq, L0_xattn_Wk,
           L0_xattn_Wv, L0_xattn_Wo, L0_xattn_bo, L0_ffn_Wr, L0_ffn_br, L0_ffn_Wl1, L0_ffn_bl1, L0_ffn_Wl2, L0_ffn_bl2,
           L0_ffn_biases_N):
    import numpy as np
    import concourse.bacc as bacc
    from concourse.bass_utils import run_bass_kernel_spmd

    def lay(v, shape=None, order=None):
        v = np.asarray(v)
        if shape is not None:
            v = v.reshape(shape)
        if order is not None:
            v = v.transpose(order)
        return np.ascontiguousarray(v)

    B, S, width = x.shape
    NE, _, H2 = L0_ffn_Wl1.shape
    arrays = {
        "x": lay(x, (B * S, width)),
        "ctxT": lay(ctx_768, (B * S, -1), (1, 0)),
        "g1": lay(L0_attn_g1),
        "wqT": lay(L0_attn_Wq, None, (1, 0)),
        "wkvT": lay(L0_attn_Wkv, None, (1, 0)),
        "woutT": lay(L0_attn_Wout, (width, NBLK, P), (2, 1, 0)),
        "g2": lay(L0_attn_g2),
        "xwq": lay(L0_xattn_Wq),
        "xwk": lay(L0_xattn_Wk),
        "xwv": lay(L0_xattn_Wv),
        "xwo": lay(L0_xattn_Wo, (NBLK, P, width), (1, 0, 2)),
        "bo": lay(L0_xattn_bo),
        "wrT": lay(L0_ffn_Wr, None, (1, 0)),
        "br": lay(L0_ffn_br),
        "wl1": lay(L0_ffn_Wl1, None, (1, 0, 2)),
        "bl1": lay(L0_ffn_bl1, (NE, H2 // P, P), (2, 0, 1)),
        "wl2": lay(L0_ffn_Wl2, (NE, H2 // 2 // P, P, width), (2, 0, 1, 3)),
        "bl2": lay(L0_ffn_bl2),
        "bN": lay(L0_ffn_biases_N),
    }
    nc = bacc.Bacc("TRN2", target_bir_lowering=False, num_devices=1)
    args = [nc.dram_tensor(f"in_{n}", v.shape, F32, kind="ExternalInput").ap() for n, v in arrays.items()]
    out = nc.dram_tensor("out", (B * S, width), F32, kind="ExternalOutput").ap()
    decoder(nc, *args, out)
    r = run_bass_kernel_spmd(nc, [{f"in_{n}": v for n, v in arrays.items()}], core_ids=[0])
    return r.results[0]["out"].reshape(B, S, width)
```

```python
from contextlib import ExitStack

import concourse.bass as bass
from concourse import mybir

F32 = mybir.dt.float32
F32R = mybir.dt.float32r
BF16 = mybir.dt.bfloat16
ALU = mybir.AluOpType
ACT = mybir.ActivationFunctionType
AX = mybir.AxisListType

P = 128
D = 128
SEQ = 64
PB = P // SEQ
HEADS = 16
DH = 64
NBLK = HEADS * DH // P
HBLK = NBLK // 2
EPS = 1e-5
FUTURE = -32768.0


def later(t, n):
    return t >= n if isinstance(t, int) else True


def decoder(nc, x, ctxT, g1, wqT, wkvT, woutT, g2, xwq, xwk, xwvT, xwo, bo, wrT, br, wl1, bl1, wl2, bl2, bN, out):
    TOK = x.shape[0]
    T = TOK // P
    CD = ctxT.shape[0]
    NE = wrT.shape[1]
    HID = wl2.shape[2] * P
    NH = HID // P
    GT = 4
    G = T // GT
    GN = GT * P
    W = NBLK * P
    HW = W // 2
    NVO = HEADS * D // HW
    HVO = HEADS // NVO

    ctx = ExitStack()
    with ctx:
        def sb(name, shape, dt=F32):
            return ctx.enter_context(nc.sbuf_tensor(name, shape, dt))

        def sem(name):
            return ctx.enter_context(nc.semaphore(name))

        bank = [ctx.enter_context(nc.psum_tensor(f"bank{i}", [P, 512], F32)) for i in range(8)]

        ident = sb("ident", [P, P])
        ident_b = sb("ident_b", [P, P], BF16)
        causal = sb("causal", [P, HEADS // 2, SEQ], BF16)
        seen = sb("seen", [P, 2])
        ones = sb("ones", [P, 1])
        mhalf = sb("mhalf", [P, 32])
        euler = sb("euler", [P, 32])
        caps = sb("caps", [P, HEADS + 1])
        g1_sb = sb("g1_sb", [P, 1])
        g2_sb = sb("g2_sb", [P, D])
        bo_sb = sb("bo_sb", [P, D])
        br_sb = sb("br_sb", [P, NE])
        bN_sb = sb("bN_sb", [P, NE])
        stage = sb("stage", [P, 512])
        wq_hi, wq_lo = sb("wq_hi", [P, W], F32R), sb("wq_lo", [P, W], F32R)
        wkv_sb = sb("wkv_sb", [P, 2 * DH])
        wout_sb = sb("wout_sb", [P, NBLK, D])
        xwq_sb = sb("xwq_sb", [P, W])
        xwk_sb = sb("xwk_sb", [CD, W])
        room = sb("room", [P, 2 * NH * GN])
        xwvT_sb = room[:, 0:NBLK * CD].rearrange("p (a c) -> p a c", a=NBLK)
        xwo_sb = room[:, NH * GN:NH * GN + NBLK * D].rearrange("p (a d) -> p a d", a=NBLK)
        gT = room[:, :].rearrange("p (b a t) -> p b a t", b=2, a=NH)
        vo_hi, vo_lo = sb("vo_hi", [CD, NVO, HW], F32R), sb("vo_lo", [CD, NVO, HW], F32R)
        wr_sb = sb("wr_sb", [P, NE])
        wl1_hi, wl1_lo = sb("wl1_hi", [P, NE, 2 * HID], F32R), sb("wl1_lo", [P, NE, 2 * HID], F32R)
        wl2_sb = sb("wl2_sb", [P, NE, NH, D])
        bl1_sb = sb("bl1_sb", [P, NE, 2 * NH])
        bl2_sb = sb("bl2_sb", [NE, D])

        X = sb("X", [P, T, D])

        st = sb("st", [P, 6])
        mv = sb("mv", [P, 2, 2])
        ve = sb("ve", [P, 2, 1])
        rs = sb("rs", [P, 2, 1])
        xn = sb("xn", [P, 2, D])
        xs = sb("xs", [P, 2, D])
        yS = sb("yS", [P, D])
        yg = sb("yg", [P, D])
        vS = sb("vS", [P, 2, DH])
        xT = sb("xT", [P, 2, P])
        xT_hi, xT_lo = sb("xT_hi", [P, 2, P], F32R), sb("xT_lo", [P, 2, P], F32R)
        wide = sb("wide", [P, W + DH])
        ssq = sb("ssq", [P, HEADS + 1])
        rq = sb("rq", [P, HEADS + 1])
        rinv = sb("rinv", [P, HEADS + 1])
        qn = sb("qn", [P, W])
        kn = sb("kn", [P, PB, DH])
        QT = sb("QT", [P, 2, NBLK, P])
        KBD = sb("KBD", [P, 2, PB, NBLK, P])
        VBD = sb("VBD", [P, 2, PB, NBLK, P])
        PR = sb("PR", [P, 2, W])
        PT = sb("PT", [P, W])
        OT = sb("OT", [P, NBLK, P])
        L = sb("L", [P, HEADS])
        rL = sb("rL", [P, 2, HEADS])
        mx = sb("mx", [P, HEADS])
        st2 = sb("st2", [P, 6])
        mv2 = sb("mv2", [P, 2])
        ve2 = sb("ve2", [P, 1])
        rs2 = sb("rs2", [P, 1])
        r1 = sb("r1", [P, D])
        r2 = sb("r2", [P, D])
        st3 = sb("st3", [P, 6])
        mv3 = sb("mv3", [P, 2])
        ve3 = sb("ve3", [P, 1])
        rs3 = sb("rs3", [P, 1])
        cT = sb("cT", [CD, 2, P])
        cT_hi, cT_lo = sb("cT_hi", [CD, 2, P], F32R), sb("cT_lo", [CD, 2, P], F32R)

        xg = sb("xg", [P, GT, D])
        iota8 = sb("iota8", [P, NE])
        topi = sb("topi", [P, GT, 8], mybir.dt.uint32)
        topf = sb("topf", [P, GT, 8])
        sel1 = sb("sel1", [P, GT, NE])
        fT = sb("fT", [P, 2, GN])
        fT_hi, fT_lo = sb("fT_hi", [P, 2, GN], F32R), sb("fT_lo", [P, 2, GN], F32R)
        sg = sb("sg", [P, 2, GN])
        sc = sb("sc", [P, GT, NE])
        scb = sb("scb", [P, GT, NE])
        top = sb("top", [P, GT, 8])
        sel = sb("sel", [P, GT, NE])
        smax = sb("smax", [P, GT])
        sh = sb("sh", [P, GT, NE])
        ex = sb("ex", [P, GT, NE])
        exs = sb("exs", [P, GT, NE])
        es = sb("es", [P, GT])
        er = sb("er", [P, GT])
        ew = sb("ew", [P, 2, GT, NE])
        ewT = sb("ewT", [NE, GN])
        yacc = sb("yacc", [P, GT, D])
        fst = sb("fst", [P, GT, 6])
        fmv = sb("fmv", [P, GT, 2])
        fve = sb("fve", [P, GT])
        frs = sb("frs", [P, GT])
        yo = wide[:, 0:2 * GT * D].rearrange("p (b a d) -> p b a d", b=2, a=GT)

        block = ctx.enter_context(nc.Block())

        x_first, x_rest = sem("x_first"), sem("x_rest")
        w_self, w_vo, w_cross, w_ffn = sem("w_self"), sem("w_vo"), sem("w_cross"), sem("w_ffn")
        staged, split, consts = sem("staged"), sem("split"), sem("consts")
        zeroed = sem("zeroed")

        slices = []
        for c in range(2):
            slices.append((wqT[:, c * HW:(c + 1) * HW], P, wq_hi[:, c * HW:(c + 1) * HW], wq_lo[:, c * HW:(c + 1) * HW]))
        for n in range(NE):
            slices.append((wl1[:, n, :], P, wl1_hi[:, n, :], wl1_lo[:, n, :]))
        SELF_SPLITS, ALL_SPLITS = 2, len(slices)

        def staging(n):
            return PT[:, n * HW:(n + 1) * HW] if n < SELF_SPLITS else stage[0:slices[n][1], :]

        a = {n: sem("a_" + n) for n in (
            "stats", "aggr", "var", "rstd", "xn", "xT_ps", "xT", "xhi", "xlo", "kv", "q", "sq", "vS", "v", "ssq", "pow",
            "cap", "qn", "kn", "knT", "kbd", "qT_ps", "qT", "s", "exp", "sum", "rl", "norm", "pT_ps", "pT",
            "o", "oT", "y", "yS", "y1", "y2", "y3", "yrstd", "yn", "yr", "z1", "z2", "z3", "zrstd", "x1")}
        b = {n: sem("b_" + n) for n in (
            "ctx", "chi", "clo", "xs", "xT_ps", "xT", "q", "qT", "k", "kbd", "u", "u_act", "u_dve", "vo_even", "vo", "vo_hi", "vo_lo", "norm", "s", "max", "sub", "exp",
            "zero", "sum", "rl", "pT_ps", "pT", "y", "r", "rb", "z1", "z2", "z3", "zrstd", "x2")}
        f = {n: sem("f_" + n) for n in (
            "xs", "xT_ps", "xT", "xhi", "xlo", "sc_ps", "sc", "scb", "top", "topi", "topf", "sel1", "sel", "smax",
            "sh", "ex", "exs", "es", "er", "ew", "ewT_ps", "ewT", "bias", "init", "w1", "silu", "g", "w2", "acc",
            "st", "mv", "ve", "rstd", "yo", "out")}

        def pipeline(eng, body, first, last):
            for i in range(first):
                body(i, i % 2)
            with eng.Fori(first // 2, T // 2 - 1) as j:
                body(2 * j, 0)
                body(2 * j + 1, 1)
            for i in range(T - 2, last + 1):
                body(i, i % 2)

        A_FIRST, B_FIRST = 6, 4

        def ffn_loop(eng, group):
            group(0, 0)
            group(1, 1)
            with eng.Fori(1, G // 2 - 1) as j:
                group(2 * j, 0)
                group(2 * j + 1, 1)
            group(G - 2, 0)
            group(G - 1, 1)

        def dve_wait(sem_, value):
            nc.vector.wait_ge(sem_, value)
            nc.vector.tensor_copy(seen[:, 1:2], seen[:, 0:1])

        def pool_copy(dst, src):
            one = ones[:, :]
            if len(src.shape) == 3:
                one = one.unsqueeze(2)
            return nc.gpsimd.tensor_tensor(dst, src, one.broadcast_to(list(src.shape)), ALU.mult)

        U_BANK = (7, 2, 3, 4)

        def b_u(copy, eng, t, p, c):
            eng.wait_ge(b["u"], NVO * t + c + 1)
            if later(t, 2):
                eng.wait_ge(b["y"], t - 1)
            blocks = HVO // 2
            for s in range(PB):
                for h in range(2):
                    u = copy(VBD[h * SEQ:(h + 1) * SEQ, p, s, c * blocks:(c + 1) * blocks, :],
                             bank[U_BANK[c]][s * SEQ:(s + 1) * SEQ, :]
                             .rearrange("k (a h d) -> k a h d", a=blocks, h=2)[:, :, h, :])
            u.then_inc(b["u_dve" if c % 2 else "u_act"], 1)

        def stage_of(fn, i, p, back):
            t = i - back
            if isinstance(t, int) and not 0 <= t < T:
                return
            fn(t, (p - back) % 2)

        @block.sync
        def _(sp):
            x_v = x.rearrange("(t p) d -> p t d", p=P)
            sp.dma_start(X[:, 0:4, :], x_v[:, 0:4, :]).then_inc(x_first, 16)
            small = ((g1_sb[:, :], g1.rearrange("(p a) -> p a", a=1)), (wkv_sb[:, :], wkvT))
            for dst, src in small:
                sp.dma_start(dst, src).then_inc(w_self, 16)
            for n, (src, rows, _, _) in enumerate(slices):
                if n >= SELF_SPLITS:
                    sp.wait_ge(split, 2 * n)
                sp.dma_start(staging(n), src).then_inc(staged, 16)
                if n == 0:
                    sp.dma_start(wout_sb[:, :, :], woutT).then_inc(w_self, 16)
                    sp.dma_start(g2_sb[:, :], g2.partition_broadcast(P)).then_inc(w_self, 16)
                if n == 1:
                    sp.dma_start(X[:, 4:T, :], x_v[:, 4:T, :]).then_inc(x_rest, 16)

        @block.gpsimd
        def _(pool):
            def ln_in(t, p):
                pool.wait_ge(a["var"], t + 1)
                nc.gpsimd.tensor_tensor(rs[:, p, :], ve[:, p, :], mhalf[:, 0:1], ALU.pow).then_inc(a["rstd"], 1)

            nc.gpsimd.memset(ident[:, :], 1.0).then_inc(consts, 1)
            nc.gpsimd.memset(ones[:, :], 1.0)
            nc.gpsimd.memset(ident_b[:, :], 1.0)
            nc.gpsimd.memset(causal[:, :, :], 0.0).then_inc(consts, 1)
            nc.gpsimd.memset(mhalf[:, :], -0.5).then_inc(consts, 1)
            nc.gpsimd.memset(euler[:, :], 2.718281828459045).then_inc(consts, 1)
            nc.gpsimd.memset(caps[:, 0:HEADS], 16.0e12).then_inc(consts, 1)
            nc.gpsimd.memset(caps[:, HEADS:HEADS + 1], 1.0e12).then_inc(consts, 1)
            pool.wait_ge(consts, 6)
            nc.gpsimd.affine_select(out=ident[:, :], in_=ident[:, :], compare_op=ALU.is_equal, fill=0.0, base=0,
                                    pattern=[[-1, P]], channel_multiplier=1).then_inc(consts, 1)
            pool.wait_ge(consts, 7)
            nc.gpsimd.iota(iota8[:, :], pattern=[[1, NE]], base=0, channel_multiplier=0,
                           allow_small_or_imprecise_dtypes=True).then_inc(consts, 1)
            for h in range(PB):
                pool.wait_ge(consts, 8 + h)
                c = causal[h * SEQ:(h + 1) * SEQ, :, :]
                nc.gpsimd.affine_select(out=c, in_=c, compare_op=ALU.is_ge, fill=FUTURE, base=0,
                                        pattern=[[0, HEADS // 2], [-1, SEQ]], channel_multiplier=1)\
                  .then_inc(consts, 1)
            pool.wait_ge(consts, 8 + PB)
            nc.gpsimd.affine_select(out=ident_b[:, :], in_=ident_b[:, :], compare_op=ALU.is_equal, fill=0.0, base=0,
                                    pattern=[[-1, P]], channel_multiplier=1).then_inc(consts, 1)
            pool.wait_ge(consts, 11)
            ln_in(0, 0)
            nc.gpsimd.dma_start(xwq_sb[:, :], xwq).then_inc(w_cross, 16)
            nc.gpsimd.dma_start(xwk_sb[:, :], xwk).then_inc(w_cross, 16)
            nc.gpsimd.dma_start(bo_sb[:, :], bo.partition_broadcast(P)).then_inc(w_cross, 16)
            nc.gpsimd.dma_start(wr_sb[:, :], wrT).then_inc(w_ffn, 16)
            nc.gpsimd.dma_start(br_sb[:, :], br.partition_broadcast(P)).then_inc(w_ffn, 16)
            nc.gpsimd.dma_start(bN_sb[:, :], bN.partition_broadcast(P)).then_inc(w_ffn, 16)
            nc.gpsimd.dma_start(wl2_sb[:, :, :, :], wl2).then_inc(w_ffn, 16)
            nc.gpsimd.dma_start(bl1_sb[:, :, :], bl1).then_inc(w_ffn, 16)
            nc.gpsimd.dma_start(bl2_sb[:, :], bl2).then_inc(w_ffn, 16)

            def norms(t, p):
                pool.wait_ge(a["ssq"], t + 1)
                if later(t, 1):
                    pool.wait_ge(a["cap"], t)
                nc.gpsimd.tensor_tensor(rq[:, :], ssq[:, :], mhalf[:, 0:HEADS + 1], ALU.pow).then_inc(a["pow"], 1)

            def weights(t, p):
                pool.wait_ge(a["rl"], t + 1)
                v = PR[:, p, :].rearrange("q (h k) -> q h k", k=SEQ)
                nc.gpsimd.tensor_tensor(v, v, rL[:, p, :].unsqueeze(2).broadcast_to([P, HEADS, SEQ]), ALU.mult)\
                  .then_inc(a["norm"], 1)

            def y_rstd(t, p):
                pool.wait_ge(a["y3"], t + 1)
                nc.gpsimd.tensor_tensor(rs2[:, :], ve2[:, :], mhalf[:, 0:1], ALU.pow).then_inc(a["yrstd"], 1)

            def z_rstd(t, p):
                pool.wait_ge(a["z3"], t + 1)
                nc.gpsimd.tensor_tensor(rs3[:, :], ve3[:, :], mhalf[:, 0:1], ALU.pow).then_inc(a["zrstd"], 1)

            def body(i, p):
                stage_of(ln_in, i, p, -1)
                stage_of(y_rstd, i, p, 4)
                stage_of(norms, i, p, 0)
                stage_of(z_rstd, i, p, 4)
                stage_of(weights, i, p, 1)
            pipeline(pool, body, A_FIRST, T + 1)

            def fetch(t, p):
                pool.wait_ge(a["x1"], t + 1)
                if later(t, 2):
                    pool.wait_ge(b["xT_ps"], t - 1)
                pool_copy(xs[:, p, :], X[:, bass.ds(t, 1), :].rearrange("q a d -> q (a d)"))\
                  .then_inc(b["xs"], 1)

            def b_weights(t, p):
                pool.wait_ge(b["rl"], t + 1)
                v = PR[:, p, :].rearrange("q (h k) -> q h k", k=SEQ)
                nc.gpsimd.tensor_tensor(v, v, rL[:, p, :].unsqueeze(2).broadcast_to([P, HEADS, SEQ]), ALU.mult)\
                  .then_inc(b["norm"], 1)

            def cross_tail(t, p):
                pool.wait_ge(b["z3"], t + 1)
                nc.gpsimd.tensor_tensor(rs3[:, :], ve3[:, :], mhalf[:, 0:1], ALU.pow).then_inc(b["zrstd"], 1)

            def cross(i, p):
                if isinstance(i, int) and i == 0:
                    fetch(0, 0)
                    body(T + 2, 0)
                stage_of(fetch, i, p, -1)
                stage_of(cross_tail, i, p, 3)
                stage_of(b_weights, i, p, 1)
                if isinstance(i, int) and i == 1:
                    body(T + 3, 1)
            pipeline(pool, cross, B_FIRST, T - 1)

            def group_front(g, p):
                pool.wait_ge(b["x2"], GT * (g + 1))
                if later(g, 1):
                    pool.wait_ge(f["xT_ps"], g)
                pool_copy(xg[:, :, :], X[:, bass.ds(g * GT, GT), :]).then_inc(f["xs"], 1)

            def router_exp(g, p):
                pool.wait_ge(f["sh"], g + 1)
                nc.gpsimd.tensor_tensor(ex[:, :, :].rearrange("p a b -> p (a b)"), euler[:, 0:GT * NE],
                                        sh[:, :, :].rearrange("p a b -> p (a b)"), ALU.pow).then_inc(f["ex"], 1)

            def group_tail(g, p):
                pool.wait_ge(f["ve"], g + 1)
                nc.gpsimd.tensor_tensor(frs[:, :], fve[:, :], mhalf[:, 0:GT], ALU.pow).then_inc(f["rstd"], 1)

            def group(g, p):
                if later(g, 1):
                    group_tail(g - 1, 1 - p)
                if not (isinstance(g, int) and g == G - 1):
                    group_front(g + 1, 1 - p)
                    router_exp(g + 1, 1 - p)
            group_front(0, 0)
            cross(T, 0)
            cross(T + 1, 1)
            router_exp(0, 0)
            cross(T + 2, 0)
            ffn_loop(pool, group)
            group_tail(G - 1, 1)

        @block.scalar
        def _(act):
            def x_T(t, p):
                act.wait_ge(a["xT_ps"], t + 1)
                if later(t, 2):
                    act.wait_ge(a["q"], 2 * (t - 1))
                    act.wait_ge(a["xlo"], t - 1)
                nc.scalar.activation(xT[:, p, :], bank[0][:, 0:P], ACT.Copy, scale=g1_sb[:, 0:1]).then_inc(a["xT"], 1)
                act.wait_ge(a["xT"], t + 1)
                nc.scalar.activation(xT_hi[:, p, :], xT[:, p, :], ACT.Copy).then_inc(a["xhi"], 1)

            def vo_round(c):
                act.wait_ge(b["vo"], c + 1)
                nc.scalar.activation(vo_hi[:, c, :], bank[4 + c][0:CD, :], ACT.Copy).then_inc(b["vo_hi"], 1)

            def squares(t, p):
                act.wait_ge(a["kv"], t + 1)
                if later(t, 1):
                    act.wait_ge(a["ssq"], t)
                nc.scalar.activation(wide[:, W:W + DH], bank[1][:, 0:DH], ACT.Square).then_inc(a["sq"], 1)
                if later(t, 2):
                    act.wait_ge(a["v"], t - 1)
                nc.scalar.activation(vS[:, p, :], bank[1][:, DH:2 * DH], ACT.Copy).then_inc(a["vS"], 1)
                for c in range(2):
                    act.wait_ge(a["q"], 2 * t + c + 1)
                    nc.scalar.activation(wide[:, c * HW:(c + 1) * HW], bank[2 + c][:, :], ACT.Square)\
                      .then_inc(a["sq"], 1)

            def q_T(t, p):
                act.wait_ge(a["knT"], t + 1)
                if later(t, 2):
                    act.wait_ge(a["s"], 2 * (t - 1))
                for h in range(2):
                    r = slice(h * DH, (h + 1) * DH)
                    k = nc.scalar.activation(KBD[r, p, :, 0, r], bank[7][r, 0:P].rearrange("d (s k) -> d s k", s=PB),
                                             ACT.Copy)
                k.then_inc(a["kbd"], 1)
                for c in range(2):
                    act.wait_ge(a["qT_ps"], 2 * t + c + 1)
                    nc.scalar.activation(QT[:, p, c * HBLK:(c + 1) * HBLK, :].rearrange("d a q -> d (a q)"),
                                         bank[4 + c][:, :], ACT.Copy).then_inc(a["qT"], 1)

            def exp_half(t, p, c):
                if later(t, 2):
                    act.wait_ge(a["pT_ps"], 2 * (t - 1))
                act.wait_ge(a["s"], 2 * t + c + 1)
                nc.scalar.activation(PR[:, p, c * HW:(c + 1) * HW], bank[6][:, :], ACT.Exp, scale=16.0)\
                  .then_inc(a["exp"], 1)

            def p_T(t, p, c):
                if later(t, 1):
                    act.wait_ge(a["o"], 2 * t)
                v = PT[:, :].rearrange("k (s a q) -> k s a q", s=PB, a=NBLK)
                act.wait_ge(a["pT_ps"], 2 * t + c + 1)
                nc.scalar.activation(v[:, :, c * HBLK:(c + 1) * HBLK, :],
                                     bank[4 + c][:, :].rearrange("k (a s q) -> k s a q", a=HBLK, s=PB),
                                     ACT.Copy).then_inc(a["pT"], 1)

            def o_T(t, p, s):
                if later(t, 1):
                    act.wait_ge(a["y"], t)
                act.wait_ge(a["o"], 2 * t + s + 1)
                nc.scalar.activation(OT[:, :, s * SEQ:(s + 1) * SEQ],
                                     bank[0 if s else 7][:, :].rearrange("d (a q) -> d a q", a=NBLK), ACT.Copy)\
                  .then_inc(a["oT"], 1)

            def y_evac(t, p):
                act.wait_ge(a["y"], t + 1)
                if later(t, 1):
                    act.wait_ge(a["yn"], t)
                nc.scalar.activation(yS[:, :], bank[0][:, 0:D], ACT.Copy).then_inc(a["yS"], 1)

            act.dma_start(xwvT_sb[:, :, :], xwvT).then_inc(w_vo, 16)
            act.dma_start(xwo_sb[:, :, :], xwo).then_inc(w_vo, 16)
            act.dma_start(cT[:, 0, :], ctxT[:, 0:P]).then_inc(b["ctx"], 16)
            act.wait_ge(w_self, 64)
            act.wait_ge(zeroed, 1)

            def body(i, p):
                if isinstance(i, int) and i == 0:
                    x_T(0, 0)
                stage_of(squares, i, p, 0)
                stage_of(q_T, i, p, 1)
                stage_of(y_evac, i, p, 3)
                stage_of(lambda t, q: exp_half(t, q, 0), i, p, 1)
                stage_of(lambda t, q: p_T(t, q, 0), i, p, 2)
                stage_of(lambda t, q: p_T(t, q, 1), i, p, 2)
                stage_of(x_T, i, p, -1)
                stage_of(lambda t, q: exp_half(t, q, 1), i, p, 1)
                stage_of(lambda t, q: o_T(t, q, 0), i, p, 2)
                stage_of(lambda t, q: o_T(t, q, 1), i, p, 2)
                if isinstance(i, int) and i == 0:
                    for c in range(NVO):
                        vo_round(c)
            pipeline(act, body, A_FIRST, T + 2)

            act.wait_ge(a["xlo"], T)
            act.wait_ge(b["zero"], 1)

            def bx_T(t, p):
                act.wait_ge(b["xT_ps"], t + 1)
                if later(t, 2):
                    act.wait_ge(b["q"], 2 * (t - 1))
                nc.scalar.activation(xT[:, p, :], bank[0][:, 0:P], ACT.Copy).then_inc(b["xT"], 1)

            def c_hi(t, p):
                act.wait_ge(b["ctx"], 16 * (t + 1))
                if later(t, 2):
                    act.wait_ge(b["u"], NVO * (t - 1))
                nc.scalar.activation(cT_hi[:, p, :], cT[:, p, :], ACT.Copy).then_inc(b["chi"], 1)

            def load_ctx(t, p):
                if later(t, 1):
                    act.wait_ge(b["ctx"], 16 * t)
                if later(t, 2):
                    act.wait_ge(b["k"], 2 * (t - 1))
                    act.wait_ge(b["chi"], t - 1)
                    act.wait_ge(b["clo"], t - 1)
                act.dma_start(cT[:, p, :], ctxT[:, bass.ds(t * P, P)]).then_inc(b["ctx"], 16)

            def b_q(t, p, c):
                if later(t, 2):
                    act.wait_ge(b["s"], 2 * (t - 1))
                act.wait_ge(b["q"], 2 * t + c + 1)
                nc.scalar.activation(QT[:, p, c * HBLK:(c + 1) * HBLK, :].rearrange("d a q -> d (a q)"),
                                     bank[2 + c][:, :], ACT.Copy).then_inc(b["qT"], 1)

            def b_k(t, p, c):
                act.wait_ge(b["k"], 2 * t + c + 1)
                for h in range(2):
                    r = slice(h * DH, (h + 1) * DH)
                    k = nc.scalar.activation(KBD[r, p, :, c * HBLK:(c + 1) * HBLK, r],
                                             bank[2 + c][r, :].rearrange("d (a s k) -> d s a k", a=HBLK, s=PB),
                                             ACT.Copy)
                k.then_inc(b["kbd"], 1)

            def b_exp(t, p, c):
                act.wait_ge(b["sub"], 2 * t + c + 1)
                v = PR[:, p, c * HW:(c + 1) * HW]
                nc.scalar.activation(v, v, ACT.Exp, scale=DH ** -0.5).then_inc(b["exp"], 1)

            def b_pT(t, p):
                if later(t, 1):
                    act.wait_ge(b["y"], t)
                for c in range(2):
                    act.wait_ge(b["pT_ps"], 2 * t + c + 1)
                    nc.scalar.activation(PT[:, c * HW:(c + 1) * HW], bank[4 + c][:, :], ACT.Copy)\
                      .then_inc(b["pT"], 1)

            def cross(i, p):
                if isinstance(i, int) and i == 0:
                    load_ctx(1, 1)
                    c_hi(0, 0)
                    bx_T(0, 0)
                stage_of(lambda t, q: b_q(t, q, 0), i, p, 0)
                stage_of(lambda t, q: b_exp(t, q, 0), i, p, 1)
                stage_of(lambda t, q: b_q(t, q, 1), i, p, 0)
                stage_of(b_pT, i, p, 2)
                stage_of(lambda t, q: b_exp(t, q, 1), i, p, 1)
                stage_of(lambda t, q: b_k(t, q, 0), i, p, 0)
                stage_of(lambda t, q: b_k(t, q, 1), i, p, 0)
                stage_of(bx_T, i, p, -1)
                stage_of(c_hi, i, p, -1)
                stage_of(load_ctx, i, p, -2)
                stage_of(lambda t, q: b_u(nc.scalar.copy, act, t, q, 0), i, p, 0)
                stage_of(lambda t, q: b_u(nc.scalar.copy, act, t, q, 2), i, p, 0)
            pipeline(act, cross, B_FIRST, T - 1)


            def front_x(g, p, bk=6):
                act.wait_ge(f["xT_ps"], g + 1)
                if later(g, 2):
                    act.wait_ge(f["sc_ps"], g - 1)
                    act.wait_ge(f["xlo"], g - 1)
                nc.scalar.activation(fT[:, p, :], bank[bk][:, :], ACT.Copy).then_inc(f["xT"], 1)
                act.wait_ge(f["xT"], g + 1)
                if later(g, 2):
                    act.wait_ge(f["w1"], 2 * NH * NE * (g - 1))
                nc.scalar.activation(fT_hi[:, p, :], fT[:, p, :], ACT.Copy).then_inc(f["xhi"], 1)

            def front_ew(g, p):
                act.wait_ge(f["ewT_ps"], g + 1)
                if later(g, 1):
                    act.wait_ge(f["bias"], g)
                nc.scalar.activation(ewT[:, :], bank[6][0:NE, :], ACT.Copy).then_inc(f["ewT"], 1)

            out_v = out.rearrange("(t p) d -> p t d", p=P)

            def store(g, p):
                act.wait_ge(f["yo"], g + 1)
                if later(g, 1):
                    act.wait_ge(f["out"], 16 * g)
                act.dma_start(out_v[:, bass.ds(g * GT, GT), :], yo[:, p, :, :]).then_inc(f["out"], 16)

            def silus(g, n):
                for c in range(NH):
                    k = NE * NH * g + NH * n + c
                    act.wait_ge(f["w1"], 2 * k + 1)
                    if later(k, NH):
                        act.wait_ge(f["g"], k - NH + 1)
                    nc.scalar.activation(sg[:, c, :], bank[2 * c][:, :], ACT.Silu, bias=bl1_sb[:, n, c:c + 1])\
                      .then_inc(f["silu"], 1)

            def group(g, p):
                more = not (isinstance(g, int) and g == G - 1)
                for n in range(NE):
                    silus(g, n)
                    if n == 0 and isinstance(g, int) and g == 0:
                        b_pT(T - 1, 1)
                    if n == 1 and isinstance(g, int) and g == 0:
                        front_ew(0, 0)
                    if n == 1 and more:
                        front_x(g + 1, 1 - p)
                    if n == 6 and more:
                        front_ew(g + 1, 1 - p)
                    if n == 4 and later(g, 1):
                        store(g - 1, 1 - p)
            b_exp(T - 1, 1, 0)
            front_x(0, 0, 7)
            b_pT(T - 2, 0)
            b_exp(T - 1, 1, 1)
            act.wait_ge(w_ffn, 96)
            ffn_loop(act, group)
            store(G - 1, 1)
            act.wait_ge(f["out"], 16 * G)

        @block.vector
        def _(dve):
            V = nc.vector

            V.memset(seen[:, :], 0.0)
            V.memset(KBD[:, :, :, 0, :], 0.0)
            V.memset(VBD[:, :, :, 0, :], 0.0).then_inc(zeroed, 1)
            V.memset(KBD[:, :, :, 1:NBLK, :], 0.0).then_inc(b["zero"], 1)

            def split_slice(n):
                _, rows, hi, lo = slices[n]
                dve.wait_ge(staged, 16 * max(n + 1, SELF_SPLITS))
                V.tensor_copy(hi, staging(n)).then_inc(split, 1)
                dve.wait_ge(split, 2 * n + 1)
                V.tensor_tensor(lo, staging(n), hi.bitcast(F32), ALU.subtract).then_inc(split, 1)

            def vo_split(c):
                dve.wait_ge(b["vo_hi"], c + 1)
                V.tensor_tensor(vo_lo[:, c, :], bank[4 + c][0:CD, :], vo_hi[:, c, :].bitcast(F32), ALU.subtract)\
                 .then_inc(b["vo_lo"], 1)

            def ln_a(t, p):
                V.bn_stats(st[:, :], X[:, bass.ds(t, 1), :].rearrange("q a d -> q (a d)")).then_inc(a["stats"], 1)
                dve_wait(a["stats"], t + 1)
                V.bn_aggr(mv[:, p, :], st[:, :]).then_inc(a["aggr"], 1)
                dve.wait_ge(a["aggr"], t + 1)
                V.tensor_scalar(ve[:, p, :], mv[:, p, 1:2], EPS, None, ALU.add).then_inc(a["var"], 1)

            def ln_b(t, p):
                dve.wait_ge(a["rstd"], t + 1)
                if later(t, 2):
                    dve.wait_ge(a["xT_ps"], t - 1)
                V.tensor_scalar(xn[:, p, :], X[:, bass.ds(t, 1), :].rearrange("q a d -> q (a d)"), mv[:, p, 0:1],
                                rs[:, p, :], ALU.subtract, ALU.mult).then_inc(a["xn"], 1)

            def x_lo(t, p):
                dve.wait_ge(a["xhi"], t + 1)
                V.tensor_tensor(xT_lo[:, p, :], xT[:, p, :], xT_hi[:, p, :].bitcast(F32), ALU.subtract)\
                  .then_inc(a["xlo"], 1)

            def sums(t, p):
                dve.wait_ge(a["sq"], 3 * (t + 1))
                if later(t, 1):
                    dve.wait_ge(a["pow"], t)
                V.tensor_reduce(ssq[:, :], wide[:, :].rearrange("q (h d) -> q h d", d=DH), AX.X, ALU.add)\
                 .then_inc(a["ssq"], 1)

            def normalise(t, p):
                dve.wait_ge(a["pow"], t + 1)
                if later(t, 1):
                    dve.wait_ge(a["kn"], t)
                V.tensor_tensor(rinv[:, :], rq[:, :], caps[:, :], ALU.min).then_inc(a["cap"], 1)
                dve.wait_ge(a["cap"], t + 1)
                dve.wait_ge(a["vS"], t + 1)
                if later(t, 1):
                    dve.wait_ge(a["knT"], t)
                V.tensor_scalar(kn[:, :, :], bank[1][:, 0:DH].unsqueeze(1).broadcast_to([P, PB, DH]),
                                rinv[:, HEADS:HEADS + 1], None, ALU.mult).then_inc(a["kn"], 1)
                for c in range(2):
                    if later(t, 1):
                        dve.wait_ge(a["qT_ps"], 2 * t)
                    hs = slice(c * HEADS // 2, (c + 1) * HEADS // 2)
                    V.tensor_tensor(qn[:, c * HW:(c + 1) * HW].rearrange("q (h d) -> q h d", d=DH),
                                    bank[2 + c][:, :].rearrange("q (h d) -> q h d", d=DH),
                                    rinv[:, hs].unsqueeze(2).broadcast_to([P, HEADS // 2, DH]), ALU.mult)\
                     .then_inc(a["qn"], 1)

            def v_bd(t, p):
                dve.wait_ge(a["vS"], t + 1)
                if later(t, 2):
                    dve.wait_ge(a["o"], 2 * (t - 1))
                for s in range(PB):
                    for h in range(2):
                        v = V.tensor_copy(VBD[h * DH:(h + 1) * DH, p, s, 0, h * DH:(h + 1) * DH],
                                          vS[s * SEQ:(s + 1) * SEQ, p, :])
                v.then_inc(a["v"], 1)

            def softmax(t, p):
                dve.wait_ge(a["exp"], 2 * (t + 1))
                v = PR[:, p, :].rearrange("q (h k) -> q h k", k=SEQ)
                V.tensor_reduce(L[:, :], v, AX.X, ALU.add).then_inc(a["sum"], 1)
                dve.wait_ge(a["sum"], t + 1)
                V.reciprocal(rL[:, p, :], L[:, :]).then_inc(a["rl"], 1)

            def tail_a(t, p):
                dve.wait_ge(a["yS"], t + 1)
                V.bn_stats(st2[:, :], yS[:, :]).then_inc(a["y1"], 1)
                dve_wait(a["y1"], t + 1)
                V.bn_aggr(mv2[:, :], st2[:, :]).then_inc(a["y2"], 1)
                dve.wait_ge(a["y2"], t + 1)
                V.tensor_scalar(ve2[:, :], mv2[:, 1:2], EPS, None, ALU.add).then_inc(a["y3"], 1)
                V.scalar_tensor_tensor(out=yg[:, :], in0=yS[:, :], scalar=mv2[:, 0:1], in1=g2_sb[:, :],
                                       op0=ALU.subtract, op1=ALU.mult).then_inc(a["yn"], 1)

            def tail_b(t, p):
                dve.wait_ge(a["yrstd"], t + 1)
                if later(t, 1):
                    dve.wait_ge(a["x1"], t)
                dve.wait_ge(a["yn"], t + 1)
                V.scalar_tensor_tensor(out=r1[:, :], in0=yg[:, :], scalar=rs2[:, :],
                                       in1=X[:, bass.ds(t, 1), :].rearrange("q a d -> q (a d)"),
                                       op0=ALU.mult, op1=ALU.add).then_inc(a["yr"], 1)
                dve.wait_ge(a["yr"], t + 1)
                V.bn_stats(st3[:, :], r1[:, :]).then_inc(a["z1"], 1)
                dve_wait(a["z1"], t + 1)
                V.bn_aggr(mv3[:, :], st3[:, :]).then_inc(a["z2"], 1)
                dve.wait_ge(a["z2"], t + 1)
                V.tensor_scalar(ve3[:, :], mv3[:, 1:2], EPS, None, ALU.add).then_inc(a["z3"], 1)

            def tail_c(t, p):
                dve.wait_ge(a["zrstd"], t + 1)
                V.tensor_scalar(X[:, bass.ds(t, 1), :].rearrange("q a d -> q (a d)"), r1[:, :], mv3[:, 0:1],
                                rs3[:, :], ALU.subtract, ALU.mult).then_inc(a["x1"], 1)

            dve.wait_ge(x_first, 16)
            ln_a(0, 0)
            for n in range(SELF_SPLITS):
                split_slice(n)
            dve.wait_ge(consts, 11)
            dve.wait_ge(w_self, 64)

            def body(i, p):
                if isinstance(i, int) and i == 0:
                    ln_b(0, 0)
                    x_lo(0, 0)
                if isinstance(i, int) and i == 3:
                    dve.wait_ge(x_rest, 16)
                stage_of(ln_a, i, p, -1)
                stage_of(sums, i, p, 0)
                stage_of(tail_b, i, p, 4)
                stage_of(ln_b, i, p, -1)
                if isinstance(i, int) and 0 < i < 5:
                    split_slice(2 * i)
                stage_of(tail_a, i, p, 3)
                stage_of(v_bd, i, p, 1)
                stage_of(normalise, i, p, 0)
                stage_of(x_lo, i, p, -1)
                stage_of(softmax, i, p, 1)
                stage_of(tail_c, i, p, 4)
                if isinstance(i, int) and i == 0:
                    for c in range(NVO):
                        vo_split(c)
                elif isinstance(i, int) and i < 5:
                    split_slice(2 * i + 1)
            pipeline(dve, body, A_FIRST, T + 2)


            def c_lo(t, p):
                dve.wait_ge(b["chi"], t + 1)
                if later(t, 2):
                    dve.wait_ge(b["u"], NVO * (t - 1))
                V.tensor_tensor(cT_lo[:, p, :], cT[:, p, :], cT_hi[:, p, :].bitcast(F32), ALU.subtract)\
                 .then_inc(b["clo"], 1)

            def b_max(t, p, c):
                dve.wait_ge(b["s"], 2 * t + c + 1)
                v = bank[6][:, :].rearrange("q (h k) -> q h k", k=SEQ)
                V.tensor_reduce(mx[:, 0:HEADS // 2], v, AX.X, ALU.max).then_inc(b["max"], 1)
                dve.wait_ge(b["max"], 2 * t + c + 1)
                if later(t, 2):
                    dve.wait_ge(b["pT_ps"], 2 * (t - 1))
                V.tensor_tensor(PR[:, p, c * HW:(c + 1) * HW].rearrange("q (h k) -> q h k", k=SEQ), v,
                                mx[:, 0:HEADS // 2].unsqueeze(2).broadcast_to([P, HEADS // 2, SEQ]), ALU.subtract)\
                 .then_inc(b["sub"], 1)

            def b_sum(t, p):
                dve.wait_ge(b["exp"], 2 * (t + 1))
                V.tensor_reduce(L[:, :], PR[:, p, :].rearrange("q (h k) -> q h k", k=SEQ), AX.X, ALU.add)\
                 .then_inc(b["sum"], 1)
                dve.wait_ge(b["sum"], t + 1)
                V.reciprocal(rL[:, p, :], L[:, :]).then_inc(b["rl"], 1)

            def b_tail_a(t, p, bk=1):
                dve.wait_ge(b["y"], t + 1)
                V.tensor_tensor(r1[:, :], bank[bk][:, 0:D], X[:, bass.ds(t, 1), :].rearrange("q a d -> q (a d)"),
                                ALU.add).then_inc(b["r"], 1)
                dve.wait_ge(b["r"], t + 1)
                V.tensor_tensor(r2[:, :], r1[:, :], bo_sb[:, :], ALU.add).then_inc(b["rb"], 1)
                dve.wait_ge(b["rb"], t + 1)
                V.bn_stats(st3[:, :], r2[:, :]).then_inc(b["z1"], 1)
                dve_wait(b["z1"], t + 1)
                V.bn_aggr(mv3[:, :], st3[:, :]).then_inc(b["z2"], 1)
                dve.wait_ge(b["z2"], t + 1)
                V.tensor_scalar(ve3[:, :], mv3[:, 1:2], EPS, None, ALU.add).then_inc(b["z3"], 1)

            def b_tail_b(t, p):
                dve.wait_ge(b["zrstd"], t + 1)
                V.tensor_scalar(X[:, bass.ds(t, 1), :].rearrange("q a d -> q (a d)"), r2[:, :], mv3[:, 0:1],
                                rs3[:, :], ALU.subtract, ALU.mult).then_inc(b["x2"], 1)

            dve.wait_ge(w_cross, 48)

            def cross(i, p):
                if isinstance(i, int) and i == 0:
                    c_lo(0, 0)
                if isinstance(i, int) and i == 1:
                    dve.wait_ge(a["pT_ps"], 2 * T)
                    dve.wait_ge(a["norm"], T)
                stage_of(lambda t, q: b_max(t, q, 0), i, p, 1)
                stage_of(b_tail_a, i, p, 3)
                stage_of(lambda t, q: b_max(t, q, 1), i, p, 1)
                stage_of(b_tail_b, i, p, 3)
                stage_of(b_sum, i, p, 1)
                stage_of(c_lo, i, p, -1)
                stage_of(lambda t, q: b_u(V.tensor_copy, dve, t, q, 1), i, p, 0)
                stage_of(lambda t, q: b_u(V.tensor_copy, dve, t, q, 3), i, p, 0)
                if isinstance(i, int) and i == 1:
                    body(T + 3, 1)
            pipeline(dve, cross, B_FIRST, T - 1)


            def front(g, p):
                dve.wait_ge(f["xhi"], g + 1)
                if later(g, 2):
                    dve.wait_ge(f["w1"], 2 * NH * NE * (g - 1))
                V.tensor_tensor(fT_lo[:, p, :], fT[:, p, :], fT_hi[:, p, :].bitcast(F32), ALU.subtract)\
                 .then_inc(f["xlo"], 1)

            def router(g, p, bk=7):
                shape = [P, GT, NE]
                dve.wait_ge(f["sc_ps"], g + 1)
                V.tensor_tensor(sc[:, :, :], bank[bk][:, 0:GT * NE].rearrange("p (a b) -> p a b", a=GT),
                                br_sb[:, :].unsqueeze(1).broadcast_to(shape), ALU.add).then_inc(f["sc"], 1)
                dve.wait_ge(f["sc"], g + 1)
                V.tensor_tensor(scb[:, :, :], sc[:, :, :], bN_sb[:, :].unsqueeze(1).broadcast_to(shape), ALU.add)\
                 .then_inc(f["scb"], 1)
                V.tensor_reduce(smax[:, :], sc[:, :, :], AX.X, ALU.max).then_inc(f["smax"], 1)
                dve.wait_ge(f["smax"], g + 1)
                V.tensor_tensor(sh[:, :, :], sc[:, :, :], smax[:, :].unsqueeze(2).broadcast_to(shape), ALU.subtract)\
                 .then_inc(f["sh"], 1)
                dve_wait(f["scb"], g + 1)
                for k in range(GT):
                    V.max(top[:, k, :], scb[:, k, :]).then_inc(f["top"], 1)
                dve_wait(f["top"], GT * (g + 1))
                for k in range(GT):
                    m = V.max_index(topi[:, k, :], top[:, k, :], scb[:, k, :])
                m.then_inc(f["topi"], 1)
                dve.wait_ge(f["topi"], g + 1)
                V.tensor_copy(topf[:, :, :], topi[:, :, :]).then_inc(f["topf"], 1)
                dve.wait_ge(f["topf"], g + 1)
                io = iota8[:, :].unsqueeze(1).broadcast_to(shape)
                V.tensor_tensor(sel[:, :, :], io, topf[:, :, 0:1].broadcast_to(shape), ALU.is_equal)
                V.tensor_tensor(sel1[:, :, :], io, topf[:, :, 1:2].broadcast_to(shape), ALU.is_equal)\
                 .then_inc(f["sel1"], 1)
                dve.wait_ge(f["sel1"], g + 1)
                V.tensor_tensor(sel[:, :, :], sel[:, :, :], sel1[:, :, :], ALU.add).then_inc(f["sel"], 1)

            def router_weights(g, p):
                shape = [P, GT, NE]
                dve.wait_ge(f["sel"], g + 1)
                dve.wait_ge(f["ex"], g + 1)
                V.tensor_tensor(exs[:, :, :], ex[:, :, :], sel[:, :, :], ALU.mult).then_inc(f["exs"], 1)
                dve.wait_ge(f["exs"], g + 1)
                V.tensor_reduce(es[:, :], exs[:, :, :], AX.X, ALU.add).then_inc(f["es"], 1)
                dve.wait_ge(f["es"], g + 1)
                V.reciprocal(er[:, :], es[:, :]).then_inc(f["er"], 1)
                dve.wait_ge(f["er"], g + 1)
                V.tensor_tensor(ew[:, p, :, :], exs[:, :, :], er[:, :].unsqueeze(2).broadcast_to(shape), ALU.mult)\
                 .then_inc(f["ew"], 1)

            def gates(g, n):
                q = n % 2
                for c in range(NH):
                    k = NE * NH * g + NH * n + c
                    dve.wait_ge(f["silu"], k + 1)
                    dve.wait_ge(f["w1"], 2 * k + 2)
                    if c == 0 and later(NE * g + n, 2):
                        dve.wait_ge(f["w2"], NE * g + n - 1)
                    V.scalar_tensor_tensor(out=gT[:, q, c, :], in0=bank[2 * c + 1][:, :],
                                           scalar=bl1_sb[:, n, NH + c:NH + c + 1], in1=sg[:, c, :],
                                           op0=ALU.add, op1=ALU.mult).then_inc(f["g"], 1)

            def accumulate(g, n, p):
                k = NE * g + n
                dve.wait_ge(f["w2"], k + 1)
                dve.wait_ge(f["init"], g + 1)
                if later(k, 1):
                    dve.wait_ge(f["acc"], k)
                for tt in range(GT):
                    m = V.scalar_tensor_tensor(out=yacc[:, tt, :], in0=bank[4 + n % 2][:, tt * D:(tt + 1) * D],
                                               scalar=ew[:, p, tt, n:n + 1], in1=yacc[:, tt, :],
                                               op0=ALU.mult, op1=ALU.add)
                m.then_inc(f["acc"], 1)

            def init(g, p):
                dve.wait_ge(f["bias"], g + 1)
                V.tensor_tensor(yacc[:, :, :], bank[7][:, :].rearrange("p (a d) -> p a d", a=GT),
                                X[:, bass.ds(g * GT, GT), :], ALU.add).then_inc(f["init"], 1)

            def out_a(g):
                dve.wait_ge(f["acc"], NE * (g + 1))
                for tt in range(GT):
                    m = V.bn_stats(fst[:, tt, :], yacc[:, tt, :])
                m.then_inc(f["st"], 1)
                dve_wait(f["st"], g + 1)
                for tt in range(GT):
                    m = V.bn_aggr(fmv[:, tt, :], fst[:, tt, :])
                m.then_inc(f["mv"], 1)
                dve.wait_ge(f["mv"], g + 1)
                V.tensor_scalar(fve[:, :], fmv[:, :, 1], EPS, None, ALU.add).then_inc(f["ve"], 1)

            def out_b(g, p):
                dve.wait_ge(f["rstd"], g + 1)
                if later(g, 2):
                    dve.wait_ge(f["out"], 16 * (g - 1))
                for tt in range(GT):
                    m = V.tensor_scalar(yo[:, p, tt, :], yacc[:, tt, :], fmv[:, tt, 0:1], frs[:, tt:tt + 1],
                                        ALU.subtract, ALU.mult)
                m.then_inc(f["yo"], 1)

            def group(g, p):
                more = not (isinstance(g, int) and g == G - 1)
                for n in range(NE):
                    gates(g, n)
                    if n == 0:
                        if later(g, 1):
                            accumulate(g - 1, NE - 1, 1 - p)
                            out_a(g - 1)
                        elif not later(g, 1):
                            b_tail_a(T - 1, 1, 7)
                    else:
                        if n == 1 and isinstance(g, int) and g == 0:
                            router_weights(0, 0)
                            b_tail_b(T - 1, 1)
                            init(0, 0)
                        if n == 1 and later(g, 1):
                            out_b(g - 1, 1 - p)
                            dve.wait_ge(f["yo"], g)
                            init(g, p)
                        accumulate(g, n - 1, p)
                    if n == 2 and more:
                        front(g + 1, 1 - p)
                    if n == 3 and more:
                        router(g + 1, 1 - p)
                    if n == 5 and more:
                        router_weights(g + 1, 1 - p)
            b_max(T - 1, 1, 0)
            b_tail_a(T - 3, 1)
            b_max(T - 1, 1, 1)
            b_tail_b(T - 3, 1)
            front(0, 0)
            b_sum(T - 1, 1)
            dve.wait_ge(w_ffn, 96)
            router(0, 0, 6)
            cross(T + 1, 1)
            ffn_loop(dve, group)
            accumulate(G - 1, NE - 1, 1)
            out_a(G - 1)
            out_b(G - 1, 1)

        @block.tensor
        def _(pe):
            M = nc.tensor.matmul

            def three(out_, l_hi, l_lo, r_hi, r_lo):
                M(out_, l_hi, r_lo, start=True, stop=False)
                M(out_, l_lo, r_hi, start=False, stop=False)
                return M(out_, l_hi, r_hi, start=False, stop=True)

            def x_T(t, p):
                pe.wait_ge(a["xn"], t + 1)
                if later(t, 4):
                    pe.wait_ge(a["yS"], t - 3)
                elif t:
                    pe.wait_ge(a["xT"], t)
                nc.tensor.transpose(bank[0][:, 0:P], xn[:, p, :], ident[:, :]).then_inc(a["xT_ps"], 1)

            def qkv(t, p):
                pe.wait_ge(a["xT"], t + 1)
                if later(t, 1):
                    pe.wait_ge(a["kn"], t)
                M(bank[1][:, 0:2 * DH], xT[:, p, :], wkv_sb[:, :], start=True, stop=True).then_inc(a["kv"], 1)
                pe.wait_ge(a["xlo"], t + 1)
                if later(t, 1):
                    pe.wait_ge(a["qn"], 2 * t)
                for c in range(2):
                    s = slice(c * HW, (c + 1) * HW)
                    three(bank[2 + c][:, :], xT_hi[:, p, :], xT_lo[:, p, :], wq_hi[:, s], wq_lo[:, s])\
                        .then_inc(a["q"], 1)

            def qk_T(t, p):
                pe.wait_ge(a["kn"], t + 1)
                if later(t, 2):
                    pe.wait_ge(a["oT"], 2 * (t - 1))
                elif t:
                    pe.wait_ge(a["kbd"], t)
                nc.tensor.transpose(bank[7][:, 0:P], kn[:, :, :].rearrange("q s d -> q (s d)"), ident[:, :])\
                  .then_inc(a["knT"], 1)
                for c in range(2):
                    pe.wait_ge(a["qn"], 2 * t + c + 1)
                    if later(t, 2):
                        pe.wait_ge(a["pT"], 2 * (t - 2) + c + 1)
                    for k in range(HBLK):
                        blk = c * HBLK + k
                        m = nc.tensor.transpose(bank[4 + c][:, k * P:(k + 1) * P], qn[:, blk * P:(blk + 1) * P],
                                                ident[:, :])
                    m.then_inc(a["qT_ps"], 1)

            def scores(t, p, c):
                pe.wait_ge(a["kbd"], t + 1)
                pe.wait_ge(a["qT"], 2 * t + c + 1)
                if later(t, 1) or c:
                    pe.wait_ge(a["exp"], 2 * t + c)
                M(bank[6][:, :], ident_b[:, :], causal[:, :, :].rearrange("q h k -> q (h k)"), start=True, stop=False)
                for k in range(HBLK):
                    for s in range(PB):
                        m = M(bank[6][s * SEQ:(s + 1) * SEQ, k * P:(k + 1) * P],
                              QT[:, p, c * HBLK + k, s * SEQ:(s + 1) * SEQ], KBD[:, p, s, 0, :],
                              start=False, stop=(k == HBLK - 1))
                m.then_inc(a["s"], 1)

            def p_T(t, p, c):
                pe.wait_ge(a["norm"], t + 1)
                if isinstance(t, int) and t + 1 >= T:
                    pe.wait_ge(a["qT"], 2 * T)
                else:
                    pe.wait_ge(a["qT"], 2 * (t + 1) + c + 1)
                for k in range(HBLK):
                    blk = c * HBLK + k
                    m = nc.tensor.transpose(bank[4 + c][:, k * P:(k + 1) * P], PR[:, p, blk * P:(blk + 1) * P],
                                            ident[:, :])
                m.then_inc(a["pT_ps"], 1)

            def values(t, p, s):
                pe.wait_ge(a["pT"], 2 * (t + 1))
                pe.wait_ge(a["v"], t + 1)
                if s and isinstance(t, int) and t >= T - 3:
                    pe.wait_ge(a["xT"], T)
                    pe.wait_ge(a["yS"], t)
                elif s:
                    pe.wait_ge(a["xT"], t + 4)
                elif isinstance(t, int) and t == T - 1:
                    pe.wait_ge(a["oT"], 2 * t)
                else:
                    pe.wait_ge(a["kbd"], t + 2)
                M(bank[0 if s else 7][:, :], VBD[:, p, s, 0, :], PT[:, s * HW:(s + 1) * HW], start=True, stop=True)\
                    .then_inc(a["o"], 1)

            def project(t, p):
                pe.wait_ge(a["oT"], 2 * (t + 1))
                for k in range(NBLK):
                    m = M(bank[0][:, 0:D], OT[:, k, :], wout_sb[:, k, :], start=(k == 0), stop=(k == NBLK - 1))
                m.then_inc(a["y"], 1)

            pe.wait_ge(consts, 11)
            pe.wait_ge(w_self, 64)
            pe.wait_ge(split, 2 * SELF_SPLITS)
            pe.wait_ge(zeroed, 1)

            def vo_product():
                pe.wait_ge(w_vo, 32)
                for odd in range(2):
                    if odd:
                        pe.wait_ge(b["vo_even"], NVO)
                    r = slice(odd * DH, (odd + 1) * DH)
                    for c in range(NVO):
                        for k in range(odd, HVO, 2):
                            blk = (HVO * c + k) // 2
                            m = M(bank[4 + c][0:CD, k * D:(k + 1) * D], xwvT_sb[r, blk, :], xwo_sb[r, blk, :],
                                  start=True, stop=True)
                        m.then_inc(b["vo" if odd else "vo_even"], 1)

            def body(i, p):
                if isinstance(i, int) and i == 0:
                    x_T(0, 0)
                stage_of(qkv, i, p, 0)
                if isinstance(i, int) and i == 0:
                    vo_product()
                if isinstance(i, int) and i == 1:
                    pe.wait_ge(b["vo_lo"], NVO)
                stage_of(qk_T, i, p, 1)
                stage_of(project, i, p, 3)
                stage_of(lambda t, q: scores(t, q, 0), i, p, 1)
                stage_of(lambda t, q: p_T(t, q, 0), i, p, 2)
                stage_of(lambda t, q: p_T(t, q, 1), i, p, 2)
                stage_of(x_T, i, p, -1)
                stage_of(lambda t, q: scores(t, q, 1), i, p, 1)
                stage_of(lambda t, q: values(t, q, 0), i, p, 2)
                stage_of(lambda t, q: values(t, q, 1), i, p, 2)
            pipeline(pe, body, A_FIRST, T + 2)

            pe.wait_ge(a["yS"], T)
            pe.wait_ge(a["exp"], 2 * T)
            pe.wait_ge(w_cross, 48)
            pe.wait_ge(b["zero"], 1)

            def bx_T(t, p):
                pe.wait_ge(b["xs"], t + 1)
                if later(t, 1):
                    pe.wait_ge(b["xT"], t)
                nc.tensor.transpose(bank[0][:, 0:P], xs[:, p, :], ident[:, :]).then_inc(b["xT_ps"], 1)

            def b_q(t, p, c):
                pe.wait_ge(b["xT"], t + 1)
                if later(t, 1):
                    pe.wait_ge(b["u_act"] if c else b["u_dve"], 2 * t if c else 2 * t - 1)
                for k in range(HBLK):
                    blk = c * HBLK + k
                    m = M(bank[2 + c][:, k * P:(k + 1) * P], xwq_sb[:, blk * P:(blk + 1) * P], xT[:, p, :],
                          start=True, stop=True)
                m.then_inc(b["q"], 1)

            def b_k(t, p, c):
                pe.wait_ge(b["ctx"], 16 * (t + 1))
                pe.wait_ge(b["qT"], 2 * t + c + 1)
                for k in range(HBLK):
                    blk = c * HBLK + k
                    m = M(bank[2 + c][:, k * P:(k + 1) * P], xwk_sb[:, blk * P:(blk + 1) * P], cT[:, p, :],
                          start=True, stop=True)
                m.then_inc(b["k"], 1)

            def b_uv(t, p, c):
                pe.wait_ge(b["clo"], t + 1)
                if c in (1, 2):
                    pe.wait_ge(b["kbd"], 2 * t + c)
                elif c == 3:
                    if later(t, 2):
                        pe.wait_ge(b["pT"], 2 * (t - 1))
                    elif t:
                        pe.wait_ge(b["u_dve"], 2 * t)
                elif later(t, 1):
                    pe.wait_ge(b["u_act"], 2 * t - 1)
                three(bank[U_BANK[c]][:, :], cT_hi[:, p, :], cT_lo[:, p, :], vo_hi[:, c, :], vo_lo[:, c, :])\
                    .then_inc(b["u"], 1)

            def b_s(t, p, c):
                pe.wait_ge(b["qT"], 2 * t + c + 1)
                pe.wait_ge(b["kbd"], 2 * t + c + 1)
                if later(t, 1) or c:
                    pe.wait_ge(b["sub"], 2 * t + c)
                for k in range(HBLK):
                    for s in range(PB):
                        m = M(bank[6][s * SEQ:(s + 1) * SEQ, k * P:(k + 1) * P],
                              QT[:, p, c * HBLK + k, s * SEQ:(s + 1) * SEQ], KBD[:, p, s, c * HBLK + k, :],
                              start=True, stop=True)
                m.then_inc(b["s"], 1)

            def b_pT(t, p):
                pe.wait_ge(b["norm"], t + 1)
                for c in range(2):
                    if c and later(t, 1):
                        pe.wait_ge(b["pT"], 2 * t)
                    elif isinstance(t, int) and t == T - 1:
                        pe.wait_ge(b["pT"], 2 * t)
                    elif not c:
                        pe.wait_ge(b["u_dve"], 2 * (t + 2))
                    for k in range(HBLK):
                        blk = c * HBLK + k
                        m = nc.tensor.transpose(bank[4 + c][:, k * P:(k + 1) * P], PR[:, p, blk * P:(blk + 1) * P],
                                                ident[:, :])
                    m.then_inc(b["pT_ps"], 1)

            def b_y(t, p, bk=1):
                pe.wait_ge(b["pT"], 2 * (t + 1))
                pe.wait_ge(b["u_act"], 2 * (t + 1))
                pe.wait_ge(b["u_dve"], 2 * (t + 1))
                if later(t, 1):
                    pe.wait_ge(b["r"], t)
                for s in range(PB):
                    for k in range(NBLK):
                        m = M(bank[bk][s * SEQ:(s + 1) * SEQ, 0:D], PT[:, k * P + s * SEQ:k * P + (s + 1) * SEQ],
                              VBD[:, p, s, k, :], start=(k == 0), stop=(k == NBLK - 1))
                m.then_inc(b["y"], 1)

            def cross(i, p):
                if isinstance(i, int) and i == 0:
                    bx_T(0, 0)
                stage_of(lambda t, q: b_s(t, q, 0), i, p, 1)
                stage_of(lambda t, q: b_q(t, q, 0), i, p, 0)
                stage_of(lambda t, q: b_q(t, q, 1), i, p, 0)
                stage_of(b_pT, i, p, 2)
                stage_of(lambda t, q: b_s(t, q, 1), i, p, 1)
                stage_of(lambda t, q: b_k(t, q, 0), i, p, 0)
                stage_of(lambda t, q: b_k(t, q, 1), i, p, 0)
                stage_of(b_y, i, p, 2)
                stage_of(bx_T, i, p, -1)
                for c in range(NVO):
                    stage_of(lambda t, q: b_uv(t, q, c), i, p, 0)
            pipeline(pe, cross, B_FIRST, T - 1)


            def front_x(g, p, bk=6):
                pe.wait_ge(f["xs"], g + 1)
                if later(g, 1):
                    pe.wait_ge(f["ewT"], g)
                for tt in range(GT):
                    m = nc.tensor.transpose(bank[bk][:, tt * P:(tt + 1) * P], xg[:, tt, :], ident[:, :])
                m.then_inc(f["xT_ps"], 1)

            def front_scores(g, p, bk=7):
                pe.wait_ge(f["xT"], g + 1)
                if later(g, 1):
                    pe.wait_ge(f["init"], g)
                for tt in range(GT):
                    m = M(bank[bk][:, tt * NE:(tt + 1) * NE], fT[:, p, tt * P:(tt + 1) * P], wr_sb[:, :],
                          start=True, stop=True)
                m.then_inc(f["sc_ps"], 1)

            def front_ew(g, p):
                pe.wait_ge(f["ew"], g + 1)
                for tt in range(GT):
                    m = nc.tensor.transpose(bank[6][0:NE, tt * P:(tt + 1) * P], ew[:, p, tt, :], ident[:, :])
                m.then_inc(f["ewT_ps"], 1)

            def front_bias(g, p):
                pe.wait_ge(f["ewT"], g + 1)
                if isinstance(g, int) and g == 0:
                    pe.wait_ge(b["r"], T)
                for tt in range(GT):
                    m = M(bank[7][:, tt * D:(tt + 1) * D], ewT[:, tt * P:(tt + 1) * P], bl2_sb[:, :],
                          start=True, stop=True)
                m.then_inc(f["bias"], 1)

            def layer1(g, n, p):
                for c in range(NH):
                    k = NE * NH * g + NH * n + c
                    for up in range(2):
                        if later(k, NH):
                            pe.wait_ge(f["g"] if up else f["silu"], k - NH + 1)
                        s = slice(up * HID + c * P, up * HID + (c + 1) * P)
                        three(bank[2 * c + up][:, :], wl1_hi[:, n, s], wl1_lo[:, n, s], fT_hi[:, p, :],
                              fT_lo[:, p, :]).then_inc(f["w1"], 1)

            def layer2(g, n):
                k = NE * g + n
                pe.wait_ge(f["g"], NH * (k + 1))
                if later(k, 2):
                    pe.wait_ge(f["acc"], k - 1)
                elif k == 0:
                    pe.wait_ge(b["pT"], 2 * T)
                for tt in range(GT):
                    for c in range(NH):
                        m = M(bank[4 + n % 2][:, tt * D:(tt + 1) * D], gT[:, n % 2, c, tt * P:(tt + 1) * P],
                              wl2_sb[:, n, c, :], start=(c == 0), stop=(c == NH - 1))
                m.then_inc(f["w2"], 1)

            def group(g, p):
                more = not (isinstance(g, int) and g == G - 1)
                for n in range(NE):
                    if n == 0:
                        pe.wait_ge(f["xlo"], g + 1)
                    layer1(g, n, p)
                    if n == 0 and isinstance(g, int) and g == 0:
                        b_pT(T - 1, 1)
                        b_y(T - 1, 1, 7)
                    if n == 1 and isinstance(g, int) and g == 0:
                        front_ew(0, 0)
                        front_bias(0, 0)
                    if n:
                        layer2(g, n - 1)
                    elif later(g, 1):
                        layer2(g - 1, NE - 1)
                    if more:
                        if n == 1:
                            front_x(g + 1, 1 - p)
                        if n == 2:
                            front_scores(g + 1, 1 - p)
                        if n == 6:
                            front_ew(g + 1, 1 - p)
                        if n == 7:
                            front_bias(g + 1, 1 - p)
            b_s(T - 1, 1, 0)
            pe.wait_ge(b["u_act"], 2 * T)
            front_x(0, 0, 7)
            b_pT(T - 2, 0)
            b_s(T - 1, 1, 1)
            b_y(T - 2, 0)
            pe.wait_ge(w_ffn, 96)
            pe.wait_ge(b["sub"], 2 * T)
            front_scores(0, 0, 6)
            pe.wait_ge(split, 2 * ALL_SPLITS)
            pe.wait_ge(b["u_dve"], 2 * T)
            pe.wait_ge(b["xT"], T)
            pe.wait_ge(b["r"], T - 1)
            ffn_loop(pe, group)
            layer2(G - 1, NE - 1)


def kernel(x, ctx_768, L0_attn_g1, L0_attn_Wq, L0_attn_Wkv, L0_attn_Wout, L0_attn_g2, L0_xattn_Wq, L0_xattn_Wk,
           L0_xattn_Wv, L0_xattn_Wo, L0_xattn_bo, L0_ffn_Wr, L0_ffn_br, L0_ffn_Wl1, L0_ffn_bl1, L0_ffn_Wl2, L0_ffn_bl2,
           L0_ffn_biases_N):
    import numpy as np
    import concourse.bacc as bacc
    from concourse.bass_utils import run_bass_kernel_spmd

    def lay(v, shape=None, order=None):
        v = np.asarray(v)
        if shape is not None:
            v = v.reshape(shape)
        if order is not None:
            v = v.transpose(order)
        return np.ascontiguousarray(v)

    B, S, width = x.shape
    NE, _, H2 = L0_ffn_Wl1.shape
    arrays = {
        "x": lay(x, (B * S, width)),
        "ctxT": lay(ctx_768, (B * S, -1), (1, 0)),
        "g1": lay(L0_attn_g1),
        "wqT": lay(L0_attn_Wq, None, (1, 0)),
        "wkvT": lay(L0_attn_Wkv, None, (1, 0)),
        "woutT": lay(L0_attn_Wout, (width, NBLK, P), (2, 1, 0)),
        "g2": lay(L0_attn_g2),
        "xwq": lay(L0_xattn_Wq),
        "xwk": lay(L0_xattn_Wk),
        "xwvT": lay(L0_xattn_Wv, (-1, NBLK, P), (2, 1, 0)),
        "xwo": lay(L0_xattn_Wo, (NBLK, P, width), (1, 0, 2)),
        "bo": lay(L0_xattn_bo),
        "wrT": lay(L0_ffn_Wr, None, (1, 0)),
        "br": lay(L0_ffn_br),
        "wl1": lay(L0_ffn_Wl1, None, (1, 0, 2)),
        "bl1": lay(L0_ffn_bl1, (NE, H2 // P, P), (2, 0, 1)),
        "wl2": lay(L0_ffn_Wl2, (NE, H2 // 2 // P, P, width), (2, 0, 1, 3)),
        "bl2": lay(L0_ffn_bl2),
        "bN": lay(L0_ffn_biases_N),
    }
    nc = bacc.Bacc("TRN2", target_bir_lowering=False, num_devices=1)
    args = [nc.dram_tensor(f"in_{n}", v.shape, F32, kind="ExternalInput").ap() for n, v in arrays.items()]
    out = nc.dram_tensor("out", (B * S, width), F32, kind="ExternalOutput").ap()
    decoder(nc, *args, out)
    r = run_bass_kernel_spmd(nc, [{f"in_{n}": v for n, v in arrays.items()}], core_ids=[0])
    return r.results[0]["out"].reshape(B, S, width)
```

```python
from contextlib import ExitStack

import concourse.bass as bass
from concourse import mybir

F32 = mybir.dt.float32
F32R = mybir.dt.float32r
BF16 = mybir.dt.bfloat16
ALU = mybir.AluOpType
ACT = mybir.ActivationFunctionType
AX = mybir.AxisListType

P = 128
D = 128
SEQ = 64
PB = P // SEQ
HEADS = 16
DH = 64
NBLK = HEADS * DH // P
HBLK = NBLK // 2
EPS = 1e-5
FUTURE = -32768.0


def later(t, n):
    return t >= n if isinstance(t, int) else True


def decoder(nc, x, ctxT, g1, wqT, wkvT, woutT, g2, xwq, xwk, xwvT, xwo, bo, wrT, br, wl1, bl1, wl2, bl2, bN, out):
    TOK = x.shape[0]
    T = TOK // P
    CD = ctxT.shape[0]
    NE = wrT.shape[1]
    HID = wl2.shape[2] * P
    NH = HID // P
    GT = 4
    G = T // GT
    GN = GT * P
    W = NBLK * P
    HW = W // 2
    NVO = HEADS * D // HW
    HVO = HEADS // NVO

    ctx = ExitStack()
    with ctx:
        def sb(name, shape, dt=F32):
            return ctx.enter_context(nc.sbuf_tensor(name, shape, dt))

        def sem(name):
            return ctx.enter_context(nc.semaphore(name))

        bank = [ctx.enter_context(nc.psum_tensor(f"bank{i}", [P, 512], F32)) for i in range(8)]

        ident = sb("ident", [P, P])
        ident_b = sb("ident_b", [P, P], BF16)
        causal = sb("causal", [P, HEADS // 2, SEQ], BF16)
        seen = sb("seen", [P, 2])
        ones = sb("ones", [P, 1])
        mhalf = sb("mhalf", [P, 32])
        euler = sb("euler", [P, 32])
        caps = sb("caps", [P, HEADS + 1])
        g1_sb = sb("g1_sb", [P, 1])
        g2_sb = sb("g2_sb", [P, D])
        bo_sb = sb("bo_sb", [P, D])
        br_sb = sb("br_sb", [P, NE])
        bN_sb = sb("bN_sb", [P, NE])
        stage = sb("stage", [P, 512])
        wq_hi, wq_lo = sb("wq_hi", [P, W], F32R), sb("wq_lo", [P, W], F32R)
        wkv_sb = sb("wkv_sb", [P, 2 * DH])
        wout_sb = sb("wout_sb", [P, NBLK, D])
        xwq_hi, xwk_hi = sb("xwq_hi", [P, W], F32R), sb("xwk_hi", [CD, W], F32R)
        fT = sb("fT", [P, 2, GN])
        fT_hi, fT_lo = sb("fT_hi", [P, 2, GN], F32R), sb("fT_lo", [P, 2, GN], F32R)
        xwvT_sb = fT[:, :, :].rearrange("p a t -> p (a t)")[:, 0:NBLK * CD].rearrange("p (a c) -> p a c", a=NBLK)
        xwq_lo = fT_hi[:, :, :].rearrange("p a t -> p (a t)")
        xwk_lo = fT_lo[0:CD, :, :].rearrange("p a t -> p (a t)")
        sg = sb("sg", [P, 2, GN])
        xwo_sb = sg[:, :, :].rearrange("p a t -> p (a t)").rearrange("p (a d) -> p a d", a=NBLK)
        vo_hi, vo_lo = sb("vo_hi", [CD, NVO, HW], F32R), sb("vo_lo", [CD, NVO, HW], F32R)
        wr_sb = sb("wr_sb", [P, NE])
        wl1_hi, wl1_lo = sb("wl1_hi", [P, NE, 2 * HID], F32R), sb("wl1_lo", [P, NE, 2 * HID], F32R)
        wl2_sb = sb("wl2_sb", [P, NE, NH, D])
        bl1_sb = sb("bl1_sb", [P, NE, 2 * NH])
        bl2_sb = sb("bl2_sb", [NE, D])

        X = sb("X", [P, T, D])

        st = sb("st", [P, 6])
        mv = sb("mv", [P, 2, 2])
        ve = sb("ve", [P, 2, 1])
        rs = sb("rs", [P, 2, 1])
        xn = sb("xn", [P, 2, D])
        xs = sb("xs", [P, 2, D])
        yS = sb("yS", [P, D])
        yg = sb("yg", [P, D])
        vS = sb("vS", [P, 2, DH])
        xT = sb("xT", [P, 2, P])
        xT_hi, xT_lo = sb("xT_hi", [P, 2, P], F32R), sb("xT_lo", [P, 2, P], F32R)
        wide = sb("wide", [P, W + DH])
        ssq = sb("ssq", [P, HEADS + 1])
        rq = sb("rq", [P, HEADS + 1])
        rinv = sb("rinv", [P, HEADS + 1])
        qn = sb("qn", [P, W])
        kn = sb("kn", [P, PB, DH])
        QT = sb("QT", [P, 2, NBLK, P])
        KBD = sb("KBD", [P, 2, PB, NBLK, P])
        VBD = sb("VBD", [P, 2, PB, NBLK, P])
        PR = sb("PR", [P, 2, W])
        PT = sb("PT", [P, W])
        OT = sb("OT", [P, NBLK, P])
        L = sb("L", [P, HEADS])
        rL = sb("rL", [P, 2, HEADS])
        mx = sb("mx", [P, HEADS])
        st2 = sb("st2", [P, 6])
        mv2 = sb("mv2", [P, 2])
        ve2 = sb("ve2", [P, 1])
        rs2 = sb("rs2", [P, 1])
        r1 = sb("r1", [P, D])
        r2 = sb("r2", [P, D])
        st3 = sb("st3", [P, 6])
        mv3 = sb("mv3", [P, 2])
        ve3 = sb("ve3", [P, 1])
        rs3 = sb("rs3", [P, 1])
        cT = sb("cT", [CD, 2, P])
        cT_hi, cT_lo = sb("cT_hi", [CD, 2, P], F32R), sb("cT_lo", [CD, 2, P], F32R)

        xg = sb("xg", [P, GT, D])
        iota8 = sb("iota8", [P, NE])
        topi = sb("topi", [P, GT, 8], mybir.dt.uint32)
        topf = sb("topf", [P, GT, 8])
        sel1 = sb("sel1", [P, GT, NE])
        gT = sb("gT", [P, 2, NH, GN])
        sc = sb("sc", [P, GT, NE])
        scb = sb("scb", [P, GT, NE])
        top = sb("top", [P, GT, 8])
        sel = sb("sel", [P, GT, NE])
        smax = sb("smax", [P, GT])
        sh = sb("sh", [P, GT, NE])
        ex = sb("ex", [P, GT, NE])
        exs = sb("exs", [P, GT, NE])
        es = sb("es", [P, GT])
        er = sb("er", [P, GT])
        ew = sb("ew", [P, 2, GT, NE])
        ewT = sb("ewT", [NE, GN])
        yacc = sb("yacc", [P, GT, D])
        fst = sb("fst", [P, GT, 6])
        fmv = sb("fmv", [P, GT, 2])
        fve = sb("fve", [P, GT])
        frs = sb("frs", [P, GT])
        yo = wide[:, 0:2 * GT * D].rearrange("p (b a d) -> p b a d", b=2, a=GT)

        block = ctx.enter_context(nc.Block())

        x_first, x_rest = sem("x_first"), sem("x_rest")
        w_in, w_out, w_vo, w_cross, w_ffn = sem("w_in"), sem("w_out"), sem("w_vo"), sem("w_cross"), sem("w_ffn")
        staged, split, consts = sem("staged"), sem("split"), sem("consts")
        zeroed = sem("zeroed")

        slices = []
        for c in range(2):
            slices.append((wqT[:, c * HW:(c + 1) * HW], P, wq_hi[:, c * HW:(c + 1) * HW], wq_lo[:, c * HW:(c + 1) * HW]))
        for src, rows, hi, lo in ((xwq, P, xwq_hi, xwq_lo), (xwk, CD, xwk_hi, xwk_lo)):
            for c in range(2):
                cs = slice(c * HW, (c + 1) * HW)
                slices.append((src[:, cs], rows, hi[:, cs], lo[:, cs]))
        for n in range(NE):
            slices.append((wl1[:, n, :], P, wl1_hi[:, n, :], wl1_lo[:, n, :]))
        SELF_SPLITS, CROSS_SPLITS, ALL_SPLITS = 2, 6, len(slices)

        def staging(n):
            return PT[:, n * HW:(n + 1) * HW] if n < SELF_SPLITS else stage[0:slices[n][1], :]

        a = {n: sem("a_" + n) for n in (
            "stats", "aggr", "var", "rstd", "xn", "xT_ps", "xT", "xhi", "xlo", "kv", "q", "sq", "vS", "v", "ssq", "pow",
            "cap", "qn", "kn", "knT", "kbd", "qT_ps", "qT", "s", "exp", "sum", "rl", "norm", "pT_ps", "pT",
            "o", "oT", "y", "yS", "y1", "y2", "y3", "yrstd", "yn", "yr", "z1", "z2", "z3", "zrstd", "x1")}
        b = {n: sem("b_" + n) for n in (
            "vo_even", "vo", "vo_hi", "vo_lo", "zero", "ctx", "chi", "clo", "xs", "xT_ps", "xhi", "xlo", "q", "qT",
            "k", "kbd0", "kbd1", "kbd2", "kbd3", "u", "u0", "u1", "u2", "u3", "s", "max", "sub", "exp", "norm", "sum",
            "rl", "pT_ps", "pT", "y", "r", "rb", "z1", "z2", "z3", "zrstd", "x2")}
        f = {n: sem("f_" + n) for n in (
            "xs", "xT_ps", "xT", "xhi", "xlo", "sc_ps", "sc", "scb", "top", "topi", "topf", "sel1", "sel", "smax",
            "sh", "ex", "exs", "es", "er", "ew", "ewT_ps", "ewT", "bias", "init", "w1", "silu", "g", "w2", "acc",
            "st", "mv", "ve", "rstd", "yo", "out")}

        def pipeline(eng, body, first, last):
            for i in range(first):
                body(i, i % 2)
            with eng.Fori(first // 2, T // 2 - 1) as j:
                body(2 * j, 0)
                body(2 * j + 1, 1)
            for i in range(T - 2, last + 1):
                body(i, i % 2)

        A_FIRST, B_FIRST = 8, 4

        def ffn_loop(eng, group):
            group(0, 0)
            group(1, 1)
            with eng.Fori(1, G // 2 - 1) as j:
                group(2 * j, 0)
                group(2 * j + 1, 1)
            group(G - 2, 0)
            group(G - 1, 1)

        def dve_wait(sem_, value):
            nc.vector.wait_ge(sem_, value)
            nc.vector.tensor_copy(seen[:, 1:2], seen[:, 0:1])

        def pool_copy(dst, src):
            one = ones[:, :]
            if len(src.shape) == 3:
                one = one.unsqueeze(2)
            return nc.gpsimd.tensor_tensor(dst, src, one.broadcast_to(list(src.shape)), ALU.mult)

        CHUNK_BANK = (7, 2, 3, 0)

        def x_bank(t):
            return 0 if later(t, 2) else 1

        def b_k(copy, eng, t, c):
            eng.wait_ge(b["k"], 2 * t + c + 1)
            if later(t, 1):
                eng.wait_ge(b["s"], 2 * t)
            for h in range(2):
                r = slice(h * DH, (h + 1) * DH)
                copy(KBD[r, :, :, 2 * c:2 * c + 2, r].rearrange("d p s a k -> d (p s) a k"),
                     bank[CHUNK_BANK[c]][r, :].rearrange("d (a s k) -> d s a k", a=2, k=SEQ))\
                    .then_inc(b[f"kbd{c}"], 1)

        def b_u(copy, eng, t, p, c):
            eng.wait_ge(b["u"], NVO * t + c + 1)
            if later(t, 2):
                eng.wait_ge(b["y"], t - 1)
            blocks = HVO // 2
            for s in range(PB):
                for h in range(2):
                    u = copy(VBD[h * SEQ:(h + 1) * SEQ, p, s, c * blocks:(c + 1) * blocks, :],
                             bank[CHUNK_BANK[c]][s * SEQ:(s + 1) * SEQ, :]
                             .rearrange("k (a h d) -> k a h d", a=blocks, h=2)[:, :, h, :])
            u.then_inc(b[f"u{c}"], 1)

        def has(t):
            return 0 <= t < T if isinstance(t, int) else True

        def stage_of(fn, i, p, back):
            t = i - back
            if isinstance(t, int) and not 0 <= t < T:
                return
            fn(t, (p - back) % 2)

        @block.sync
        def _(sp):
            x_v = x.rearrange("(t p) d -> p t d", p=P)
            sp.dma_start(X[:, 0:4, :], x_v[:, 0:4, :]).then_inc(x_first, 16)
            small = ((g1_sb[:, :], g1.rearrange("(p a) -> p a", a=1)), (wkv_sb[:, :], wkvT))
            for dst, src in small:
                sp.dma_start(dst, src).then_inc(w_in, 16)
            for n, (src, rows, _, _) in enumerate(slices):
                if n >= SELF_SPLITS:
                    sp.wait_ge(split, 2 * n)
                sp.dma_start(staging(n), src).then_inc(staged, 16)
                if n == 1:
                    sp.dma_start(wout_sb[:, :, :], woutT).then_inc(w_out, 16)
                    sp.dma_start(g2_sb[:, :], g2.partition_broadcast(P)).then_inc(w_out, 16)
                    sp.dma_start(X[:, 4:T, :], x_v[:, 4:T, :]).then_inc(x_rest, 16)

        @block.gpsimd
        def _(pool):
            def ln_in(t, p):
                pool.wait_ge(a["var"], t + 1)
                nc.gpsimd.tensor_tensor(rs[:, p, :], ve[:, p, :], mhalf[:, 0:1], ALU.pow).then_inc(a["rstd"], 1)

            nc.gpsimd.memset(ident[:, :], 1.0).then_inc(consts, 1)
            nc.gpsimd.memset(ones[:, :], 1.0)
            nc.gpsimd.memset(ident_b[:, :], 1.0)
            nc.gpsimd.memset(causal[:, :, :], 0.0).then_inc(consts, 1)
            nc.gpsimd.memset(mhalf[:, :], -0.5).then_inc(consts, 1)
            nc.gpsimd.memset(euler[:, :], 2.718281828459045).then_inc(consts, 1)
            nc.gpsimd.memset(caps[:, 0:HEADS], 16.0e12).then_inc(consts, 1)
            nc.gpsimd.memset(caps[:, HEADS:HEADS + 1], 1.0e12).then_inc(consts, 1)
            pool.wait_ge(consts, 6)
            nc.gpsimd.affine_select(out=ident[:, :], in_=ident[:, :], compare_op=ALU.is_equal, fill=0.0, base=0,
                                    pattern=[[-1, P]], channel_multiplier=1).then_inc(consts, 1)
            pool.wait_ge(consts, 7)
            nc.gpsimd.iota(iota8[:, :], pattern=[[1, NE]], base=0, channel_multiplier=0,
                           allow_small_or_imprecise_dtypes=True).then_inc(consts, 1)
            for h in range(PB):
                pool.wait_ge(consts, 8 + h)
                c = causal[h * SEQ:(h + 1) * SEQ, :, :]
                nc.gpsimd.affine_select(out=c, in_=c, compare_op=ALU.is_ge, fill=FUTURE, base=0,
                                        pattern=[[0, HEADS // 2], [-1, SEQ]], channel_multiplier=1)\
                  .then_inc(consts, 1)
            pool.wait_ge(consts, 8 + PB)
            nc.gpsimd.affine_select(out=ident_b[:, :], in_=ident_b[:, :], compare_op=ALU.is_equal, fill=0.0, base=0,
                                    pattern=[[-1, P]], channel_multiplier=1).then_inc(consts, 1)
            pool.wait_ge(consts, 11)
            ln_in(0, 0)
            nc.gpsimd.dma_start(bo_sb[:, :], bo.partition_broadcast(P)).then_inc(w_cross, 16)
            nc.gpsimd.dma_start(wr_sb[:, :], wrT).then_inc(w_ffn, 16)
            nc.gpsimd.dma_start(br_sb[:, :], br.partition_broadcast(P)).then_inc(w_ffn, 16)
            nc.gpsimd.dma_start(bN_sb[:, :], bN.partition_broadcast(P)).then_inc(w_ffn, 16)
            nc.gpsimd.dma_start(wl2_sb[:, :, :, :], wl2).then_inc(w_ffn, 16)
            nc.gpsimd.dma_start(bl1_sb[:, :, :], bl1).then_inc(w_ffn, 16)
            nc.gpsimd.dma_start(bl2_sb[:, :], bl2).then_inc(w_ffn, 16)

            def norms(t, p):
                pool.wait_ge(a["ssq"], t + 1)
                if later(t, 1):
                    pool.wait_ge(a["cap"], t)
                nc.gpsimd.tensor_tensor(rq[:, :], ssq[:, :], mhalf[:, 0:HEADS + 1], ALU.pow).then_inc(a["pow"], 1)

            def weights(t, p):
                pool.wait_ge(a["rl"], t + 1)
                v = PR[:, p, :].rearrange("q (h k) -> q h k", k=SEQ)
                nc.gpsimd.tensor_tensor(v, v, rL[:, p, :].unsqueeze(2).broadcast_to([P, HEADS, SEQ]), ALU.mult)\
                  .then_inc(a["norm"], 1)

            def y_rstd(t, p):
                pool.wait_ge(a["y3"], t + 1)
                nc.gpsimd.tensor_tensor(rs2[:, :], ve2[:, :], mhalf[:, 0:1], ALU.pow).then_inc(a["yrstd"], 1)

            def z_rstd(t, p):
                pool.wait_ge(a["z3"], t + 1)
                nc.gpsimd.tensor_tensor(rs3[:, :], ve3[:, :], mhalf[:, 0:1], ALU.pow).then_inc(a["zrstd"], 1)

            def fetch(t, p):
                pool.wait_ge(a["x1"], t + 1)
                if later(t, 2):
                    pool.wait_ge(b["xT_ps"], t - 1)
                pool_copy(xs[:, p, :], X[:, bass.ds(t, 1), :].rearrange("q a d -> q (a d)"))\
                  .then_inc(b["xs"], 1)

            def body(i, p):
                if isinstance(i, int) and i == T - 1:
                    fetch(0, 0)
                    fetch(1, 1)
                stage_of(ln_in, i, p, -1)
                stage_of(y_rstd, i, p, 4)
                stage_of(norms, i, p, 0)
                stage_of(z_rstd, i, p, 4)
                stage_of(weights, i, p, 1)
            pipeline(pool, body, A_FIRST, T - 1)

            def b_weights(t, p):
                pool.wait_ge(b["rl"], t + 1)
                v = PR[:, p, :].rearrange("q (h k) -> q h k", k=SEQ)
                nc.gpsimd.tensor_tensor(v, v, rL[:, p, :].unsqueeze(2).broadcast_to([P, HEADS, SEQ]), ALU.mult)\
                  .then_inc(b["norm"], 1)

            def cross_tail(t, p):
                pool.wait_ge(b["z3"], t + 1)
                nc.gpsimd.tensor_tensor(rs3[:, :], ve3[:, :], mhalf[:, 0:1], ALU.pow).then_inc(b["zrstd"], 1)

            def cross(i, p):
                if p == 0 and has(i + 2):
                    fetch(i + 2, 0)
                    fetch(i + 3, 1)
                stage_of(cross_tail, i, p, 3)
                stage_of(b_weights, i, p, 1)
                if isinstance(i, int) and i == 0:
                    body(T + 1, 1)
                    body(T + 2, 0)
                if isinstance(i, int) and i == 1:
                    body(T + 3, 1)
            body(T, 0)
            pipeline(pool, cross, B_FIRST, T - 1)

            def group_front(g, p):
                pool.wait_ge(b["x2"], GT * (g + 1))
                if later(g, 1):
                    pool.wait_ge(f["xT_ps"], g)
                pool_copy(xg[:, :, :], X[:, bass.ds(g * GT, GT), :]).then_inc(f["xs"], 1)

            def router_exp(g, p):
                pool.wait_ge(f["sh"], g + 1)
                nc.gpsimd.tensor_tensor(ex[:, :, :].rearrange("p a b -> p (a b)"), euler[:, 0:GT * NE],
                                        sh[:, :, :].rearrange("p a b -> p (a b)"), ALU.pow).then_inc(f["ex"], 1)

            def group_tail(g, p):
                pool.wait_ge(f["ve"], g + 1)
                nc.gpsimd.tensor_tensor(frs[:, :], fve[:, :], mhalf[:, 0:GT], ALU.pow).then_inc(f["rstd"], 1)

            def group(g, p):
                more = not (isinstance(g, int) and g == G - 1)
                if more:
                    group_front(g + 1, 1 - p)
                if later(g, 1):
                    group_tail(g - 1, 1 - p)
                if more:
                    router_exp(g + 1, 1 - p)
            group_front(0, 0)
            cross(T, 0)
            cross(T + 1, 1)
            router_exp(0, 0)
            cross(T + 2, 0)
            ffn_loop(pool, group)
            group_tail(G - 1, 1)

        @block.scalar
        def _(act):
            def x_T(t, p):
                act.wait_ge(a["xT_ps"], t + 1)
                if later(t, 2):
                    act.wait_ge(a["q"], 2 * (t - 1))
                    act.wait_ge(a["xlo"], t - 1)
                nc.scalar.activation(xT[:, p, :], bank[0][:, 0:P], ACT.Copy, scale=g1_sb[:, 0:1]).then_inc(a["xT"], 1)
                act.wait_ge(a["xT"], t + 1)
                nc.scalar.activation(xT_hi[:, p, :], xT[:, p, :], ACT.Copy).then_inc(a["xhi"], 1)

            def vo_round(c):
                act.wait_ge(b["vo"], c + 1)
                nc.scalar.activation(vo_hi[:, c, :], bank[4 + c][0:CD, :], ACT.Copy).then_inc(b["vo_hi"], 1)

            def squares(t, p):
                act.wait_ge(a["kv"], t + 1)
                if later(t, 1):
                    act.wait_ge(a["ssq"], t)
                nc.scalar.activation(wide[:, W:W + DH], bank[1][:, 0:DH], ACT.Square).then_inc(a["sq"], 1)
                if later(t, 2):
                    act.wait_ge(a["v"], t - 1)
                nc.scalar.activation(vS[:, p, :], bank[1][:, DH:2 * DH], ACT.Copy).then_inc(a["vS"], 1)
                for c in range(2):
                    act.wait_ge(a["q"], 2 * t + c + 1)
                    nc.scalar.activation(wide[:, c * HW:(c + 1) * HW], bank[2 + c][:, :], ACT.Square)\
                      .then_inc(a["sq"], 1)

            def q_T(t, p):
                act.wait_ge(a["knT"], t + 1)
                if later(t, 2):
                    act.wait_ge(a["s"], 2 * (t - 1))
                for h in range(2):
                    r = slice(h * DH, (h + 1) * DH)
                    k = nc.scalar.activation(KBD[r, p, :, 0, r], bank[7][r, 0:P].rearrange("d (s k) -> d s k", s=PB),
                                             ACT.Copy)
                k.then_inc(a["kbd"], 1)
                for c in range(2):
                    act.wait_ge(a["qT_ps"], 2 * t + c + 1)
                    nc.scalar.activation(QT[:, p, c * HBLK:(c + 1) * HBLK, :].rearrange("d a q -> d (a q)"),
                                         bank[4 + c][:, :], ACT.Copy).then_inc(a["qT"], 1)

            def exp_half(t, p, c):
                if later(t, 2):
                    act.wait_ge(a["pT_ps"], 2 * (t - 1))
                act.wait_ge(a["s"], 2 * t + c + 1)
                nc.scalar.activation(PR[:, p, c * HW:(c + 1) * HW], bank[6][:, :], ACT.Exp, scale=16.0)\
                  .then_inc(a["exp"], 1)

            def p_T(t, p, c):
                if later(t, 1):
                    act.wait_ge(a["o"], 2 * t)
                v = PT[:, :].rearrange("k (s a q) -> k s a q", s=PB, a=NBLK)
                act.wait_ge(a["pT_ps"], 2 * t + c + 1)
                nc.scalar.activation(v[:, :, c * HBLK:(c + 1) * HBLK, :],
                                     bank[4 + c][:, :].rearrange("k (a s q) -> k s a q", a=HBLK, s=PB),
                                     ACT.Copy).then_inc(a["pT"], 1)

            def o_T(t, p, s):
                if later(t, 1):
                    act.wait_ge(a["y"], t)
                act.wait_ge(a["o"], 2 * t + s + 1)
                nc.scalar.activation(OT[:, :, s * SEQ:(s + 1) * SEQ],
                                     bank[0 if s else 7][:, :].rearrange("d (a q) -> d a q", a=NBLK), ACT.Copy)\
                  .then_inc(a["oT"], 1)

            def y_evac(t, p):
                act.wait_ge(a["y"], t + 1)
                if later(t, 1):
                    act.wait_ge(a["yn"], t)
                nc.scalar.activation(yS[:, :], bank[0][:, 0:D], ACT.Copy).then_inc(a["yS"], 1)

            act.dma_start(xwvT_sb[:, :, :], xwvT).then_inc(w_vo, 16)
            act.dma_start(xwo_sb[:, :, :], xwo).then_inc(w_vo, 16)
            act.dma_start(cT[:, :, :], ctxT[:, 0:2 * P].rearrange("c (a t) -> c a t", a=2)).then_inc(b["ctx"], 16)
            act.wait_ge(w_in, 32)
            act.wait_ge(zeroed, 1)

            def body(i, p):
                if isinstance(i, int) and i == 0:
                    x_T(0, 0)
                stage_of(squares, i, p, 0)
                stage_of(q_T, i, p, 1)
                stage_of(y_evac, i, p, 3)
                stage_of(lambda t, q: exp_half(t, q, 0), i, p, 1)
                stage_of(lambda t, q: p_T(t, q, 0), i, p, 2)
                stage_of(lambda t, q: p_T(t, q, 1), i, p, 2)
                stage_of(x_T, i, p, -1)
                stage_of(lambda t, q: exp_half(t, q, 1), i, p, 1)
                stage_of(lambda t, q: o_T(t, q, 0), i, p, 2)
                stage_of(lambda t, q: o_T(t, q, 1), i, p, 2)
                if isinstance(i, int) and i == 0:
                    for c in range(NVO):
                        vo_round(c)
            pipeline(act, body, A_FIRST, T - 1)


            def x_hi(t, p):
                act.wait_ge(b["xT_ps"], t - p + 2)
                if later(t, 2):
                    act.wait_ge(b["q"], 2 * (t - p))
                nc.scalar.activation(xT_hi[:, p, :], bank[x_bank(t)][:, p * P:(p + 1) * P], ACT.Copy)\
                  .then_inc(b["xhi"], 1)

            def c_hi(t, p):
                act.wait_ge(b["ctx"], 8 * (t - p) + 16)
                if later(t, 2):
                    act.wait_ge(b["u"], NVO * (t - 1))
                nc.scalar.activation(cT_hi[:, p, :], cT[:, p, :], ACT.Copy).then_inc(b["chi"], 1)

            def load_ctx(t):
                act.wait_ge(b["ctx"], 8 * t)
                act.wait_ge(b["clo"], t)
                act.dma_start(cT[:, :, :], ctxT[:, bass.ds(t * P, 2 * P)].rearrange("c (a t) -> c a t", a=2))\
                   .then_inc(b["ctx"], 16)

            def b_q(t, c):
                if later(t, 1):
                    act.wait_ge(b["s"], 2 * t)
                act.wait_ge(b["q"], 2 * t + c + 1)
                nc.scalar.activation(QT[:, :, 2 * c:2 * c + 2, :],
                                     bank[CHUNK_BANK[c]][:, :].rearrange("d (a p q) -> d p a q", a=2, p=2),
                                     ACT.Copy).then_inc(b["qT"], 1)

            def b_exp(t, p, c):
                act.wait_ge(b["sub"], 2 * t + c + 1)
                v = PR[:, p, c * HW:(c + 1) * HW]
                nc.scalar.activation(v, v, ACT.Exp, scale=DH ** -0.5).then_inc(b["exp"], 1)

            def b_pT(t, p):
                if later(t, 1):
                    act.wait_ge(b["y"], t)
                for c in range(2):
                    act.wait_ge(b["pT_ps"], 2 * t + c + 1)
                    nc.scalar.activation(PT[:, c * HW:(c + 1) * HW], bank[4 + c][:, :], ACT.Copy)\
                      .then_inc(b["pT"], 1)

            def cross(i, p):
                pair = p == 0 and has(i)
                if pair:
                    c_hi(i, 0)
                    c_hi(i + 1, 1)
                if p == 1 and has(i + 1):
                    x_hi(i + 1, 0)
                    x_hi(i + 2, 1)
                stage_of(lambda t, q: b_exp(t, q, 0), i, p, 1)
                if p == 1 and has(i + 1):
                    load_ctx(i + 1)
                if p == 1:
                    stage_of(b_pT, i, p, 2)
                if p == 1 and has(i):
                    b_u(nc.scalar.copy, act, i - 1, 0, 0)
                if pair:
                    for c in (0, 1, 2):
                        b_q(i, c)
                stage_of(lambda t, q: b_exp(t, q, 1), i, p, 1)
                if p == 0:
                    stage_of(b_pT, i, p, 2)
                if pair:
                    b_q(i, 3)
                    b_k(nc.scalar.copy, act, i, 0)
                    b_k(nc.scalar.copy, act, i, 2)
                if p == 1 and has(i):
                    b_u(nc.scalar.copy, act, i - 1, 0, 2)
                    for c in (0, 1, 2, 3):
                        b_u(nc.scalar.copy, act, i, 1, c)
                if isinstance(i, int) and i == 0:
                    for c in range(2):
                        p_T(T - 1, 1, c)
                    y_evac(T - 2, 0)
                    for c in range(2):
                        o_T(T - 1, 1, c)
                    y_evac(T - 1, 1)
            x_hi(0, 0)
            x_hi(1, 1)
            body(T, 0)
            act.wait_ge(b["zero"], 1)
            pipeline(act, cross, B_FIRST, T - 1)


            def front_x(g, p, bk=6):
                act.wait_ge(f["xT_ps"], g + 1)
                if later(g, 2):
                    act.wait_ge(f["sc_ps"], g - 1)
                    act.wait_ge(f["xlo"], g - 1)
                nc.scalar.activation(fT[:, p, :], bank[bk][:, :], ACT.Copy).then_inc(f["xT"], 1)
                act.wait_ge(f["xT"], g + 1)
                if later(g, 2):
                    act.wait_ge(f["w1"], 2 * NH * NE * (g - 1))
                nc.scalar.activation(fT_hi[:, p, :], fT[:, p, :], ACT.Copy).then_inc(f["xhi"], 1)

            def front_ew(g, p):
                act.wait_ge(f["ewT_ps"], g + 1)
                if later(g, 1):
                    act.wait_ge(f["bias"], g)
                nc.scalar.activation(ewT[:, :], bank[6][0:NE, :], ACT.Copy).then_inc(f["ewT"], 1)

            out_v = out.rearrange("(t p) d -> p t d", p=P)

            def store(g, p):
                act.wait_ge(f["yo"], g + 1)
                if later(g, 1):
                    act.wait_ge(f["out"], 16 * g)
                act.dma_start(out_v[:, bass.ds(g * GT, GT), :], yo[:, p, :, :]).then_inc(f["out"], 16)

            def silus(g, n):
                for c in range(NH):
                    k = NE * NH * g + NH * n + c
                    act.wait_ge(f["w1"], 2 * k + 1)
                    if later(k, NH):
                        act.wait_ge(f["g"], k - NH + 1)
                    nc.scalar.activation(sg[:, c, :], bank[2 * c][:, :], ACT.Silu, bias=bl1_sb[:, n, c:c + 1])\
                      .then_inc(f["silu"], 1)

            def group(g, p):
                more = not (isinstance(g, int) and g == G - 1)
                for n in range(NE):
                    silus(g, n)
                    if n == 0 and isinstance(g, int) and g == 0:
                        b_pT(T - 1, 1)
                    if n == 1 and isinstance(g, int) and g == 0:
                        front_ew(0, 0)
                    if n == 1 and more:
                        front_x(g + 1, 1 - p)
                    if n == 6 and more:
                        front_ew(g + 1, 1 - p)
                    if n == 4 and later(g, 1):
                        store(g - 1, 1 - p)
            b_exp(T - 1, 1, 0)
            b_pT(T - 2, 0)
            front_x(0, 0, 7)
            b_exp(T - 1, 1, 1)
            act.wait_ge(w_ffn, 96)
            ffn_loop(act, group)
            store(G - 1, 1)
            act.wait_ge(f["out"], 16 * G)

        @block.vector
        def _(dve):
            V = nc.vector

            V.memset(seen[:, :], 0.0)
            V.memset(KBD[:, :, :, 0, :], 0.0)
            V.memset(VBD[:, :, :, 0, :], 0.0).then_inc(zeroed, 1)
            V.memset(KBD[:, :, :, 1:NBLK, :], 0.0).then_inc(b["zero"], 1)

            def split_slice(n):
                _, rows, hi, lo = slices[n]
                dve.wait_ge(staged, 16 * max(n + 1, SELF_SPLITS))
                V.tensor_copy(hi, staging(n)).then_inc(split, 1)
                dve.wait_ge(split, 2 * n + 1)
                V.tensor_tensor(lo, staging(n), hi.bitcast(F32), ALU.subtract).then_inc(split, 1)

            def vo_split(c):
                dve.wait_ge(b["vo_hi"], c + 1)
                V.tensor_tensor(vo_lo[:, c, :], bank[4 + c][0:CD, :], vo_hi[:, c, :].bitcast(F32), ALU.subtract)\
                 .then_inc(b["vo_lo"], 1)

            def ln_a(t, p):
                V.bn_stats(st[:, :], X[:, bass.ds(t, 1), :].rearrange("q a d -> q (a d)")).then_inc(a["stats"], 1)
                dve_wait(a["stats"], t + 1)
                V.bn_aggr(mv[:, p, :], st[:, :]).then_inc(a["aggr"], 1)
                dve.wait_ge(a["aggr"], t + 1)
                V.tensor_scalar(ve[:, p, :], mv[:, p, 1:2], EPS, None, ALU.add).then_inc(a["var"], 1)

            def ln_b(t, p):
                dve.wait_ge(a["rstd"], t + 1)
                if later(t, 2):
                    dve.wait_ge(a["xT_ps"], t - 1)
                V.tensor_scalar(xn[:, p, :], X[:, bass.ds(t, 1), :].rearrange("q a d -> q (a d)"), mv[:, p, 0:1],
                                rs[:, p, :], ALU.subtract, ALU.mult).then_inc(a["xn"], 1)

            def x_lo(t, p):
                dve.wait_ge(a["xhi"], t + 1)
                V.tensor_tensor(xT_lo[:, p, :], xT[:, p, :], xT_hi[:, p, :].bitcast(F32), ALU.subtract)\
                  .then_inc(a["xlo"], 1)

            def sums(t, p):
                dve.wait_ge(a["sq"], 3 * (t + 1))
                if later(t, 1):
                    dve.wait_ge(a["pow"], t)
                V.tensor_reduce(ssq[:, :], wide[:, :].rearrange("q (h d) -> q h d", d=DH), AX.X, ALU.add)\
                 .then_inc(a["ssq"], 1)

            def normalise(t, p):
                dve.wait_ge(a["pow"], t + 1)
                if later(t, 1):
                    dve.wait_ge(a["kn"], t)
                V.tensor_tensor(rinv[:, :], rq[:, :], caps[:, :], ALU.min).then_inc(a["cap"], 1)
                dve.wait_ge(a["cap"], t + 1)
                dve.wait_ge(a["vS"], t + 1)
                if later(t, 1):
                    dve.wait_ge(a["knT"], t)
                V.tensor_scalar(kn[:, :, :], bank[1][:, 0:DH].unsqueeze(1).broadcast_to([P, PB, DH]),
                                rinv[:, HEADS:HEADS + 1], None, ALU.mult).then_inc(a["kn"], 1)
                for c in range(2):
                    if later(t, 1):
                        dve.wait_ge(a["qT_ps"], 2 * t)
                    hs = slice(c * HEADS // 2, (c + 1) * HEADS // 2)
                    V.tensor_tensor(qn[:, c * HW:(c + 1) * HW].rearrange("q (h d) -> q h d", d=DH),
                                    bank[2 + c][:, :].rearrange("q (h d) -> q h d", d=DH),
                                    rinv[:, hs].unsqueeze(2).broadcast_to([P, HEADS // 2, DH]), ALU.mult)\
                     .then_inc(a["qn"], 1)

            def v_bd(t, p):
                dve.wait_ge(a["vS"], t + 1)
                if later(t, 2):
                    dve.wait_ge(a["o"], 2 * (t - 1))
                for s in range(PB):
                    for h in range(2):
                        v = V.tensor_copy(VBD[h * DH:(h + 1) * DH, p, s, 0, h * DH:(h + 1) * DH],
                                          vS[s * SEQ:(s + 1) * SEQ, p, :])
                v.then_inc(a["v"], 1)

            def softmax(t, p):
                dve.wait_ge(a["exp"], 2 * (t + 1))
                v = PR[:, p, :].rearrange("q (h k) -> q h k", k=SEQ)
                V.tensor_reduce(L[:, :], v, AX.X, ALU.add).then_inc(a["sum"], 1)
                dve.wait_ge(a["sum"], t + 1)
                V.reciprocal(rL[:, p, :], L[:, :]).then_inc(a["rl"], 1)

            def tail_a(t, p):
                dve.wait_ge(a["yS"], t + 1)
                V.bn_stats(st2[:, :], yS[:, :]).then_inc(a["y1"], 1)
                dve_wait(a["y1"], t + 1)
                V.bn_aggr(mv2[:, :], st2[:, :]).then_inc(a["y2"], 1)
                dve.wait_ge(a["y2"], t + 1)
                V.tensor_scalar(ve2[:, :], mv2[:, 1:2], EPS, None, ALU.add).then_inc(a["y3"], 1)
                V.scalar_tensor_tensor(out=yg[:, :], in0=yS[:, :], scalar=mv2[:, 0:1], in1=g2_sb[:, :],
                                       op0=ALU.subtract, op1=ALU.mult).then_inc(a["yn"], 1)

            def tail_b(t, p):
                dve.wait_ge(a["yrstd"], t + 1)
                if later(t, 1):
                    dve.wait_ge(a["x1"], t)
                dve.wait_ge(a["yn"], t + 1)
                V.scalar_tensor_tensor(out=r1[:, :], in0=yg[:, :], scalar=rs2[:, :],
                                       in1=X[:, bass.ds(t, 1), :].rearrange("q a d -> q (a d)"),
                                       op0=ALU.mult, op1=ALU.add).then_inc(a["yr"], 1)
                dve.wait_ge(a["yr"], t + 1)
                V.bn_stats(st3[:, :], r1[:, :]).then_inc(a["z1"], 1)
                dve_wait(a["z1"], t + 1)
                V.bn_aggr(mv3[:, :], st3[:, :]).then_inc(a["z2"], 1)
                dve.wait_ge(a["z2"], t + 1)
                V.tensor_scalar(ve3[:, :], mv3[:, 1:2], EPS, None, ALU.add).then_inc(a["z3"], 1)

            def tail_c(t, p):
                dve.wait_ge(a["zrstd"], t + 1)
                V.tensor_scalar(X[:, bass.ds(t, 1), :].rearrange("q a d -> q (a d)"), r1[:, :], mv3[:, 0:1],
                                rs3[:, :], ALU.subtract, ALU.mult).then_inc(a["x1"], 1)

            dve.wait_ge(x_first, 16)
            ln_a(0, 0)
            ln_b(0, 0)
            for n in range(SELF_SPLITS):
                split_slice(n)
            dve.wait_ge(consts, 11)

            def body(i, p):
                if isinstance(i, int) and i == 0:
                    x_lo(0, 0)
                if isinstance(i, int) and i == 3:
                    dve.wait_ge(x_rest, 16)
                    dve.wait_ge(w_out, 32)
                stage_of(ln_a, i, p, -1)
                stage_of(sums, i, p, 0)
                stage_of(tail_b, i, p, 4)
                stage_of(ln_b, i, p, -1)
                if isinstance(i, int) and 2 <= 2 * i + 1 < ALL_SPLITS:
                    split_slice(2 * i + 1)
                stage_of(tail_a, i, p, 3)
                stage_of(v_bd, i, p, 1)
                stage_of(normalise, i, p, 0)
                stage_of(x_lo, i, p, -1)
                stage_of(softmax, i, p, 1)
                stage_of(tail_c, i, p, 4)
                if isinstance(i, int) and i == 0:
                    for c in range(NVO):
                        vo_split(c)
                if isinstance(i, int) and 2 * i + 2 < ALL_SPLITS:
                    split_slice(2 * i + 2)
            pipeline(dve, body, A_FIRST, T - 1)


            def x_lo2(t, p):
                dve.wait_ge(b["xhi"], t - p + 2)
                if later(t, 2):
                    dve.wait_ge(b["q"], 2 * (t - p))
                V.tensor_tensor(xT_lo[:, p, :], bank[x_bank(t)][:, p * P:(p + 1) * P], xT_hi[:, p, :].bitcast(F32),
                                ALU.subtract).then_inc(b["xlo"], 1)

            def c_lo(t, p):
                dve.wait_ge(b["chi"], t + 1)
                if later(t, 2):
                    dve.wait_ge(b["u"], NVO * (t - 1))
                V.tensor_tensor(cT_lo[:, p, :], cT[:, p, :], cT_hi[:, p, :].bitcast(F32), ALU.subtract)\
                 .then_inc(b["clo"], 1)

            def b_max(t, p, c):
                dve.wait_ge(b["s"], 2 * t + c + 1)
                v = bank[6][:, :].rearrange("q (h k) -> q h k", k=SEQ)
                V.tensor_reduce(mx[:, 0:HEADS // 2], v, AX.X, ALU.max).then_inc(b["max"], 1)
                dve.wait_ge(b["max"], 2 * t + c + 1)
                if later(t, 2):
                    dve.wait_ge(b["pT_ps"], 2 * (t - 1))
                V.tensor_tensor(PR[:, p, c * HW:(c + 1) * HW].rearrange("q (h k) -> q h k", k=SEQ), v,
                                mx[:, 0:HEADS // 2].unsqueeze(2).broadcast_to([P, HEADS // 2, SEQ]), ALU.subtract)\
                 .then_inc(b["sub"], 1)

            def b_sum(t, p):
                dve.wait_ge(b["exp"], 2 * (t + 1))
                V.tensor_reduce(L[:, :], PR[:, p, :].rearrange("q (h k) -> q h k", k=SEQ), AX.X, ALU.add)\
                 .then_inc(b["sum"], 1)
                dve.wait_ge(b["sum"], t + 1)
                V.reciprocal(rL[:, p, :], L[:, :]).then_inc(b["rl"], 1)

            def b_tail_a(t, p, bk=1):
                dve.wait_ge(b["y"], t + 1)
                V.tensor_tensor(r1[:, :], bank[bk][:, 0:D], X[:, bass.ds(t, 1), :].rearrange("q a d -> q (a d)"),
                                ALU.add).then_inc(b["r"], 1)
                dve.wait_ge(b["r"], t + 1)
                V.tensor_tensor(r2[:, :], r1[:, :], bo_sb[:, :], ALU.add).then_inc(b["rb"], 1)
                dve.wait_ge(b["rb"], t + 1)
                V.bn_stats(st3[:, :], r2[:, :]).then_inc(b["z1"], 1)
                dve_wait(b["z1"], t + 1)
                V.bn_aggr(mv3[:, :], st3[:, :]).then_inc(b["z2"], 1)
                dve.wait_ge(b["z2"], t + 1)
                V.tensor_scalar(ve3[:, :], mv3[:, 1:2], EPS, None, ALU.add).then_inc(b["z3"], 1)

            def b_tail_b(t, p):
                dve.wait_ge(b["zrstd"], t + 1)
                V.tensor_scalar(X[:, bass.ds(t, 1), :].rearrange("q a d -> q (a d)"), r2[:, :], mv3[:, 0:1],
                                rs3[:, :], ALU.subtract, ALU.mult).then_inc(b["x2"], 1)

            dve.wait_ge(w_cross, 16)

            def cross(i, p):
                if isinstance(i, int) and i == 1:
                    dve.wait_ge(a["pT_ps"], 2 * T)
                    dve.wait_ge(a["norm"], T)
                pair = p == 0 and has(i)
                stage_of(lambda t, q: b_max(t, q, 0), i, p, 1)
                stage_of(b_tail_a, i, p, 3)
                if p == 1 and has(i + 1):
                    x_lo2(i + 1, 0)
                    x_lo2(i + 2, 1)
                stage_of(lambda t, q: b_max(t, q, 1), i, p, 1)
                if pair:
                    c_lo(i, 0)
                    c_lo(i + 1, 1)
                if p == 1 and has(i):
                    b_u(V.tensor_copy, dve, i - 1, 0, 1)
                stage_of(b_tail_b, i, p, 3)
                stage_of(b_sum, i, p, 1)
                if pair:
                    b_k(V.tensor_copy, dve, i, 1)
                    b_k(V.tensor_copy, dve, i, 3)
                if p == 1 and has(i):
                    b_u(V.tensor_copy, dve, i - 1, 0, 3)
                if isinstance(i, int) and i == 0:
                    body(T + 1, 1)
                    body(T + 2, 0)
                if isinstance(i, int) and i == 1:
                    body(T + 3, 1)
            x_lo2(0, 0)
            x_lo2(1, 1)
            body(T, 0)
            pipeline(dve, cross, B_FIRST, T - 1)


            def front(g, p):
                dve.wait_ge(f["xhi"], g + 1)
                if later(g, 2):
                    dve.wait_ge(f["w1"], 2 * NH * NE * (g - 1))
                V.tensor_tensor(fT_lo[:, p, :], fT[:, p, :], fT_hi[:, p, :].bitcast(F32), ALU.subtract)\
                 .then_inc(f["xlo"], 1)

            def router(g, p, bk=7):
                shape = [P, GT, NE]
                dve.wait_ge(f["sc_ps"], g + 1)
                V.tensor_tensor(sc[:, :, :], bank[bk][:, 0:GT * NE].rearrange("p (a b) -> p a b", a=GT),
                                br_sb[:, :].unsqueeze(1).broadcast_to(shape), ALU.add).then_inc(f["sc"], 1)
                dve.wait_ge(f["sc"], g + 1)
                V.tensor_tensor(scb[:, :, :], sc[:, :, :], bN_sb[:, :].unsqueeze(1).broadcast_to(shape), ALU.add)\
                 .then_inc(f["scb"], 1)
                V.tensor_reduce(smax[:, :], sc[:, :, :], AX.X, ALU.max).then_inc(f["smax"], 1)
                dve.wait_ge(f["smax"], g + 1)
                V.tensor_tensor(sh[:, :, :], sc[:, :, :], smax[:, :].unsqueeze(2).broadcast_to(shape), ALU.subtract)\
                 .then_inc(f["sh"], 1)
                dve_wait(f["scb"], g + 1)
                for k in range(GT):
                    V.max(top[:, k, :], scb[:, k, :]).then_inc(f["top"], 1)
                dve_wait(f["top"], GT * (g + 1))
                for k in range(GT):
                    m = V.max_index(topi[:, k, :], top[:, k, :], scb[:, k, :])
                m.then_inc(f["topi"], 1)
                dve.wait_ge(f["topi"], g + 1)
                V.tensor_copy(topf[:, :, :], topi[:, :, :]).then_inc(f["topf"], 1)
                dve.wait_ge(f["topf"], g + 1)
                io = iota8[:, :].unsqueeze(1).broadcast_to(shape)
                V.tensor_tensor(sel[:, :, :], io, topf[:, :, 0:1].broadcast_to(shape), ALU.is_equal)
                V.tensor_tensor(sel1[:, :, :], io, topf[:, :, 1:2].broadcast_to(shape), ALU.is_equal)\
                 .then_inc(f["sel1"], 1)
                dve.wait_ge(f["sel1"], g + 1)
                V.tensor_tensor(sel[:, :, :], sel[:, :, :], sel1[:, :, :], ALU.add).then_inc(f["sel"], 1)

            def router_weights(g, p):
                shape = [P, GT, NE]
                dve.wait_ge(f["sel"], g + 1)
                dve.wait_ge(f["ex"], g + 1)
                V.tensor_tensor(exs[:, :, :], ex[:, :, :], sel[:, :, :], ALU.mult).then_inc(f["exs"], 1)
                dve.wait_ge(f["exs"], g + 1)
                V.tensor_reduce(es[:, :], exs[:, :, :], AX.X, ALU.add).then_inc(f["es"], 1)
                dve.wait_ge(f["es"], g + 1)
                V.reciprocal(er[:, :], es[:, :]).then_inc(f["er"], 1)
                dve.wait_ge(f["er"], g + 1)
                V.tensor_tensor(ew[:, p, :, :], exs[:, :, :], er[:, :].unsqueeze(2).broadcast_to(shape), ALU.mult)\
                 .then_inc(f["ew"], 1)

            def gates(g, n):
                q = n % 2
                for c in range(NH):
                    k = NE * NH * g + NH * n + c
                    dve.wait_ge(f["silu"], k + 1)
                    dve.wait_ge(f["w1"], 2 * k + 2)
                    if c == 0 and later(NE * g + n, 2):
                        dve.wait_ge(f["w2"], NE * g + n - 1)
                    V.scalar_tensor_tensor(out=gT[:, q, c, :], in0=bank[2 * c + 1][:, :],
                                           scalar=bl1_sb[:, n, NH + c:NH + c + 1], in1=sg[:, c, :],
                                           op0=ALU.add, op1=ALU.mult).then_inc(f["g"], 1)

            def accumulate(g, n, p):
                k = NE * g + n
                dve.wait_ge(f["w2"], k + 1)
                dve.wait_ge(f["init"], g + 1)
                if later(k, 1):
                    dve.wait_ge(f["acc"], k)
                for tt in range(GT):
                    m = V.scalar_tensor_tensor(out=yacc[:, tt, :], in0=bank[4 + n % 2][:, tt * D:(tt + 1) * D],
                                               scalar=ew[:, p, tt, n:n + 1], in1=yacc[:, tt, :],
                                               op0=ALU.mult, op1=ALU.add)
                m.then_inc(f["acc"], 1)

            def init(g, p):
                dve.wait_ge(f["bias"], g + 1)
                V.tensor_tensor(yacc[:, :, :], bank[7][:, :].rearrange("p (a d) -> p a d", a=GT),
                                X[:, bass.ds(g * GT, GT), :], ALU.add).then_inc(f["init"], 1)

            def out_a(g):
                dve.wait_ge(f["acc"], NE * (g + 1))
                for tt in range(GT):
                    m = V.bn_stats(fst[:, tt, :], yacc[:, tt, :])
                m.then_inc(f["st"], 1)
                dve_wait(f["st"], g + 1)
                for tt in range(GT):
                    m = V.bn_aggr(fmv[:, tt, :], fst[:, tt, :])
                m.then_inc(f["mv"], 1)
                dve.wait_ge(f["mv"], g + 1)
                V.tensor_scalar(fve[:, :], fmv[:, :, 1], EPS, None, ALU.add).then_inc(f["ve"], 1)

            def out_b(g, p):
                dve.wait_ge(f["rstd"], g + 1)
                if later(g, 2):
                    dve.wait_ge(f["out"], 16 * (g - 1))
                for tt in range(GT):
                    m = V.tensor_scalar(yo[:, p, tt, :], yacc[:, tt, :], fmv[:, tt, 0:1], frs[:, tt:tt + 1],
                                        ALU.subtract, ALU.mult)
                m.then_inc(f["yo"], 1)

            def group(g, p):
                more = not (isinstance(g, int) and g == G - 1)
                for n in range(NE):
                    gates(g, n)
                    if n == 0:
                        if later(g, 1):
                            accumulate(g - 1, NE - 1, 1 - p)
                            out_a(g - 1)
                        else:
                            b_tail_a(T - 1, 1, 7)
                            router_weights(0, 0)
                    else:
                        if n == 1 and isinstance(g, int) and g == 0:
                            b_tail_b(T - 1, 1)
                            init(0, 0)
                        if n == 1 and later(g, 1):
                            out_b(g - 1, 1 - p)
                            dve.wait_ge(f["yo"], g)
                            init(g, p)
                        accumulate(g, n - 1, p)
                    if n == 2 and more:
                        front(g + 1, 1 - p)
                    if n == 3 and more:
                        router(g + 1, 1 - p)
                    if n == 5 and more:
                        router_weights(g + 1, 1 - p)
            b_max(T - 1, 1, 0)
            b_tail_a(T - 3, 1)
            b_max(T - 1, 1, 1)
            b_tail_b(T - 3, 1)
            front(0, 0)
            b_sum(T - 1, 1)
            b_tail_a(T - 2, 0)
            dve.wait_ge(w_ffn, 96)
            router(0, 0, 6)
            b_tail_b(T - 2, 0)
            ffn_loop(dve, group)
            accumulate(G - 1, NE - 1, 1)
            out_a(G - 1)
            out_b(G - 1, 1)

        @block.tensor
        def _(pe):
            M = nc.tensor.matmul

            def three(out_, l_hi, l_lo, r_hi, r_lo):
                M(out_, l_hi, r_lo, start=True, stop=False)
                M(out_, l_lo, r_hi, start=False, stop=False)
                return M(out_, l_hi, r_hi, start=False, stop=True)

            def x_T(t, p):
                pe.wait_ge(a["xn"], t + 1)
                if later(t, 4):
                    pe.wait_ge(a["yS"], t - 3)
                elif t:
                    pe.wait_ge(a["xT"], t)
                nc.tensor.transpose(bank[0][:, 0:P], xn[:, p, :], ident[:, :]).then_inc(a["xT_ps"], 1)

            def qkv(t, p):
                pe.wait_ge(a["xT"], t + 1)
                if later(t, 1):
                    pe.wait_ge(a["kn"], t)
                M(bank[1][:, 0:2 * DH], xT[:, p, :], wkv_sb[:, :], start=True, stop=True).then_inc(a["kv"], 1)
                pe.wait_ge(a["xlo"], t + 1)
                if later(t, 1):
                    pe.wait_ge(a["qn"], 2 * t)
                for c in range(2):
                    s = slice(c * HW, (c + 1) * HW)
                    three(bank[2 + c][:, :], xT_hi[:, p, :], xT_lo[:, p, :], wq_hi[:, s], wq_lo[:, s])\
                        .then_inc(a["q"], 1)

            def qk_T(t, p):
                pe.wait_ge(a["kn"], t + 1)
                if later(t, 2):
                    pe.wait_ge(a["oT"], 2 * (t - 1))
                elif t:
                    pe.wait_ge(a["kbd"], t)
                nc.tensor.transpose(bank[7][:, 0:P], kn[:, :, :].rearrange("q s d -> q (s d)"), ident[:, :])\
                  .then_inc(a["knT"], 1)
                for c in range(2):
                    pe.wait_ge(a["qn"], 2 * t + c + 1)
                    if later(t, 2):
                        pe.wait_ge(a["pT"], 2 * (t - 2) + c + 1)
                    for k in range(HBLK):
                        blk = c * HBLK + k
                        m = nc.tensor.transpose(bank[4 + c][:, k * P:(k + 1) * P], qn[:, blk * P:(blk + 1) * P],
                                                ident[:, :])
                    m.then_inc(a["qT_ps"], 1)

            def scores(t, p, c):
                pe.wait_ge(a["kbd"], t + 1)
                pe.wait_ge(a["qT"], 2 * t + c + 1)
                if later(t, 1) or c:
                    pe.wait_ge(a["exp"], 2 * t + c)
                M(bank[6][:, :], ident_b[:, :], causal[:, :, :].rearrange("q h k -> q (h k)"), start=True, stop=False)
                for k in range(HBLK):
                    for s in range(PB):
                        m = M(bank[6][s * SEQ:(s + 1) * SEQ, k * P:(k + 1) * P],
                              QT[:, p, c * HBLK + k, s * SEQ:(s + 1) * SEQ], KBD[:, p, s, 0, :],
                              start=False, stop=(k == HBLK - 1))
                m.then_inc(a["s"], 1)

            def p_T(t, p, c):
                pe.wait_ge(a["norm"], t + 1)
                if isinstance(t, int) and t + 1 >= T:
                    pe.wait_ge(a["qT"], 2 * T)
                else:
                    pe.wait_ge(a["qT"], 2 * (t + 1) + c + 1)
                for k in range(HBLK):
                    blk = c * HBLK + k
                    m = nc.tensor.transpose(bank[4 + c][:, k * P:(k + 1) * P], PR[:, p, blk * P:(blk + 1) * P],
                                            ident[:, :])
                m.then_inc(a["pT_ps"], 1)

            def values(t, p, s):
                pe.wait_ge(a["pT"], 2 * (t + 1))
                pe.wait_ge(a["v"], t + 1)
                if s and isinstance(t, int) and t >= T - 3:
                    pe.wait_ge(a["xT"], T)
                    pe.wait_ge(a["yS"], t)
                elif s:
                    pe.wait_ge(a["xT"], t + 4)
                elif isinstance(t, int) and t == T - 1:
                    pe.wait_ge(a["oT"], 2 * t)
                else:
                    pe.wait_ge(a["kbd"], t + 2)
                M(bank[0 if s else 7][:, :], VBD[:, p, s, 0, :], PT[:, s * HW:(s + 1) * HW], start=True, stop=True)\
                    .then_inc(a["o"], 1)

            def project(t, p):
                pe.wait_ge(a["oT"], 2 * (t + 1))
                for k in range(NBLK):
                    m = M(bank[0][:, 0:D], OT[:, k, :], wout_sb[:, k, :], start=(k == 0), stop=(k == NBLK - 1))
                m.then_inc(a["y"], 1)

            pe.wait_ge(consts, 11)

            def vo_product():
                pe.wait_ge(w_vo, 32)
                for odd in range(2):
                    if odd:
                        pe.wait_ge(b["vo_even"], NVO)
                    r = slice(odd * DH, (odd + 1) * DH)
                    for c in range(NVO):
                        for k in range(odd, HVO, 2):
                            blk = (HVO * c + k) // 2
                            m = M(bank[4 + c][0:CD, k * D:(k + 1) * D], xwvT_sb[r, blk, :], xwo_sb[r, blk, :],
                                  start=True, stop=True)
                        m.then_inc(b["vo" if odd else "vo_even"], 1)

            def body(i, p):
                if isinstance(i, int) and i == 0:
                    x_T(0, 0)
                    pe.wait_ge(w_in, 32)
                    pe.wait_ge(split, 2 * SELF_SPLITS)
                    pe.wait_ge(zeroed, 1)
                if isinstance(i, int) and i == 3:
                    pe.wait_ge(w_out, 32)
                stage_of(qkv, i, p, 0)
                if isinstance(i, int) and i == 0:
                    vo_product()
                if isinstance(i, int) and i == 1:
                    pe.wait_ge(b["vo_lo"], NVO)
                stage_of(qk_T, i, p, 1)
                stage_of(project, i, p, 3)
                stage_of(lambda t, q: scores(t, q, 0), i, p, 1)
                stage_of(lambda t, q: p_T(t, q, 0), i, p, 2)
                stage_of(lambda t, q: p_T(t, q, 1), i, p, 2)
                stage_of(x_T, i, p, -1)
                stage_of(lambda t, q: scores(t, q, 1), i, p, 1)
                stage_of(lambda t, q: values(t, q, 0), i, p, 2)
                stage_of(lambda t, q: values(t, q, 1), i, p, 2)
            pipeline(pe, body, A_FIRST, T - 1)


            def bx_T(t, p):
                pe.wait_ge(b["xs"], t + 1)
                if p == 0 and later(t, 1):
                    pe.wait_ge(b["kbd3"], t)
                if isinstance(t, int) and t == 2:
                    pe.wait_ge(a["yS"], T)
                nc.tensor.transpose(bank[x_bank(t)][:, p * P:(p + 1) * P], xs[:, p, :], ident[:, :])\
                  .then_inc(b["xT_ps"], 1)

            def pair_product(t, c, hi, lo, r_hi, r_lo):
                for k in range(2):
                    s = slice((2 * c + k) * P, (2 * c + k + 1) * P)
                    m = three(bank[CHUNK_BANK[c]][:, 2 * k * P:2 * (k + 1) * P], hi[:, s], lo[:, s],
                              r_hi[:, :, :].rearrange("d a t -> d (a t)"), r_lo[:, :, :].rearrange("d a t -> d (a t)"))
                return m

            def b_q(t, c):
                pe.wait_ge(b["xlo"], t + 2)
                if later(t, 1):
                    pe.wait_ge(b[f"u{c}"], t)
                pair_product(t, c, xwq_hi, xwq_lo, xT_hi, xT_lo).then_inc(b["q"], 1)

            def b_k(t, c):
                pe.wait_ge(b["clo"], t + 2)
                pe.wait_ge(b["qT"], 2 * t + c + 1)
                pair_product(t, c, xwk_hi, xwk_lo, cT_hi, cT_lo).then_inc(b["k"], 1)

            def b_uv(t, p, c):
                if p:
                    pe.wait_ge(b[f"u{c}"], t)
                else:
                    pe.wait_ge(b[f"kbd{c}"], t + 2)
                    if c == 3:
                        pe.wait_ge(b["xlo"], T if isinstance(t, int) and t + 2 >= T else t + 4)
                three(bank[CHUNK_BANK[c]][:, :], cT_hi[:, p, :], cT_lo[:, p, :], vo_hi[:, c, :], vo_lo[:, c, :])\
                    .then_inc(b["u"], 1)

            def b_s(t, p, c):
                pe.wait_ge(b["qT"], 2 * (t - p) + 2 * c + 2)
                for n in (2 * c, 2 * c + 1):
                    pe.wait_ge(b[f"kbd{n}"], t - p + 2)
                if later(t, 1) or c:
                    pe.wait_ge(b["sub"], 2 * t + c)
                for k in range(HBLK):
                    for s in range(PB):
                        m = M(bank[6][s * SEQ:(s + 1) * SEQ, k * P:(k + 1) * P],
                              QT[:, p, c * HBLK + k, s * SEQ:(s + 1) * SEQ], KBD[:, p, s, c * HBLK + k, :],
                              start=True, stop=True)
                m.then_inc(b["s"], 1)

            def b_pT(t, p):
                pe.wait_ge(b["norm"], t + 1)
                for c in range(2):
                    if later(t, 1):
                        pe.wait_ge(b["pT"], 2 * t)
                    for k in range(HBLK):
                        blk = c * HBLK + k
                        m = nc.tensor.transpose(bank[4 + c][:, k * P:(k + 1) * P], PR[:, p, blk * P:(blk + 1) * P],
                                                ident[:, :])
                    m.then_inc(b["pT_ps"], 1)

            def b_y(t, p, bk=1):
                pe.wait_ge(b["pT"], 2 * (t + 1))
                for c in range(NVO):
                    pe.wait_ge(b[f"u{c}"], t + 1)
                if later(t, 1):
                    pe.wait_ge(b["r"], t)
                for s in range(PB):
                    for k in range(NBLK):
                        m = M(bank[bk][s * SEQ:(s + 1) * SEQ, 0:D], PT[:, k * P + s * SEQ:k * P + (s + 1) * SEQ],
                              VBD[:, p, s, k, :], start=(k == 0), stop=(k == NBLK - 1))
                m.then_inc(b["y"], 1)

            def cross(i, p):
                stage_of(lambda t, q: b_s(t, q, 0), i, p, 1)
                stage_of(b_pT, i, p, 2)
                if p == 0 and has(i):
                    b_q(i, 0)
                if p == 1 and has(i + 1):
                    bx_T(i + 1, 0)
                    bx_T(i + 2, 1)
                if p == 1 and has(i):
                    b_uv(i - 1, 0, 0)
                stage_of(lambda t, q: b_s(t, q, 1), i, p, 1)
                if p == 0 and has(i):
                    for c in (1, 2, 3):
                        b_q(i, c)
                    for c in range(4):
                        b_k(i, c)
                if p == 1 and has(i):
                    for c in (1, 2, 3):
                        b_uv(i - 1, 0, c)
                stage_of(b_y, i, p, 2)
                if p == 1 and has(i):
                    for c in range(NVO):
                        b_uv(i, 1, c)
                if isinstance(i, int) and i == 0:
                    pe.wait_ge(b["kbd0"], 2)
                    pe.wait_ge(b["kbd3"], 2)
                    for c in range(2):
                        p_T(T - 1, 1, c)
                    project(T - 2, 0)
                    for c in range(2):
                        values(T - 1, 1, c)
                    project(T - 1, 1)
            pe.wait_ge(a["kn"], T)
            bx_T(0, 0)
            bx_T(1, 1)
            body(T, 0)
            pe.wait_ge(a["oT"], 2 * (T - 1))
            pe.wait_ge(a["exp"], 2 * T)
            pe.wait_ge(split, 2 * CROSS_SPLITS)
            pe.wait_ge(b["zero"], 1)
            pipeline(pe, cross, B_FIRST, T - 1)


            def front_x(g, p, bk=6):
                pe.wait_ge(f["xs"], g + 1)
                if later(g, 1):
                    pe.wait_ge(f["ewT"], g)
                for tt in range(GT):
                    m = nc.tensor.transpose(bank[bk][:, tt * P:(tt + 1) * P], xg[:, tt, :], ident[:, :])
                m.then_inc(f["xT_ps"], 1)

            def front_scores(g, p, bk=7):
                pe.wait_ge(f["xT"], g + 1)
                if later(g, 1):
                    pe.wait_ge(f["init"], g)
                for tt in range(GT):
                    m = M(bank[bk][:, tt * NE:(tt + 1) * NE], fT[:, p, tt * P:(tt + 1) * P], wr_sb[:, :],
                          start=True, stop=True)
                m.then_inc(f["sc_ps"], 1)

            def front_ew(g, p):
                pe.wait_ge(f["ew"], g + 1)
                for tt in range(GT):
                    m = nc.tensor.transpose(bank[6][0:NE, tt * P:(tt + 1) * P], ew[:, p, tt, :], ident[:, :])
                m.then_inc(f["ewT_ps"], 1)

            def front_bias(g, p):
                pe.wait_ge(f["ewT"], g + 1)
                if isinstance(g, int) and g == 0:
                    pe.wait_ge(b["r"], T)
                for tt in range(GT):
                    m = M(bank[7][:, tt * D:(tt + 1) * D], ewT[:, tt * P:(tt + 1) * P], bl2_sb[:, :],
                          start=True, stop=True)
                m.then_inc(f["bias"], 1)

            def layer1(g, n, p):
                for c in range(NH):
                    k = NE * NH * g + NH * n + c
                    for up in range(2):
                        if later(k, NH):
                            pe.wait_ge(f["g"] if up else f["silu"], k - NH + 1)
                        s = slice(up * HID + c * P, up * HID + (c + 1) * P)
                        three(bank[2 * c + up][:, :], wl1_hi[:, n, s], wl1_lo[:, n, s], fT_hi[:, p, :],
                              fT_lo[:, p, :]).then_inc(f["w1"], 1)

            def layer2(g, n):
                k = NE * g + n
                pe.wait_ge(f["g"], NH * (k + 1))
                if later(k, 2):
                    pe.wait_ge(f["acc"], k - 1)
                elif k == 0:
                    pe.wait_ge(b["pT"], 2 * T)
                for tt in range(GT):
                    for c in range(NH):
                        m = M(bank[4 + n % 2][:, tt * D:(tt + 1) * D], gT[:, n % 2, c, tt * P:(tt + 1) * P],
                              wl2_sb[:, n, c, :], start=(c == 0), stop=(c == NH - 1))
                m.then_inc(f["w2"], 1)

            def group(g, p):
                more = not (isinstance(g, int) and g == G - 1)
                for n in range(NE):
                    if n == 0:
                        pe.wait_ge(f["xlo"], g + 1)
                    layer1(g, n, p)
                    if n == 0 and isinstance(g, int) and g == 0:
                        b_pT(T - 1, 1)
                        b_y(T - 1, 1, 7)
                    if n == 1 and isinstance(g, int) and g == 0:
                        front_ew(0, 0)
                        front_bias(0, 0)
                    if n:
                        layer2(g, n - 1)
                    elif later(g, 1):
                        layer2(g - 1, NE - 1)
                    if more:
                        if n == 1:
                            front_x(g + 1, 1 - p)
                        if n == 2:
                            front_scores(g + 1, 1 - p)
                        if n == 6:
                            front_ew(g + 1, 1 - p)
                        if n == 7:
                            front_bias(g + 1, 1 - p)
            b_s(T - 1, 1, 0)
            pe.wait_ge(b["u0"], T)
            front_x(0, 0, 7)
            b_pT(T - 2, 0)
            b_s(T - 1, 1, 1)
            b_y(T - 2, 0)
            pe.wait_ge(w_ffn, 96)
            pe.wait_ge(b["sub"], 2 * T)
            front_scores(0, 0, 6)
            pe.wait_ge(split, 2 * ALL_SPLITS)
            for c in (1, 2, 3):
                pe.wait_ge(b[f"u{c}"], T)
            pe.wait_ge(b["r"], T - 1)
            ffn_loop(pe, group)
            layer2(G - 1, NE - 1)


def kernel(x, ctx_768, L0_attn_g1, L0_attn_Wq, L0_attn_Wkv, L0_attn_Wout, L0_attn_g2, L0_xattn_Wq, L0_xattn_Wk,
           L0_xattn_Wv, L0_xattn_Wo, L0_xattn_bo, L0_ffn_Wr, L0_ffn_br, L0_ffn_Wl1, L0_ffn_bl1, L0_ffn_Wl2, L0_ffn_bl2,
           L0_ffn_biases_N):
    import numpy as np
    import concourse.bacc as bacc
    from concourse.bass_utils import run_bass_kernel_spmd

    def lay(v, shape=None, order=None):
        v = np.asarray(v)
        if shape is not None:
            v = v.reshape(shape)
        if order is not None:
            v = v.transpose(order)
        return np.ascontiguousarray(v)

    B, S, width = x.shape
    NE, _, H2 = L0_ffn_Wl1.shape
    arrays = {
        "x": lay(x, (B * S, width)),
        "ctxT": lay(ctx_768, (B * S, -1), (1, 0)),
        "g1": lay(L0_attn_g1),
        "wqT": lay(L0_attn_Wq, None, (1, 0)),
        "wkvT": lay(L0_attn_Wkv, None, (1, 0)),
        "woutT": lay(L0_attn_Wout, (width, NBLK, P), (2, 1, 0)),
        "g2": lay(L0_attn_g2),
        "xwq": lay(L0_xattn_Wq),
        "xwk": lay(L0_xattn_Wk),
        "xwvT": lay(L0_xattn_Wv, (-1, NBLK, P), (2, 1, 0)),
        "xwo": lay(L0_xattn_Wo, (NBLK, P, width), (1, 0, 2)),
        "bo": lay(L0_xattn_bo),
        "wrT": lay(L0_ffn_Wr, None, (1, 0)),
        "br": lay(L0_ffn_br),
        "wl1": lay(L0_ffn_Wl1, None, (1, 0, 2)),
        "bl1": lay(L0_ffn_bl1, (NE, H2 // P, P), (2, 0, 1)),
        "wl2": lay(L0_ffn_Wl2, (NE, H2 // 2 // P, P, width), (2, 0, 1, 3)),
        "bl2": lay(L0_ffn_bl2),
        "bN": lay(L0_ffn_biases_N),
    }
    nc = bacc.Bacc("TRN2", target_bir_lowering=False, num_devices=1)
    args = [nc.dram_tensor(f"in_{n}", v.shape, F32, kind="ExternalInput").ap() for n, v in arrays.items()]
    out = nc.dram_tensor("out", (B * S, width), F32, kind="ExternalOutput").ap()
    decoder(nc, *args, out)
    r = run_bass_kernel_spmd(nc, [{f"in_{n}": v for n, v in arrays.items()}], core_ids=[0])
    return r.results[0]["out"].reshape(B, S, width)
```
